# Optimizing a Trainium2 kernel written in Bass

```python
import numpy as np
import jax
import jax.numpy as jnp

def _softmax(x, axis=-1):
    return jax.nn.softmax(x, axis=axis)

def _gelu(x):
    return jax.nn.gelu(x, approximate=True)

def _silu(x):
    return jax.nn.silu(x)

def _sigmoid(x):
    return jax.nn.sigmoid(x)

def _layernorm(x, axis=-1, eps=1e-05):
    m = jnp.mean(x, axis=axis, keepdims=True)
    v = jnp.var(x, axis=axis, keepdims=True)
    return (x - m) / jnp.sqrt(v + eps)

def _scatter_add(tgt, idx, src, axis=0):
    return tgt.at[idx].add(src)

def _segment_sum(src, seg, n):
    return jax.ops.segment_sum(src, seg, n)
kernel_name = 'mk_gnn_ffn_d2_gnn_r16_ad7b88'

def setup_inputs(seed: int=0):
    np.random.seed(seed)
    _w = jnp.asarray

    def _rec_inputs():
        import jax
        import jax.numpy as jnp
        _gk = jax.random.key(seed)
        x = -0.0002117 + 1 * jax.random.normal(jax.random.fold_in(_gk, 1), (6250, 256), jnp.float32)
        src = jax.random.randint(jax.random.fold_in(_gk, 2), (100000,), 0, 6250, jnp.int32)
        dst = jax.random.randint(jax.random.fold_in(_gk, 3), (100000,), 0, 6250, jnp.int32)
        _o = jnp.argsort(dst, stable=True)
        src = src[_o]
        dst = dst[_o]
        edge_weight = jax.random.uniform(jax.random.fold_in(_gk, 13), (100000,), jnp.float32, 0.0, 1)
        return (x, src, dst, edge_weight)
    x, src, dst, edge_weight = _rec_inputs()

    def _L0_gnn_setup():
        import jax, jax.numpy as jnp
        import numpy as np
        N = 6250
        NNZ = 200000
        IN_DIM = 256
        OUT_DIM = 256
        BN_EPS = 1e-05
        key = jax.random.key(seed)
        ks = jax.random.split(key, 6)
        x = jax.random.normal(ks[0], (N, IN_DIM), dtype=jnp.float32)
        A_indices = jax.random.randint(ks[1], (2, NNZ), 0, N, dtype=jnp.int64)
        A_values = jax.random.uniform(ks[2], (NNZ,), dtype=jnp.float32)
        W = jax.random.normal(ks[3], (IN_DIM, OUT_DIM), dtype=jnp.float32) / np.sqrt(IN_DIM)
        bias = jax.random.normal(ks[4], (OUT_DIM,), dtype=jnp.float32) * 0.02
        gamma = jnp.ones((OUT_DIM,), dtype=jnp.float32)
        beta = jnp.zeros((OUT_DIM,), dtype=jnp.float32)
        return {'x': x, 'A_indices': A_indices, 'A_values': A_values, 'A_shape': N, 'W': W, 'bias': bias, 'gamma': gamma, 'beta': beta}
    _L0_gnn_all = _L0_gnn_setup()
    _L0_gnn_in = {k: v for k, v in _L0_gnn_all.items() if k in ('W', 'bias', 'gamma', 'beta')}
    del _L0_gnn_all

    def _L0_ffn_setup():
        import jax, jax.numpy as jnp
        import numpy as np
        B, S, D = (8, 256, 256)
        H = 4 * D
        CAPACITY = 0.5
        key = jax.random.key(seed)
        ks = jax.random.split(key, 6)
        x = jax.random.normal(ks[0], (B, S, D), dtype=jnp.float32)
        attention_mask = jnp.zeros((B, 1, 1, S), dtype=jnp.float32)
        wr = jax.random.normal(ks[1], (D, 1), dtype=jnp.float32) * 0.02
        br = jnp.zeros((1,), dtype=jnp.float32)
        w1 = jax.random.normal(ks[2], (D, H), dtype=jnp.float32) * 0.02
        b1 = jnp.zeros((H,), dtype=jnp.float32)
        w2 = jax.random.normal(ks[3], (H, D), dtype=jnp.float32) * 0.02
        b2 = jnp.zeros((D,), dtype=jnp.float32)
        return {'x': x, 'attention_mask': attention_mask, 'wr': wr, 'br': br, 'w1': w1, 'b1': b1, 'w2': w2, 'b2': b2}
    _L0_ffn_all = _L0_ffn_setup()
    _L0_ffn_in = {k: v for k, v in _L0_ffn_all.items() if k in ('attention_mask', 'wr', 'br', 'w1', 'b1', 'w2', 'b2')}
    del _L0_ffn_all

    def _L1_gnn_setup():
        import jax, jax.numpy as jnp
        import numpy as np
        N_NODES = 6250
        N_EDGES = 200000
        DIM_IN = 256
        DIM_OUT = 256
        key = jax.random.key(seed)
        ks = jax.random.split(key, 8)
        feat_in = jax.random.normal(ks[0], (N_NODES, DIM_IN), dtype=jnp.float32)
        edge_row = jax.random.randint(ks[1], (N_EDGES,), 0, N_NODES, dtype=jnp.int32)
        edge_col = jax.random.randint(ks[2], (N_EDGES,), 0, N_NODES, dtype=jnp.int32)
        edge_val = jax.random.uniform(ks[3], (N_EDGES,), dtype=jnp.float32)
        s1 = 1.0 / np.sqrt(DIM_IN)
        s2 = 1.0 / np.sqrt(DIM_OUT)
        W1 = jax.random.normal(ks[4], (DIM_IN, DIM_OUT), dtype=jnp.float32) * s1
        b1 = jnp.zeros((DIM_OUT,), dtype=jnp.float32)
        W2 = jax.random.normal(ks[5], (DIM_OUT, DIM_OUT), dtype=jnp.float32) * s2
        b2 = jnp.zeros((DIM_OUT,), dtype=jnp.float32)
        eps = jnp.zeros((1,), dtype=jnp.float32)
        offset = jnp.zeros((DIM_OUT,), dtype=jnp.float32)
        scale = jnp.ones((DIM_OUT,), dtype=jnp.float32)
        return {'feat_in': feat_in, 'edge_row': edge_row, 'edge_col': edge_col, 'edge_val': edge_val, 'W1': W1, 'b1': b1, 'W2': W2, 'b2': b2, 'eps': eps, 'offset': offset, 'scale': scale}
    _L1_gnn_all = _L1_gnn_setup()
    _L1_gnn_in = {k: v for k, v in _L1_gnn_all.items() if k in ('W1', 'b1', 'W2', 'b2', 'eps', 'offset', 'scale')}
    del _L1_gnn_all

    def _L1_ffn_setup():
        import jax, jax.numpy as jnp
        import numpy as np
        TOP_K = 2
        LN_EPS = 1e-05
        key = jax.random.key(seed)
        ks = jax.random.split(key, 8)
        B, S, D, E, H = (16, 1024, 256, 8, 1024)
        x = jax.random.normal(ks[0], (B, S, D), dtype=jnp.float32)
        Wr = jax.random.normal(ks[1], (D, E), dtype=jnp.float32) * 0.1
        br = jnp.zeros((E,), dtype=jnp.float32)
        ln_g = jnp.ones((E, D), dtype=jnp.float32)
        ln_b = jnp.zeros((E, D), dtype=jnp.float32)
        W1 = jax.random.normal(ks[2], (E, D, H), dtype=jnp.float32) * (1.0 / np.sqrt(D))
        b1 = jnp.zeros((E, H), dtype=jnp.float32)
        W2 = jax.random.normal(ks[3], (E, H, D), dtype=jnp.float32) * (1.0 / np.sqrt(H))
        b2 = jnp.zeros((E, D), dtype=jnp.float32)
        return {'x': x, 'Wr': Wr, 'br': br, 'ln_g': ln_g, 'ln_b': ln_b, 'W1': W1, 'b1': b1, 'W2': W2, 'b2': b2}
    _L1_ffn_all = _L1_ffn_setup()
    _L1_ffn_in = {k: v for k, v in _L1_ffn_all.items() if k in ('Wr', 'br', 'ln_g', 'ln_b', 'W1', 'b1', 'W2', 'b2')}
    del _L1_ffn_all
    return {'x': x, 'src': src, 'dst': dst, 'edge_weight': edge_weight, 'L0_gnn_W': _L0_gnn_in['W'], 'L0_gnn_bias': _L0_gnn_in['bias'], 'L0_gnn_gamma': _L0_gnn_in['gamma'], 'L0_gnn_beta': _L0_gnn_in['beta'], 'L0_ffn_attention_mask': _L0_ffn_in['attention_mask'], 'L0_ffn_wr': _L0_ffn_in['wr'], 'L0_ffn_br': _L0_ffn_in['br'], 'L0_ffn_w1': _L0_ffn_in['w1'], 'L0_ffn_b1': _L0_ffn_in['b1'], 'L0_ffn_w2': _L0_ffn_in['w2'], 'L0_ffn_b2': _L0_ffn_in['b2'], 'L1_gnn_W1': _L1_gnn_in['W1'], 'L1_gnn_b1': _L1_gnn_in['b1'], 'L1_gnn_W2': _L1_gnn_in['W2'], 'L1_gnn_b2': _L1_gnn_in['b2'], 'L1_gnn_eps': _L1_gnn_in['eps'], 'L1_gnn_offset': _L1_gnn_in['offset'], 'L1_gnn_scale': _L1_gnn_in['scale'], 'L1_ffn_Wr': _L1_ffn_in['Wr'], 'L1_ffn_br': _L1_ffn_in['br'], 'L1_ffn_ln_g': _L1_ffn_in['ln_g'], 'L1_ffn_ln_b': _L1_ffn_in['ln_b'], 'L1_ffn_W1': _L1_ffn_in['W1'], 'L1_ffn_b1': _L1_ffn_in['b1'], 'L1_ffn_W2': _L1_ffn_in['W2'], 'L1_ffn_b2': _L1_ffn_in['b2']}

def reference(x, src, dst, edge_weight, L0_gnn_W, L0_gnn_bias, L0_gnn_gamma, L0_gnn_beta, L0_ffn_attention_mask, L0_ffn_wr, L0_ffn_br, L0_ffn_w1, L0_ffn_b1, L0_ffn_w2, L0_ffn_b2, L1_gnn_W1, L1_gnn_b1, L1_gnn_W2, L1_gnn_b2, L1_gnn_eps, L1_gnn_offset, L1_gnn_scale, L1_ffn_Wr, L1_ffn_br, L1_ffn_ln_g, L1_ffn_ln_b, L1_ffn_W1, L1_ffn_b1, L1_ffn_W2, L1_ffn_b2):
    import jax
    import jax.numpy as jnp

    def _L0_gnn_ref(x, A_indices, A_values, A_shape, W, bias, gamma, beta):
        import jax, jax.numpy as jnp
        import numpy as np
        N = 6250
        NNZ = 200000
        IN_DIM = 256
        OUT_DIM = 256
        BN_EPS = 1e-05
        h = jnp.einsum('nd,df->nf', x, W)
        row, col = (A_indices[0], A_indices[1])
        gathered = A_values[:, None] * h[col]
        agg = jax.ops.segment_sum(gathered, row, num_segments=A_shape)
        h = agg + bias
        mean = jnp.mean(h, axis=0)
        var = jnp.mean(jnp.square(h - mean), axis=0)
        h = (h - mean) * jax.lax.rsqrt(var + BN_EPS) * gamma + beta
        return jax.nn.relu(h)

    def _L0_ffn_ref(x, attention_mask, wr, br, w1, b1, w2, b2):
        import jax, jax.numpy as jnp
        import numpy as np
        B, S, D = (8, 256, 256)
        H = 4 * D
        CAPACITY = 0.5
        b, s, d = x.shape
        weights = (jnp.einsum('bsd,do->bso', x, wr) + br)[..., 0]
        k = max(1, int(CAPACITY * s))
        kk = k - 1 if k > 1 else 1
        _, idx = jax.lax.top_k(weights, k)
        sel_idx = idx[:, :kk]
        sel = jnp.take_along_axis(x, sel_idx[:, :, None], axis=1)
        h = jax.nn.gelu(jnp.einsum('bkd,dh->bkh', sel, w1) + b1)
        y = jnp.einsum('bkh,hd->bkd', h, w2) + b2
        w_sel = jnp.take_along_axis(weights, sel_idx, axis=1)
        y = y * w_sel[..., None]
        batch_idx = jnp.arange(b)[:, None]
        processed = jnp.zeros_like(x).at[batch_idx, sel_idx].set(y)
        return processed + x

    def _L1_gnn_ref(feat_in, edge_row, edge_col, edge_val, W1, b1, W2, b2, eps, offset, scale):
        import jax, jax.numpy as jnp
        import numpy as np
        N_NODES = 6250
        N_EDGES = 200000
        DIM_IN = 256
        DIM_OUT = 256
        msg = edge_val[:, None] * feat_in[edge_col]
        aggr = jax.ops.segment_sum(msg, edge_row, num_segments=feat_in.shape[0])
        aggr = aggr + (1.0 + eps) * feat_in
        h = jnp.maximum(aggr @ W1 + b1, 0.0) @ W2 + b2
        h = jnp.maximum(h, 0.0)
        mean = jnp.mean(h, axis=1, keepdims=True)
        var = jnp.var(h, axis=1, keepdims=True) + 1e-10
        return (h - mean) * scale * jax.lax.rsqrt(var) + offset

    def _L1_ffn_ref(x, Wr, br, ln_g, ln_b, W1, b1, W2, b2):
        import jax, jax.numpy as jnp
        import numpy as np
        TOP_K = 2
        LN_EPS = 1e-05
        B, S, D = x.shape
        N = B * S
        xt = x.reshape(N, D)
        logits = xt @ Wr + br
        probs = jax.nn.softmax(logits, axis=-1)
        top_p, top_idx = jax.lax.top_k(probs, TOP_K)
        weights = top_p / top_p.sum(axis=-1, keepdims=True)
        mu = xt.mean(axis=-1, keepdims=True)
        var = ((xt - mu) ** 2).mean(axis=-1, keepdims=True)
        xn = (xt - mu) * jax.lax.rsqrt(var + LN_EPS)
        xe = xn[None, :, :] * ln_g[:, None, :] + ln_b[:, None, :]
        h = jax.nn.gelu(jnp.einsum('end,edh->enh', xe, W1) + b1[:, None, :], approximate=False)
        y = jnp.einsum('enh,ehd->end', h, W2) + b2[:, None, :]
        y_tok = jnp.transpose(y, (1, 0, 2))
        sel = jnp.take_along_axis(y_tok, top_idx[:, :, None], axis=1)
        out = (weights[:, :, None] * sel).sum(axis=1)
        return out.reshape(B, S, D)
    edge_index = jnp.stack([src, dst])
    x = x + _L0_gnn_ref(_layernorm(x, axis=-1), edge_index, edge_weight, 6250, L0_gnn_W, L0_gnn_bias, L0_gnn_gamma, L0_gnn_beta)
    x = x + _L0_ffn_ref(_layernorm(x, axis=-1)[None], L0_ffn_attention_mask, L0_ffn_wr, L0_ffn_br, L0_ffn_w1, L0_ffn_b1, L0_ffn_w2, L0_ffn_b2)[0]
    x = x + _L1_gnn_ref(_layernorm(x, axis=-1), src, dst, edge_weight, L1_gnn_W1, L1_gnn_b1, L1_gnn_W2, L1_gnn_b2, L1_gnn_eps, L1_gnn_offset, L1_gnn_scale)
    x = x + _L1_ffn_ref(_layernorm(x, axis=-1)[None], L1_ffn_Wr, L1_ffn_br, L1_ffn_ln_g, L1_ffn_ln_b, L1_ffn_W1, L1_ffn_b1, L1_ffn_W2, L1_ffn_b2)[0]
    return x

_drawn_inputs = setup_inputs


def setup_inputs(seed=0):
    import zlib

    import numpy as np

    out = dict(_drawn_inputs(seed))
    spreads = {'L0_gnn_gamma': (1.0, 0.2),
     'L0_gnn_beta': (0.0, 0.1),
     'L0_ffn_b1': (0.0, 0.8),
     'L0_ffn_b2': (0.0, 0.405),
     'L1_gnn_b1': (0.0, 0.267),
     'L1_gnn_b2': (0.0, 0.1),
     'L1_gnn_offset': (0.0, 0.1),
     'L1_gnn_scale': (1.0, 0.2),
     'L1_ffn_br': (0.0, 0.1),
     'L1_ffn_ln_g': (1.0, 0.2),
     'L1_ffn_ln_b': (0.0, 0.361),
     'L1_ffn_b1': (0.0, 0.374),
     'L1_ffn_b2': (0.0, 0.293)}
    factors = {'L0_gnn_bias': 64.0, 'L0_ffn_wr': 2.915, 'L0_ffn_w1': 3.404, 'L0_ffn_w2': 3.188}
    for name, (base, spread) in spreads.items():
        noise = np.random.default_rng([zlib.crc32(name.encode()), seed]).standard_normal(out[name].shape)
        drawn = base * np.exp(spread * noise) if base else spread * noise
        out[name] = jnp.asarray(drawn.astype(out[name].dtype))
    for name, factor in factors.items():
        out[name] = (out[name] * factor).astype(out[name].dtype)
    return out
```

```python
from contextlib import ExitStack, contextmanager

import concourse.bass as bass
from concourse import mybir

ALU = mybir.AluOpType
ACT = mybir.ActivationFunctionType
AX = mybir.AxisListType
F32 = mybir.dt.float32
I32 = mybir.dt.int32
U32 = mybir.dt.uint32

P = 128
D = 256
KD = D // P
N = 6250
NT = -(-N // P)
NLAST = N - (NT - 1) * P
E = 100000
EJ = -(-E // P)
ETAIL = E - (P - 1) * EJ
NB = NT + 1
SORT_J = 23
SORT_STEPS = EJ // SORT_J
CHUNKS = -(-((E + NT * (P - 1)) // P + 1) // 32) * 32
REC = 4
GB = 16
GSEM = 4
BANK = 512
GROUP = 7
HALF = GROUP * P // 2
TOPK = max(1, int(0.5 * N)) - 1
NE = 8
HM = 1024
MT = 2 * P
MTILES = (2 * NT * P + NE * (MT - 1)) // MT
ZEROS = MTILES // 4
assert SORT_STEPS * SORT_J == EJ and SORT_STEPS % 2 == 0 and NT % GROUP == 0 and MTILES % 4 == 0


class Steps:

    def __init__(self, engine, sem):
        self.engine, self.sem, self.base, self.n = engine, sem, 0, 0

    def __call__(self, instruction):
        self.n += 1
        instruction.then_inc(self.sem, 1)
        self.engine.wait_ge(self.sem, self.base + self.n)

    @contextmanager
    def loop(self, first, last, per):
        start = self.base + self.n
        with self.engine.Fori(first, last) as i:
            self.base, self.n = (i - first) * per + start, 0
            yield i
            assert self.n == per, self.n
        self.base, self.n = start + (last - first) * per, 0


def build(nc, x, src, dst, edge_weight, g0_w, g0_bias, g0_gamma, g0_beta, f0_wr, f0_br, f0_w1, f0_b1, f0_w2, f0_b2,
          g1_w1, g1_b1, g1_w2, g1_b2, g1_eps, g1_offset, g1_scale, m_wr, m_br, m_g, m_b, m_w1, m_b1, m_w2, m_b2, out):
    dram = lambda name, shape, dt=F32: nc.dram_tensor(name, shape, dt, kind="Internal").ap()
    table = [dram("table0", (NT * P, D)), dram("table1", (NT * P, D))]
    records = dram("records", (P * CHUNKS, REC), I32)
    chunk_tile_row = dram("chunk_tile_row", (7 * P,), I32)
    slots_in = dram("slots_in", (MTILES * MT, D))
    slots_out = dram("slots_out", (MTILES * MT, D))
    expert_row = dram("expert_row", (P,), I32)
    by_node = lambda a: a[0:(NT - 1) * P, :].rearrange("(t p) d -> p t d", p=P)

    ctx = ExitStack()
    with ctx:
        def sem(name):
            return ctx.enter_context(nc.semaphore(name))

        def sb(name, shape, dt=F32, at=None):
            return (at or ctx).enter_context(nc.sbuf_tensor(name, shape, dt))

        psum = ctx.enter_context(nc.psum_tensor("psum", [P, 8, BANK], F32))

        X = sb("X", [P, NT, D])
        A = sb("A", [P, NT, D])
        ident = sb("ident", [P, P])
        columns = sb("columns", [P, P])
        before = sb("before", [P, P])
        ones = sb("ones", [P, P])
        ones_last = sb("ones_last", [P, P])
        part = sb("part", [P, 1])
        chunk_tile = sb("chunk_tile", [1, 7 * P], I32)
        stats = sb("stats", [P, NT, 6])
        moments = sb("moments", [P, NT, 2])
        rstd = sb("rstd", [P, NT])

        def row_stats(dve, steps, rows):
            with steps.loop(0, NT, 1) as t:
                steps(dve.bn_stats(stats[:, bass.ds(t, 1), :].rearrange("p a s -> p (a s)"),
                                   rows[:, bass.ds(t, 1), :].rearrange("p a d -> p (a d)")))
            mean, var = moments[:, :, 0], moments[:, :, 1]
            steps(dve.tensor_tensor(mean, stats[:, :, 1], stats[:, :, 4], ALU.add))
            steps(dve.tensor_scalar(mean, mean, 0.5, None, ALU.mult))
            steps(dve.tensor_tensor(rstd[:], stats[:, :, 1], stats[:, :, 4], ALU.subtract))
            steps(dve.scalar_tensor_tensor(rstd[:], rstd[:], 0.25, rstd[:], ALU.mult, ALU.mult))
            steps(dve.tensor_tensor(var, stats[:, :, 2], stats[:, :, 5], ALU.add))
            steps(dve.scalar_tensor_tensor(var, var, 1.0 / D, rstd[:], ALU.mult, ALU.add))

        def row_rstd(dve, steps, eps, var_ready, root_ready, n=1):
            steps(dve.tensor_scalar(rstd[:], moments[:, :, 1], eps, None, ALU.add))
            dve.engine_nop().then_inc(var_ready, 1)
            dve.wait_ge(root_ready, n)
            steps(dve.reciprocal(rstd[:], rstd[:]))

        def row_root(act, var_ready, root_ready, n=1):
            act.wait_ge(var_ready, n)
            act.activation(rstd[:], rstd[:], ACT.Sqrt).then_inc(root_ready, 1)

        def row_normalise(dve, steps, to, rows, done=None):
            with steps.loop(0, NT, 1) as t:
                ins = dve.tensor_scalar(to[:, bass.ds(t, 1), :], rows[:, bass.ds(t, 1), :],
                                        moments[:, bass.ds(t, 1), 0], rstd[:, bass.ds(t, 1)],
                                        ALU.subtract, ALU.mult)
                steps(ins)

        with ExitStack() as scope, nc.Block() as block:
            here = lambda name, shape, dt=F32: sb(name, shape, dt, scope)
            src_i = here("src_i", [P, EJ], I32)
            dst_i = here("dst_i", [P, EJ], I32)
            w_e = here("w_e", [P, EJ])
            tile_i = here("tile_i", [P, EJ], I32)
            tile_f = here("tile_f", [P, EJ])
            local_f = here("local_f", [P, EJ])
            junk = here("junk", [P, EJ])
            count = here("count", [P, NB])
            nchunk_i = here("nchunk_i", [P, NB], I32)
            nchunk = here("nchunk", [P, NB])
            upto = here("upto", [P, NB])
            first = here("first", [P, NB])
            chunk_no_i = here("chunk_no_i", [P, 7], I32)
            chunk_no = here("chunk_no", [P, 7])
            passed = here("passed", [P, 7, NT])
            chunk_tile_f = here("chunk_tile_f", [P, 7])
            chunk_tile_i = here("chunk_tile_i", [P, 7], I32)
            hot = here("hot", [P, NB, SORT_J + 1])
            keep = here("keep", [P, NB, SORT_J + 1])
            upto_slot = here("upto_slot", [P, NB, SORT_J + 1])
            picked = here("picked", [P, NB, SORT_J])
            slot_f = here("slot_f", [P, SORT_J])
            slot_i = here("slot_i", [P, SORT_J], I32)
            slot_q = here("slot_q", [P, SORT_J], I32)
            slot_c = here("slot_c", [P, SORT_J], I32)
            place = here("place", [P, 2, SORT_J], I32)
            rec = here("rec", [P, 2, SORT_J, REC], I32)
            zero = here("zero", [P, CHUNKS * REC], I32)
            iota_i = here("iota_i", [P, P], I32)
            part_i = here("part_i", [P, 1], I32)
            w0 = here("w0", [P, KD, D])
            xn = here("xn", [P, 2, D])
            xt = here("xt", [P, 2, KD, P])
            h_out = here("h_out", [P, 2, D])

            s_step = sem("sort_step")
            loaded = sem("edges_loaded")
            x_loaded = sem("x_loaded")
            w0_loaded = sem("w0_loaded")
            pads_set = sem("pads_set")
            iota_done = sem("iota_done")
            consts_done = sem("consts_done")
            local_done = sem("local_done")
            counted = sem("counted")
            totals = sem("totals")
            zero_set = sem("zero_set")
            prefilled = sem("prefilled")
            map_ready = sem("map_ready")
            map_out = sem("map_out")
            map_in = sem("map_in")
            placed = sem("placed")
            rec_filled = sem("rec_filled")
            scattered = [sem("scattered0"), sem("scattered1")]
            step_open = sem("scatter_open")
            var_ready, root_ready = sem("ln0_var"), sem("ln0_root")
            xn_ready = sem("ln0_rows")
            turned, turned_out = sem("h_turned"), sem("h_turned_out")
            made, made_out = sem("h_made"), sem("h_made_out")
            stored = [sem("h_stored0"), sem("h_stored1")]

            @block.sync
            def _(sp):
                sp.wait_ge(pads_set, 4)
                for to, of in ((src_i, src), (dst_i, dst), (w_e, edge_weight)):
                    sp.dma_start(to[0:P - 1, :], of[0:(P - 1) * EJ].rearrange("(p j) -> p j", j=EJ)).then_inc(loaded, 16)
                    sp.dma_start(to[P - 1:P, 0:ETAIL], of[(P - 1) * EJ:E].rearrange("(a j) -> a j", a=1)).then_inc(loaded, 16)
                sp.dma_start(X[:, 0:NT - 1, :], by_node(x)).then_inc(x_loaded, 16)
                sp.dma_start(X[0:NLAST, NT - 1, :], x[(NT - 1) * P:N, :]).then_inc(x_loaded, 16)
                sp.dma_start(w0[:], g0_w.rearrange("(k p) n -> p k n", p=P)).then_inc(w0_loaded, 16)
                sp.wait_ge(zero_set, 1)
                sp.dma_start(records.rearrange("(q c) f -> q (c f)", q=P), zero[:]).then_inc(prefilled, 16)
                for m in range(ZEROS):
                    sp.dma_start(slots_in[m * 4 * MT:(m + 1) * 4 * MT, :].rearrange("(q r) d -> q (r d)", q=P),
                                 zero[:, 0:4 * MT * D // P].bitcast(F32)).then_inc(prefilled, 16)
                sp.wait_ge(map_ready, 1)
                sp.dma_start(chunk_tile_row.rearrange("(k p) -> p k", p=P), chunk_tile_i[:],
                             allow_slow_non_contiguous=True).then_inc(map_out, 16)
                sp.wait_ge(map_out, 16)
                sp.dma_start(chunk_tile[:], chunk_tile_row.rearrange("(a k) -> a k", a=1)).then_inc(map_in, 16)

                def store(t, u):
                    sp.dma_start(table[0][bass.ts(t, P), :], h_out[:, u, :]).then_inc(stored[u], 16)

                with sp.Fori(0, NT // 2) as i:
                    for u in range(2):
                        sp.wait_ge(made_out, 2 * i + (u + 1))
                        store(2 * i + u, u)
                sp.wait_ge(made_out, NT)
                store(NT - 1, 0)
                sp.wait_ge(stored[0], 16 * (NT // 2 + 1))
                sp.wait_ge(stored[1], 16 * (NT // 2))
                sp.wait_ge(map_in, 16)
                sp.wait_ge(prefilled, 16 * (1 + ZEROS))

            @block.gpsimd
            def _(pool):
                pool.memset(zero[:], 0).then_inc(zero_set, 1)
                pool.iota(iota_i[:], [[1, P]], base=0, channel_multiplier=0).then_inc(iota_done, 1)
                pool.iota(part_i[:], [[0, 1]], base=0, channel_multiplier=1).then_inc(iota_done, 1)
                pool.iota(chunk_no_i[:], [[P, 7]], base=0, channel_multiplier=1).then_inc(iota_done, 1)
                pool.wait_ge(prefilled, 16 * (1 + ZEROS))
                with pool.Fori(0, SORT_STEPS // 2) as i:
                    for u in range(2):
                        pool.wait_ge(placed, 2 * i + (u + 1))
                        pool.wait_ge(rec_filled, 6 * i + 3 * (u + 1) + 1)
                        pool.sem_inc(step_open, 1)
                        for j in range(SORT_J):
                            pool.indirect_dma_start(
                                records, bass.IndirectOffsetOnAxis(ap=place[:, u, j:j + 1].bitcast(U32), axis=0),
                                rec[:, u, j, :], None).then_inc(scattered[u], 16)
                for u in range(2):
                    pool.wait_ge(scattered[u], 16 * SORT_J * (SORT_STEPS // 2))

            @block.vector
            def _(dve):
                s = Steps(dve, s_step)
                dve.memset(src_i[:], NT * P).then_inc(pads_set, 1)
                dve.memset(dst_i[:], 0).then_inc(pads_set, 1)
                dve.memset(w_e[:], 0.0).then_inc(pads_set, 1)
                dve.memset(X[:, NT - 1, :], 0.0).then_inc(pads_set, 1)
                dve.wait_ge(iota_done, 3)
                s(dve.tensor_copy(columns[:], iota_i[:]))
                s(dve.tensor_copy(part[:], part_i[:]))
                s(dve.tensor_copy(chunk_no[:], chunk_no_i[:]))
                s(dve.tensor_scalar(ident[:], columns[:], part[:, 0:1], None, ALU.is_equal))
                s(dve.tensor_scalar(before[:], columns[:], part[:, 0:1], None, ALU.is_gt))
                s(dve.memset(ones[:], 1.0))
                s(dve.tensor_scalar(ones_last[:], ones[:], part[:, 0:1], float(NLAST), ALU.mult, ALU.is_lt))
                s(dve.memset(keep[:], 1.0))
                s(dve.memset(keep[:, :, 0:1], 0.0))
                dve.engine_nop().then_inc(consts_done, 1)
                dve.wait_ge(loaded, 96)
                s(dve.tensor_scalar(tile_i[:], src_i[:], 7, None, ALU.logical_shift_right))
                s(dve.tensor_scalar(src_i[:], src_i[:], P - 1, None, ALU.bitwise_and))
                s(dve.tensor_copy(tile_f[:], tile_i[:]))
                dve.tensor_copy(local_f[:], src_i[:]).then_inc(local_done, 1)
                for b in range(NB):
                    s(dve.tensor_scalar(junk[:], tile_f[:], float(b), 0.0, ALU.is_equal, ALU.add,
                                        accum_out=count[:, b:b + 1]))
                dve.engine_nop().then_inc(counted, 1)
                dve.wait_ge(totals, 2)
                s(dve.tensor_scalar(nchunk_i[:], psum[:, 1, 0:NB], float(P - 1), None, ALU.add))
                s(dve.tensor_scalar(nchunk_i[:], nchunk_i[:], 7, None, ALU.logical_shift_right))
                s(dve.tensor_copy(nchunk[:], nchunk_i[:]))
                s(dve.tensor_tensor_scan(upto[:], ones[:, 0:NB], nchunk[:], 0.0, ALU.mult, ALU.add))
                s(dve.tensor_tensor(first[:], upto[:], nchunk[:], ALU.subtract))
                s(dve.scalar_tensor_tensor(first[:], first[:], float(P), psum[:, 0, 0:NB], ALU.mult, ALU.add))
                s(dve.tensor_scalar(upto_slot[:, :, SORT_J], first[:], -1.0, None, ALU.add))
                s(dve.tensor_tensor(passed[:], chunk_no[:].unsqueeze(2).to_broadcast([P, 7, NT]),
                                    upto[:, 0:NT].unsqueeze(1).to_broadcast([P, 7, NT]), ALU.is_ge))
                s(dve.tensor_reduce(chunk_tile_f[:], passed[:], AX.X, ALU.add))
                dve.tensor_scalar(chunk_tile_i[:], chunk_tile_f[:], float(NT - 1), None, ALU.min).then_inc(map_ready, 1)

                def sort_step(k, u, reused):
                    s(dve.tensor_copy(hot[:, :, 0], upto_slot[:, :, SORT_J]))
                    s(dve.tensor_tensor(hot[:, :, 1:], tile_f[:, bass.ts(k, SORT_J)].unsqueeze(1).to_broadcast([P, NB, SORT_J]),
                                        columns[:, 0:NB].unsqueeze(2).to_broadcast([P, NB, SORT_J]), ALU.is_equal))
                    s(dve.tensor_tensor_scan(upto_slot[:].rearrange("p b j -> p (b j)"), keep[:].rearrange("p b j -> p (b j)"),
                                             hot[:].rearrange("p b j -> p (b j)"), 0.0, ALU.mult, ALU.add))
                    s(dve.tensor_tensor(picked[:], hot[:, :, 1:], upto_slot[:, :, 1:], ALU.mult))
                    s(dve.tensor_reduce(slot_f[:], picked[:].rearrange("p b j -> p j b"), AX.X, ALU.add))
                    s(dve.tensor_copy(slot_i[:], slot_f[:]))
                    s(dve.tensor_scalar(slot_q[:], slot_i[:], P - 1, None, ALU.bitwise_and))
                    s(dve.tensor_scalar(slot_c[:], slot_i[:], 7, None, ALU.logical_shift_right))
                    if reused is not None:
                        dve.wait_ge(scattered[u], reused)
                    dve.scalar_tensor_tensor(place[:, u, :], slot_q[:], float(CHUNKS), slot_c[:],
                                             ALU.mult, ALU.add).then_inc(placed, 1)

                for u in range(2):
                    sort_step(u, u, None)
                dve.wait_ge(x_loaded, 32)
                row_stats(dve, s, X)
                row_rstd(dve, s, 1e-5, var_ready, root_ready)

                def normalise(t, u, earlier):
                    if earlier is not None:
                        dve.wait_ge(turned, earlier)
                    dve.tensor_scalar(xn[:, u, :], X[:, bass.ds(t, 1), :].rearrange("p a d -> p (a d)"),
                                      moments[:, bass.ds(t, 1), 0], rstd[:, bass.ds(t, 1)],
                                      ALU.subtract, ALU.mult).then_inc(xn_ready, 1)

                for t in range(2):
                    normalise(t, t, None)
                with dve.Fori(1, NT // 2) as i:
                    for u in range(2):
                        normalise(2 * i + u, u, 2 * i + (u - 1))
                normalise(NT - 1, 0, NT - 2)
                with s.loop(1, SORT_STEPS // 2, 16) as i:
                    for u in range(2):
                        sort_step(2 * i + u, u, i * (16 * SORT_J))

            @block.scalar
            def _(act):
                def fill(k, u, reused):
                    if reused is not None:
                        act.wait_ge(scattered[u], reused)
                    at = bass.ts(k, SORT_J)
                    act.copy(rec[:, u, :, 0], dst_i[:, at]).then_inc(rec_filled, 1)
                    act.copy(rec[:, u, :, 1].bitcast(F32), local_f[:, at]).then_inc(rec_filled, 1)
                    act.copy(rec[:, u, :, 2].bitcast(F32), w_e[:, at]).then_inc(rec_filled, 1)

                act.wait_ge(zero_set, 1)
                act.copy(rec[:].bitcast(F32).rearrange("p a j f -> p (a j f)"), zero[:, 0:2 * SORT_J * REC].bitcast(F32)).then_inc(rec_filled, 1)
                act.wait_ge(rec_filled, 1)
                act.wait_ge(loaded, 96)
                act.wait_ge(local_done, 1)
                for u in range(2):
                    fill(u, u, None)
                row_root(act, var_ready, root_ready)

                def tile(t, u, reused):
                    act.wait_ge(turned, t + 1)
                    act.copy(xt[:, u, :, :].rearrange("p k n -> p (k n)"), psum[:, 2 + u, 0:D]).then_inc(turned_out, 1)
                    act.wait_ge(made, t + 1)
                    if reused is not None:
                        act.wait_ge(stored[u], reused)
                    act.copy(h_out[:, u, :], psum[:, 4 + u, 0:D]).then_inc(made_out, 1)

                for t in range(2):
                    tile(t, t, None)
                with act.Fori(1, NT // 2) as i:
                    for u in range(2):
                        tile(2 * i + u, u, i * 16)
                tile(NT - 1, 0, 16 * (NT // 2))
                with act.Fori(1, SORT_STEPS // 2) as i:
                    for u in range(2):
                        fill(2 * i + u, u, i * (16 * SORT_J))

            @block.tensor
            def _(pe):
                pe.wait_ge(consts_done, 1)
                pe.wait_ge(counted, 1)
                pe.matmul(psum[:, 0, 0:NB], before[:], count[:], start=True, stop=True).then_inc(totals, 1)
                pe.matmul(psum[:, 1, 0:NB], ones[:], count[:], start=True, stop=True).then_inc(totals, 1)
                pe.wait_ge(w0_loaded, 16)

                def tile(t, u, earlier):
                    if earlier is not None:
                        pe.wait_ge(turned_out, earlier)
                    pe.wait_ge(xn_ready, t + 1)
                    for k in range(KD):
                        ins = pe.transpose(psum[:, 2 + u, k * P:(k + 1) * P], xn[:, u, k * P:(k + 1) * P], ident[:])
                    ins.then_inc(turned, 1)
                    pe.wait_ge(turned_out, t + 1)
                    if earlier is not None:
                        pe.wait_ge(made_out, earlier)
                    for k in range(KD):
                        ins = pe.matmul(psum[:, 4 + u, 0:D], xt[:, u, k, :], w0[:, k, :], start=k == 0, stop=k == KD - 1)
                    ins.then_inc(made, 1)

                for t in range(2):
                    tile(t, t, None)
                with pe.Fori(1, NT // 2) as i:
                    for u in range(2):
                        tile(2 * i + u, u, 2 * i + (u - 1))
                tile(NT - 1, 0, NT - 2)

        def aggregate(rows, name, prepare):
            with ExitStack() as scope, nc.Block() as block:
                here = lambda what, shape, dt=F32: sb(name + what, shape, dt, scope)
                rec = here("rec", [P, 2, GB, REC], I32)
                got = here("got", [P, 2, GB, D])
                route = here("route", [P, 2, GB, P])
                step, added = sem(name + "step"), sem(name + "added")
                step_open = sem(name + "gather_open")
                rec_in = [sem(name + "rec_in0"), sem(name + "rec_in1")]
                gathered = [[sem(name + f"gathered{u}{g}") for g in range(GB // GSEM)] for u in range(2)]
                routed, summed = sem(name + "routed"), sem(name + "summed")
                by_chunk = records.rearrange("(q c) f -> q c f", q=P)
                STEPS = CHUNKS // GB

                def load(eng, n, u):
                    eng.dma_start(rec[:, u, :, :], by_chunk[:, bass.ts(n, GB), :]).then_inc(rec_in[u], 16)

                @block.sync
                def _(sp):
                    load(sp, 0, 0)
                    load(sp, 1, 1)
                    with sp.Fori(1, STEPS // 2) as i:
                        for u in range(2):
                            for g in range(GB // GSEM):
                                sp.wait_ge(gathered[u][g], i * (16 * GSEM))
                            sp.wait_ge(routed, 2 * i + (u - 1))
                            load(sp, 2 * i + u, u)

                @block.gpsimd
                def _(pool):
                    def gather(i, u, again):
                        pool.wait_ge(rec_in[u], 16 * (i + 1))
                        for g in range(GB // GSEM):
                            if again:
                                pool.wait_ge(summed, i * (2 * GB) + (u * GB + (g + 1) * GSEM - 2 * GB))
                            pool.sem_inc(step_open, 1)
                            for j in range(g * GSEM, (g + 1) * GSEM):
                                pool.indirect_dma_start(
                                    got[:, u, j, :], None, rows,
                                    bass.IndirectOffsetOnAxis(ap=rec[:, u, j, 0:1].bitcast(U32), axis=0)
                                ).then_inc(gathered[u][g], 16)

                    for u in range(2):
                        gather(0, u, False)
                    with pool.Fori(1, STEPS // 2) as i:
                        for u in range(2):
                            gather(i, u, True)

                @block.vector
                def _(dve):
                    s = Steps(dve, step)
                    prepare(dve, s)
                    dve.engine_nop().then_inc(added, 1)

                    def step_of(i, u, again):
                        dve.wait_ge(rec_in[u], 16 * (i + 1))
                        if again:
                            dve.wait_ge(summed, i * (2 * GB) + (u * GB - GB))
                        for j in range(GB):
                            ins = dve.tensor_scalar(route[:, u, j, :], columns[:], rec[:, u, j, 1:2].bitcast(F32),
                                                    rec[:, u, j, 2:3].bitcast(F32), ALU.is_equal, ALU.mult)
                        ins.then_inc(routed, 1)
                        first = i * (2 * GB) + u * GB
                        _, tiles = nc.values_load_multi_w_load_instructions(
                            chunk_tile[0:1, bass.ds(first, GB)], engines=(mybir.EngineType.DVE,), min_val=0, max_val=NT - 1,
                            skip_runtime_bounds_check_because="the map is clamped to the tiles")
                        for j in range(GB):
                            to = A[:, bass.ds(tiles[j], 1), :].rearrange("p a d -> p (a d)")
                            dve.wait_ge(summed, first + j + 1)
                            dve.wait_ge(added, first + j + 1)
                            dve.tensor_tensor(to, to, psum[:, j % 8, 0:D], ALU.add).then_inc(added, 1)

                    for u in range(2):
                        step_of(0, u, False)
                    with dve.Fori(1, STEPS // 2) as i:
                        for u in range(2):
                            step_of(i, u, True)
                    dve.wait_ge(added, CHUNKS + 1)

                @block.tensor
                def _(pe):
                    def step_of(i, u, again):
                        pe.wait_ge(routed, 2 * i + (u + 1))
                        for j in range(GB):
                            if j % GSEM == 0:
                                pe.wait_ge(gathered[u][j // GSEM], (i + 1) * (16 * GSEM))
                            if again or u * GB + j >= 8:
                                pe.wait_ge(added, i * (2 * GB) + (u * GB + j + 1 - 7))
                            pe.matmul(psum[:, j % 8, 0:D], route[:, u, j, :], got[:, u, j, :],
                                      start=True, stop=True).then_inc(summed, 1)

                    for u in range(2):
                        step_of(0, u, False)
                    with pe.Fori(1, STEPS // 2) as i:
                        for u in range(2):
                            step_of(i, u, True)

        def broadcast_row(eng, to, row, done):
            eng.dma_start(to[:], row.partition_broadcast(P)).then_inc(done, 16)

        with ExitStack() as scope:
            bias0 = sb("bias0", [P, D], at=scope)
            bias0_in = sem("bias0_in")

            def start_from_bias(dve, s):
                dve.wait_ge(bias0_in, 16)
                with s.loop(0, NT, 1) as t:
                    s(dve.tensor_copy(A[:, bass.ds(t, 1), :].rearrange("p a d -> p (a d)"), bias0[:]))

            with nc.Block() as block:
                @block.sync
                def _(sp):
                    broadcast_row(sp, bias0, g0_bias, bias0_in)
                    sp.wait_ge(bias0_in, 16)
            aggregate(table[0], "g0_", start_from_bias)

        ffn = ExitStack()
        mw = sb("mw", [P, NT], at=ffn)
        with ExitStack() as scope, nc.Block() as block:
            here = lambda what, shape, dt=F32: sb("bn_" + what, shape, dt, scope)
            mean = here("mean", [P, D])
            scale = here("scale", [P, D])
            gamma, beta = here("gamma", [P, D]), here("beta", [P, D])
            square = here("square", [P, 2, D])
            wr, br = here("wr", [P, D]), here("br", [P, 1])
            prod = here("prod", [P, D])
            wgt = here("wgt", [P, NT])
            valid = here("valid", [P, NT])
            sign = here("sign", [P, NT], I32)
            key = here("key", [P, NT], I32)
            half_i = here("half_i", [P, NT], I32)
            hi, lo = here("hi", [P, NT]), here("lo", [P, NT])
            junk = here("junk", [P, NT])
            bits = here("bits", [P, 16])
            T_hi, T_lo = here("T_hi", [P, 1]), here("T_lo", [P, 1])
            cand, hits, bit = here("cand", [P, 1]), here("hits", [P, 1]), here("bit", [P, 1])
            want = here("want", [P, 1])
            above, equal = here("above", [P, NT]), here("equal", [P, NT])
            rank, colsum = here("rank", [P, NT]), here("colsum", [P, NT])

            step, params = sem("bn_step"), sem("bn_params")
            summed, centred, squared, spread = sem("bn_summed"), sem("bn_centred"), sem("bn_squared"), sem("bn_spread")
            var_ready, root_ready = sem("bn_var"), sem("bn_root")
            counted, counted_all = sem("topk_counted"), sem("topk_all")

            @block.sync
            def _(sp):
                broadcast_row(sp, gamma, g0_gamma, params)
                broadcast_row(sp, beta, g0_beta, params)
                broadcast_row(sp, wr, f0_wr, params)
                broadcast_row(sp, br, f0_br, params)
                sp.wait_ge(params, 64)

            @block.tensor
            def _(pe):
                def over_nodes(bank, rows, wait):
                    if wait:
                        pe.wait_ge(squared, 1)
                    pe.matmul(psum[:, bank, 0:D], ones[:], rows(0, 0), start=True, stop=False)
                    if wait:
                        pe.matmul(psum[:, 7, 0:1], ones[:], ones[:, 0:1], start=True, stop=True).then_inc(spread, 1)
                        pe.wait_ge(squared, 2)
                        pe.matmul(psum[:, bank, 0:D], ones[:], rows(1, 1), start=False, stop=False).then_inc(spread, 1)
                        with pe.Fori(1, NT // 2) as i:
                            for u in range(2):
                                pe.wait_ge(squared, 2 * i + (u + 1))
                                pe.matmul(psum[:, bank, 0:D], ones[:], rows(0, u), start=False, stop=False).then_inc(spread, 1)
                        pe.wait_ge(squared, NT)
                    else:
                        with pe.Fori(1, NT - 1) as t:
                            pe.matmul(psum[:, bank, 0:D], ones[:], rows(t, 0), start=False, stop=False)
                    pe.matmul(psum[:, bank, 0:D], ones_last[:], rows(NT - 1, 0), start=False, stop=True).then_inc(summed, 1)

                over_nodes(0, lambda t, u: A[:, bass.ds(t, 1), :].rearrange("p a d -> p (a d)"), False)
                over_nodes(1, lambda t, u: square[:, u, :], True)

                with pe.Fori(0, 33) as i:
                    pe.wait_ge(counted, i + 1)
                    pe.matmul(psum[:, 2, 0:1], ones[:], hits[:], start=True, stop=True).then_inc(counted_all, 1)
                pe.wait_ge(counted, 34)
                pe.matmul(psum[:, 2, 0:1], ones[:], hits[:], start=True, stop=True).then_inc(counted_all, 1)
                pe.matmul(psum[:, 3, 0:NT], before[:], equal[:], start=True, stop=True).then_inc(counted_all, 1)
                pe.matmul(psum[:, 4, 0:NT], ones[:], equal[:], start=True, stop=True).then_inc(counted_all, 1)

            @block.scalar
            def _(act):
                def one(t, u, reused):
                    act.wait_ge(centred, t + 1)
                    if reused is not None:
                        act.wait_ge(spread, reused)
                    act.activation(square[:, u, :], A[:, bass.ds(t, 1), :].rearrange("p a d -> p (a d)"),
                                   ACT.Square).then_inc(squared, 1)
                one(0, 0, None)
                one(1, 1, None)
                with act.Fori(1, NT // 2) as i:
                    for u in range(2):
                        one(2 * i + u, u, 2 * i + (u - 1))
                one(NT - 1, 0, NT - 2)
                act.wait_ge(var_ready, 1)
                act.activation(scale[:], scale[:], ACT.Sqrt).then_inc(root_ready, 1)
                row_root(act, var_ready, root_ready, 2)

            @block.vector
            def _(dve):
                s = Steps(dve, step)
                dve.wait_ge(summed, 1)
                s(dve.tensor_scalar(mean[:], psum[:, 0, 0:D], 1.0 / N, None, ALU.mult))
                with dve.Fori(0, NT) as t:
                    row = A[:, bass.ds(t, 1), :].rearrange("p a d -> p (a d)")
                    dve.tensor_tensor(row, row, mean[:], ALU.subtract).then_inc(centred, 1)
                dve.wait_ge(centred, NT)
                dve.wait_ge(summed, 2)
                s(dve.tensor_scalar(scale[:], psum[:, 1, 0:D], 1.0 / N, 1e-5, ALU.mult, ALU.add))
                dve.engine_nop().then_inc(var_ready, 1)
                dve.wait_ge(root_ready, 1)
                s(dve.reciprocal(scale[:], scale[:]))
                dve.wait_ge(params, 64)
                s(dve.tensor_tensor(scale[:], scale[:], gamma[:], ALU.mult))
                with s.loop(0, NT, 3) as t:
                    row = A[:, bass.ds(t, 1), :].rearrange("p a d -> p (a d)")
                    own = X[:, bass.ds(t, 1), :].rearrange("p a d -> p (a d)")
                    s(dve.tensor_tensor(row, row, scale[:], ALU.mult))
                    s(dve.tensor_tensor(row, row, beta[:], ALU.add))
                    s(dve.scalar_tensor_tensor(own, row, 0.0, own, ALU.max, ALU.add))
                row_stats(dve, s, X)
                row_rstd(dve, s, 1e-5, var_ready, root_ready, 2)
                row_normalise(dve, s, A, X)
                with s.loop(0, NT, 3) as t:
                    row = A[:, bass.ds(t, 1), :].rearrange("p a d -> p (a d)")
                    own = X[:, bass.ds(t, 1), :].rearrange("p a d -> p (a d)")
                    s(dve.tensor_tensor(prod[:], row, wr[:], ALU.mult))
                    s(dve.tensor_reduce(wgt[:, bass.ds(t, 1)], prod[:], AX.X, ALU.add))
                    s(dve.tensor_tensor(own, own, row, ALU.add))
                s(dve.tensor_scalar(wgt[:], wgt[:], br[:, 0:1], None, ALU.add))
                s(dve.memset(valid[:], 1.0))
                s(dve.tensor_copy(valid[:, NT - 1:NT], ones_last[:, 0:1]))
                for b in range(16):
                    s(dve.memset(bits[:, b:b + 1], float(1 << (15 - b))))
                w_i = wgt[:].bitcast(I32)
                s(dve.tensor_scalar(sign[:], w_i, 31, -(1 << 31), ALU.arith_shift_right, ALU.bitwise_or))
                s(dve.tensor_tensor(key[:], w_i, sign[:], ALU.bitwise_xor))
                s(dve.tensor_scalar(half_i[:], key[:], 16, 0xFFFF, ALU.logical_shift_right, ALU.bitwise_and))
                s(dve.tensor_copy(hi[:], half_i[:]))
                s(dve.tensor_scalar(half_i[:], key[:], 0xFFFF, None, ALU.bitwise_and))
                s(dve.tensor_copy(lo[:], half_i[:]))
                s(dve.scalar_tensor_tensor(hi[:], hi[:], 1.0, valid[:], ALU.add, ALU.mult))
                s(dve.tensor_scalar(hi[:], hi[:], -1.0, None, ALU.add))
                s(dve.memset(want[:], float(TOPK)))

                def search(keys, T, at):
                    s(dve.memset(T[:], 0.0))
                    with s.loop(0, 16, 3) as b:
                        s(dve.tensor_tensor(cand[:], T[:], bits[:, bass.ds(b, 1)], ALU.add))
                        dve.tensor_scalar(junk[:], keys[:], cand[:, 0:1], 0.0, ALU.is_ge, ALU.add,
                                          accum_out=hits[:]).then_inc(counted, 1)
                        dve.wait_ge(counted_all, b + (at + 1))
                        s(dve.tensor_tensor(bit[:], psum[:, 2, 0:1], want[:], ALU.is_ge))
                        s(dve.scalar_tensor_tensor(T[:], bit[:], bits[:, bass.ds(b, 1)], T[:], ALU.mult, ALU.add))

                search(hi, T_hi, 0)
                s(dve.tensor_scalar(above[:], hi[:], T_hi[:, 0:1], 0.0, ALU.is_gt, ALU.add, accum_out=hits[:]))
                dve.engine_nop().then_inc(counted, 1)
                dve.wait_ge(counted_all, 17)
                s(dve.tensor_tensor(want[:], want[:], psum[:, 2, 0:1], ALU.subtract))
                s(dve.tensor_scalar(equal[:], hi[:], T_hi[:, 0:1], None, ALU.is_equal))
                s(dve.scalar_tensor_tensor(lo[:], lo[:], 1.0, equal[:], ALU.add, ALU.mult))
                s(dve.tensor_scalar(lo[:], lo[:], -1.0, None, ALU.add))
                search(lo, T_lo, 17)
                s(dve.tensor_scalar(junk[:], lo[:], T_lo[:, 0:1], 0.0, ALU.is_gt, ALU.add, accum_out=hits[:]))
                s(dve.tensor_tensor(above[:], above[:], junk[:], ALU.add))
                s(dve.tensor_scalar(equal[:], lo[:], T_lo[:, 0:1], None, ALU.is_equal))
                dve.engine_nop().then_inc(counted, 1)
                dve.wait_ge(counted_all, 36)
                s(dve.tensor_tensor(want[:], want[:], psum[:, 2, 0:1], ALU.subtract))
                s(dve.tensor_copy(colsum[:], psum[:, 4, 0:NT]))
                s(dve.tensor_tensor_scan(rank[:], ones[:, 0:NT], colsum[:], 0.0, ALU.mult, ALU.add))
                s(dve.tensor_tensor(rank[:], rank[:], colsum[:], ALU.subtract))
                s(dve.tensor_tensor(rank[:], rank[:], psum[:, 3, 0:NT], ALU.add))
                s(dve.scalar_tensor_tensor(rank[:], rank[:], want[:, 0:1], equal[:], ALU.is_lt, ALU.mult))
                s(dve.tensor_tensor(above[:], above[:], rank[:], ALU.add))
                s(dve.tensor_tensor(mw[:], wgt[:], above[:], ALU.mult))

        def mlp(name, w1_d, b1_d, w2_d, b2_d, width, function, finish):
            HB = width // P
            with ExitStack() as scope, nc.Block() as block:
                here = lambda what, shape, dt=F32: sb(name + what, shape, dt, scope)
                w1 = here("w1", [P, KD, width])
                w2 = here("w2", [P, HB, D])
                b1 = here("b1", [P, HB])
                b2 = here("b2", [1, D])
                stage = here("stage", [P, 2, D])
                xt = here("xt", [P, KD, GROUP * P])
                ht = here("ht", [P, HB, GROUP * P])
                params = sem(name + "params")
                staged, turned, turned_out = sem(name + "staged"), sem(name + "turned"), sem(name + "turned_out")
                hid, hid_out = sem(name + "hid"), sem(name + "hid_out")
                made, made_out = sem(name + "made"), sem(name + "made_out")
                G = NT // GROUP
                HP = 2 * HB

                @block.sync
                def _(sp):
                    sp.dma_start(w1[:], w1_d.rearrange("(k p) n -> p k n", p=P)).then_inc(params, 16)
                    sp.dma_start(w2[:], w2_d.rearrange("(k p) n -> p k n", p=P)).then_inc(params, 16)
                    sp.dma_start(b1[:], b1_d).then_inc(params, 16)
                    sp.dma_start(b2[:], b2_d.rearrange("(a n) -> a n", a=1)).then_inc(params, 16)
                    sp.wait_ge(params, 64)

                @block.gpsimd
                def _(pool):
                    def group(g, again):
                        for m in range(GROUP):
                            if again or m >= 2:
                                pool.wait_ge(turned, g * GROUP + max(m - 1, 0))
                            pool.tensor_copy(stage[:, m % 2, :], A[:, bass.ds(g * GROUP + m, 1), :]
                                             .rearrange("p a d -> p (a d)")).then_inc(staged, 1)

                    group(0, False)
                    with pool.Fori(1, G) as g:
                        group(g, True)

                @block.tensor
                def _(pe):
                    pe.wait_ge(params, 64)

                    def group(g, again):
                        for m in range(GROUP):
                            if again or m >= 2:
                                pe.wait_ge(turned_out, g * GROUP + max(m - 1, 0))
                            pe.wait_ge(staged, g * GROUP + (m + 1))
                            for k in range(KD):
                                ins = pe.transpose(psum[:, m % 2, k * P:(k + 1) * P], stage[:, m % 2, k * P:(k + 1) * P],
                                                   ident[:])
                            ins.then_inc(turned, 1)
                        pe.wait_ge(turned_out, (g + 1) * GROUP)
                        for n in range(HP):
                            b, h = n // 2, n % 2
                            if again or n >= 4:
                                pe.wait_ge(hid_out, g * HP + (n - 3))
                            for k in range(KD):
                                ins = pe.matmul(psum[:, 2 + n % 4, 0:HALF], w1[:, k, b * P:(b + 1) * P],
                                                xt[:, k, h * HALF:(h + 1) * HALF], start=k == 0, stop=k == KD - 1)
                            ins.then_inc(hid, 1)
                        pe.wait_ge(hid_out, (g + 1) * HP)
                        for m in range(GROUP):
                            if again or m >= 2:
                                pe.wait_ge(made_out, g * GROUP + max(m - 1, 0))
                            for b in range(HB):
                                pe.matmul(psum[:, 6 + m % 2, 0:D], ht[:, b, m * P:(m + 1) * P], w2[:, b, :],
                                          start=b == 0, stop=False)
                            pe.matmul(psum[:, 6 + m % 2, 0:D], ones[0:1, :], b2[:], start=False, stop=True).then_inc(made, 1)

                    group(0, False)
                    with pe.Fori(1, G) as g:
                        group(g, True)

                @block.scalar
                def _(act):
                    act.wait_ge(params, 64)

                    def group(g, again):
                        for n in range(HP):
                            b, h = n // 2, n % 2
                            act.wait_ge(hid, g * HP + (n + 1))
                            if again and n == 0:
                                act.wait_ge(made, g * GROUP)
                            act.activation(ht[:, b, h * HALF:(h + 1) * HALF], psum[:, 2 + n % 4, 0:HALF], function,
                                           bias=b1[:, b:b + 1]).then_inc(hid_out, 1)

                    group(0, False)
                    with act.Fori(1, G) as g:
                        group(g, True)

                @block.vector
                def _(dve):
                    def group(g, again):
                        for m in range(GROUP):
                            dve.wait_ge(turned, g * GROUP + (m + 1))
                            if again and m == 0:
                                dve.wait_ge(hid, g * HP)
                            dve.tensor_copy(xt[:, :, m * P:(m + 1) * P],
                                            psum[:, m % 2, 0:D].rearrange("p (k n) -> p k n", k=KD)).then_inc(turned_out, 1)
                        for m in range(GROUP):
                            dve.wait_ge(made, g * GROUP + (m + 1))
                            finish(dve, g * GROUP + m, psum[:, 6 + m % 2, 0:D]).then_inc(made_out, 1)

                    group(0, False)
                    with dve.Fori(1, G) as g:
                        group(g, True)
                    dve.wait_ge(made_out, NT)

        def token_finish(dve, t, product):
            own = X[:, bass.ds(t, 1), :].rearrange("p a d -> p (a d)")
            return dve.scalar_tensor_tensor(own, product, mw[:, bass.ds(t, 1)], own, ALU.mult, ALU.add)

        mlp("f0_", f0_w1, f0_b1, f0_w2, f0_b2, f0_w1.shape[1], ACT.Gelu_apprx_tanh, token_finish)
        ffn.close()

        with ExitStack() as scope, nc.Block() as block:
            eps1 = sb("eps1", [P, 1], at=scope)
            step, eps_in = sem("t1_step"), sem("t1_eps_in")
            var_ready, root_ready, rows_ready, stored = sem("t1_var"), sem("t1_root"), sem("t1_rows"), sem("t1_stored")

            @block.sync
            def _(sp):
                broadcast_row(sp, eps1, g1_eps, eps_in)
                sp.wait_ge(rows_ready, 1)
                sp.dma_start(table[1].rearrange("(t p) d -> p t d", p=P), A[:]).then_inc(stored, 16)
                sp.wait_ge(stored, 16)

            @block.scalar
            def _(act):
                row_root(act, var_ready, root_ready)

            @block.vector
            def _(dve):
                s = Steps(dve, step)
                row_stats(dve, s, X)
                row_rstd(dve, s, 1e-5, var_ready, root_ready)
                row_normalise(dve, s, A, X)
                dve.engine_nop().then_inc(rows_ready, 1)
                dve.wait_ge(eps_in, 16)
                s(dve.tensor_scalar(eps1[:], eps1[:], 1.0, None, ALU.add))
                dve.wait_ge(stored, 16)
                with s.loop(0, NT, 1) as t:
                    row = A[:, bass.ds(t, 1), :].rearrange("p a d -> p (a d)")
                    s(dve.tensor_scalar(row, row, eps1[:, 0:1], None, ALU.mult))

        aggregate(table[1], "g1_", lambda dve, s: None)

        def relu_finish(dve, t, product):
            row = A[:, bass.ds(t, 1), :].rearrange("p a d -> p (a d)")
            return dve.tensor_scalar(row, product, 0.0, None, ALU.max)

        mlp("m1_", g1_w1, g1_b1, g1_w2, g1_b2, D, ACT.Relu, relu_finish)

        moe = ExitStack()
        expert = sb("expert", [1, P], I32, at=moe)
        slot = sb("slot", [P, 2 * NT], I32, at=moe)
        share = sb("share", [P, NT, 2], at=moe)
        with ExitStack() as scope, nc.Block() as block:
            here = lambda what, shape, dt=F32: sb("r_" + what, shape, dt, scope)
            C = 2 * NT
            scale, offset = here("scale", [P, D]), here("offset", [P, D])
            wr, br = here("wr", [P, KD, NE]), here("br", [1, NE])
            stage = here("stage", [P, 2, D])
            xt = here("xt", [P, 2, KD, P])
            logit, work, work2 = here("logit", [P, NT, NE]), here("work", [P, NT, NE]), here("work2", [P, NT, NE])
            hot = here("hot", [P, NT, 2, NE])
            top = here("top", [P, NT, 2])
            pick = here("pick", [P, NT])
            expo, total = here("expo", [P, NT, NE]), here("total", [P, NT])
            prob = here("prob", [P, NT, 2])
            sums = here("sums", [P, NE, C + 1])
            keep = here("keep", [P, NE, C + 1])
            upto = here("upto", [P, NE, C + 1])
            ntile_i, ntile = here("ntile_i", [P, NE], I32), here("ntile", [P, NE])
            tiles_upto, first = here("tiles_upto", [P, NE]), here("first", [P, NE])
            at = here("at", [P, C, NE])
            slot_f = here("slot_f", [P, C])
            past, exp_f, exp_i = here("past", [P, NE]), here("exp_f", [P, 1]), here("exp_i", [P, 1], I32)

            step, params = sem("r_step"), sem("r_params")
            var_ready, root_ready = sem("r_var"), sem("r_root")
            rows_ready, staged = sem("r_rows"), sem("r_staged")
            turned, turned_out, scored = sem("r_turned"), sem("r_turned_out"), sem("r_scored")
            exp_ask, exp_done = sem("r_exp_ask"), sem("r_exp_done")
            hot_ready, ranked = sem("r_hot"), sem("r_ranked")
            map_ready, map_out, map_in = sem("r_map_ready"), sem("r_map_out"), sem("r_map_in")
            slots_ready, placed = sem("r_slots_ready"), sem("r_placed")

            @block.sync
            def _(sp):
                broadcast_row(sp, scale, g1_scale, params)
                broadcast_row(sp, offset, g1_offset, params)
                sp.dma_start(wr[:], m_wr.rearrange("(k p) n -> p k n", p=P)).then_inc(params, 16)
                sp.dma_start(br[:], m_br.rearrange("(a n) -> a n", a=1)).then_inc(params, 16)
                sp.wait_ge(params, 64)
                sp.wait_ge(map_ready, 1)
                sp.dma_start(expert_row.rearrange("(p a) -> p a", a=1), exp_i[:],
                             allow_slow_non_contiguous=True).then_inc(map_out, 16)
                sp.wait_ge(map_out, 16)
                sp.dma_start(expert[:], expert_row.rearrange("(a p) -> a p", a=1)).then_inc(map_in, 16)
                sp.wait_ge(map_in, 16)

            @block.scalar
            def _(act):
                row_root(act, var_ready, root_ready, 1)
                row_root(act, var_ready, root_ready, 2)

                def tile(t, u):
                    act.wait_ge(turned, t + 1)
                    act.copy(xt[:, u, :, :].rearrange("p k n -> p (k n)"), psum[:, u, 0:D]).then_inc(turned_out, 1)
                with act.Fori(0, NT // 2) as i:
                    for u in range(2):
                        tile(2 * i + u, u)
                tile(NT - 1, 0)
                row_root(act, var_ready, root_ready, 3)
                act.wait_ge(exp_ask, 1)
                act.activation(expo[:].rearrange("p t e -> p (t e)"), work[:].rearrange("p t e -> p (t e)"),
                               ACT.Exp).then_inc(exp_done, 1)
                act.activation(prob[:].rearrange("p t e -> p (t e)"), top[:].rearrange("p t e -> p (t e)"),
                               ACT.Exp).then_inc(exp_done, 1)

            @block.tensor
            def _(pe):
                pe.wait_ge(params, 64)

                def tile(t, u, again):
                    pe.wait_ge(staged, t + 1)
                    for k in range(KD):
                        ins = pe.transpose(psum[:, u, k * P:(k + 1) * P], stage[:, u, k * P:(k + 1) * P], ident[:])
                    ins.then_inc(turned, 1)
                    pe.wait_ge(turned_out, t + 1)
                    to = psum[:, 2, bass.ds(t * NE, NE)]
                    for k in range(KD):
                        pe.matmul(to, xt[:, u, k, :], wr[:, k, :], start=k == 0, stop=False)
                    pe.matmul(to, ones[0:1, :], br[:], start=False, stop=True).then_inc(scored, 1)
                with pe.Fori(0, NT // 2) as i:
                    for u in range(2):
                        tile(2 * i + u, u, True)
                tile(NT - 1, 0, True)
                pe.wait_ge(hot_ready, 1)
                flat = hot[:].rearrange("p t k e -> p (t k e)")
                for h in range(2):
                    part_of = flat[:, h * NT * NE:(h + 1) * NT * NE]
                    pe.matmul(psum[:, 3 + h, 0:NT * NE], before[:], part_of, start=True, stop=True).then_inc(ranked, 1)
                    pe.matmul(psum[:, 5 + h, 0:NT * NE], ones[:], part_of, start=True, stop=True).then_inc(ranked, 1)

            @block.gpsimd
            def _(pool):
                def stage_tile(t, u, earlier):
                    if earlier is not None:
                        pool.wait_ge(turned, earlier)
                    pool.tensor_copy(stage[:, u, :], A[:, bass.ds(t, 1), :].rearrange("p a d -> p (a d)")).then_inc(staged, 1)

                pool.wait_ge(rows_ready, 1)
                for t in range(2):
                    stage_tile(t, t, None)
                with pool.Fori(1, NT // 2) as i:
                    for u in range(2):
                        stage_tile(2 * i + u, u, 2 * i + (u - 1))
                stage_tile(NT - 1, 0, NT - 2)
                pool.wait_ge(slots_ready, 1)
                for t in range(NT):
                    for k in range(2):
                        c = 2 * t + k
                        pool.indirect_dma_start(
                            slots_in, bass.IndirectOffsetOnAxis(ap=slot[:, c:c + 1].bitcast(U32), axis=0),
                            A[:, t, :], None).then_inc(placed, 16)
                pool.wait_ge(placed, 16 * C)

            @block.vector
            def _(dve):
                s = Steps(dve, step)
                row_stats(dve, s, A)
                row_rstd(dve, s, 1e-10, var_ready, root_ready, 1)
                row_normalise(dve, s, A, A)
                dve.wait_ge(params, 64)
                with s.loop(0, NT, 3) as t:
                    row = A[:, bass.ds(t, 1), :].rearrange("p a d -> p (a d)")
                    own = X[:, bass.ds(t, 1), :].rearrange("p a d -> p (a d)")
                    s(dve.tensor_tensor(row, row, scale[:], ALU.mult))
                    s(dve.tensor_tensor(row, row, offset[:], ALU.add))
                    s(dve.tensor_tensor(own, own, row, ALU.add))
                row_stats(dve, s, X)
                row_rstd(dve, s, 1e-5, var_ready, root_ready, 2)
                row_normalise(dve, s, A, X)
                dve.engine_nop().then_inc(rows_ready, 1)
                row_stats(dve, s, A)
                row_rstd(dve, s, 1e-5, var_ready, root_ready, 3)
                dve.wait_ge(scored, NT)
                row_normalise(dve, s, A, A)

                s(dve.tensor_copy(logit[:].rearrange("p t e -> p (t e)"), psum[:, 2, 0:NT * NE]))
                numbers = columns[:, 0:NE].unsqueeze(1).to_broadcast([P, NT, NE])
                wide = lambda a: a.unsqueeze(2).to_broadcast([P, NT, NE])

                def best(k, scores):
                    s(dve.tensor_reduce(top[:, :, k], scores[:], AX.X, ALU.max))
                    s(dve.tensor_tensor(work2[:], scores[:], wide(top[:, :, k]), ALU.is_equal))
                    s(dve.tensor_scalar(work2[:], work2[:], -float(NE), float(NE), ALU.mult, ALU.add))
                    s(dve.tensor_tensor(work2[:], work2[:], numbers, ALU.add))
                    s(dve.tensor_reduce(pick[:], work2[:], AX.X, ALU.min))
                    s(dve.tensor_tensor(hot[:, :, k, :], numbers, wide(pick[:]), ALU.is_equal))

                best(0, logit)
                s(dve.scalar_tensor_tensor(work[:], hot[:, :, 0, :], -1e30, logit[:], ALU.mult, ALU.add))
                best(1, work)
                dve.engine_nop().then_inc(hot_ready, 1)
                s(dve.tensor_tensor(work[:], logit[:], wide(top[:, :, 0]), ALU.subtract))
                s(dve.tensor_copy(pick[:], top[:, :, 0]))
                s(dve.tensor_tensor(top[:], top[:], pick[:].unsqueeze(2).to_broadcast([P, NT, 2]), ALU.subtract))
                dve.engine_nop().then_inc(exp_ask, 1)
                dve.wait_ge(exp_done, 2)
                s(dve.tensor_reduce(total[:], expo[:], AX.X, ALU.add))
                s(dve.reciprocal(total[:], total[:]))
                s(dve.tensor_tensor(prob[:], prob[:], total[:].unsqueeze(2).to_broadcast([P, NT, 2]), ALU.mult))
                s(dve.tensor_reduce(total[:], prob[:], AX.X, ALU.add))
                s(dve.reciprocal(total[:], total[:]))
                s(dve.tensor_tensor(share[:], prob[:], total[:].unsqueeze(2).to_broadcast([P, NT, 2]), ALU.mult))
                s(dve.memset(keep[:], 1.0))
                s(dve.memset(keep[:, :, 0:1], 0.0))
                s(dve.memset(sums[:, :, 0:1], 0.0))
                dve.wait_ge(ranked, 4)
                for h in range(2):
                    s(dve.tensor_copy(sums[:, :, 1 + h * NT:1 + (h + 1) * NT],
                                      psum[:, 5 + h, 0:NT * NE].rearrange("p (c e) -> p e c", e=NE)))
                s(dve.tensor_tensor_scan(upto[:].rearrange("p e c -> p (e c)"), keep[:].rearrange("p e c -> p (e c)"),
                                         sums[:].rearrange("p e c -> p (e c)"), 0.0, ALU.mult, ALU.add))
                s(dve.tensor_scalar(ntile_i[:], upto[:, :, C], float(MT - 1), None, ALU.add))
                s(dve.tensor_scalar(ntile_i[:], ntile_i[:], 8, None, ALU.logical_shift_right))
                s(dve.tensor_copy(ntile[:], ntile_i[:]))
                s(dve.tensor_tensor_scan(tiles_upto[:], ones[:, 0:NE], ntile[:], 0.0, ALU.mult, ALU.add))
                s(dve.tensor_tensor(first[:], tiles_upto[:], ntile[:], ALU.subtract))
                s(dve.tensor_scalar(first[:], first[:], float(MT), None, ALU.mult))
                for h in range(2):
                    s(dve.tensor_tensor(at[:, h * NT:(h + 1) * NT, :], psum[:, 3 + h, 0:NT * NE].rearrange("p (c e) -> p c e", e=NE),
                                        upto[:, :, h * NT:(h + 1) * NT].rearrange("p e c -> p c e"), ALU.add))
                s(dve.tensor_tensor(at[:], at[:], first[:].unsqueeze(1).to_broadcast([P, C, NE]), ALU.add))
                s(dve.tensor_tensor(at[:], at[:], hot[:].rearrange("p t k e -> p (t k) e"), ALU.mult))
                s(dve.tensor_reduce(slot_f[:], at[:], AX.X, ALU.add))
                s(dve.tensor_copy(slot[:], slot_f[:]))
                dve.engine_nop().then_inc(slots_ready, 1)
                s(dve.tensor_scalar(past[:], tiles_upto[:], part[:, 0:1], None, ALU.is_le))
                s(dve.tensor_reduce(exp_f[:], past[:], AX.X, ALU.add))
                s(dve.tensor_scalar(exp_i[:], exp_f[:], float(NE - 1), None, ALU.min))
                dve.engine_nop().then_inc(map_ready, 1)

        HB = HM // P
        with ExitStack() as scope, nc.Block() as block:
            here = lambda what, shape, dt=F32: sb("e_" + what, shape, dt, scope)
            w1, w2 = here("w1", [P, 2, KD, HM]), here("w2", [P, 2, HB, D])
            gain, shift, b1 = here("gain", [P, 2, KD]), here("shift", [P, 2, KD]), here("b1", [P, 2, HB])
            b2 = here("b2", [1, 2, D])
            rows = here("rows", [P, 2, 2, D])
            xt = here("xt", [P, 2, KD, MT])
            ht = here("ht", [P, 2, HB, MT])
            y = here("y", [P, 2, 2, D])
            loaded = [sem("e_loaded0"), sem("e_loaded1")]
            turned, turned_out = sem("e_turned"), sem("e_turned_out")
            hid, hid_out = sem("e_hid"), sem("e_hid_out")
            made, made_out = sem("e_made"), sem("e_made_out")
            stored = [sem("e_stored0"), sem("e_stored1")]
            LOADS = 7
            PAIRS = MTILES // 2

            @block.sync
            def _(sp):
                def load(n, u):
                    e = sp.value_load(expert[0:1, bass.ds(n, 1)], min_val=0, max_val=NE - 1)
                    one = bass.ds(e, 1)
                    sp.dma_start(rows[:, u, :, :], slots_in[bass.ts(n, MT), :].rearrange("(s p) d -> p s d", p=P)).then_inc(loaded[u], 16)
                    sp.dma_start(w1[:, u, :, :], m_w1[one, :, :, :].rearrange("a p k n -> p (a k) n")).then_inc(loaded[u], 16)
                    sp.dma_start(w2[:, u, :, :], m_w2[one, :, :, :].rearrange("a p k n -> p (a k) n")).then_inc(loaded[u], 16)
                    sp.dma_start(gain[:, u, :], m_g[one, :, :].rearrange("a p k -> p (a k)")).then_inc(loaded[u], 16)
                    sp.dma_start(shift[:, u, :], m_b[one, :, :].rearrange("a p k -> p (a k)")).then_inc(loaded[u], 16)
                    sp.dma_start(b1[:, u, :], m_b1[one, :, :].rearrange("a p k -> p (a k)")).then_inc(loaded[u], 16)
                    sp.dma_start(b2[:, u, :], m_b2[one, :]).then_inc(loaded[u], 16)
                load(0, 0)
                load(1, 1)
                with sp.Fori(1, PAIRS) as i:
                    for u in range(2):
                        sp.wait_ge(made, 4 * i + (2 * u - 2))
                        load(2 * i + u, u)

            @block.tensor
            def _(pe):
                def turn(i, u, again):
                    pe.wait_ge(loaded[u], (i + 1) * (16 * LOADS))
                    if again:
                        pe.wait_ge(turned_out, 4 * i + 2 * u)
                    for k in range(KD):
                        for m in range(2):
                            ins = pe.transpose(psum[:, 0, k * MT + m * P:k * MT + (m + 1) * P],
                                               rows[:, u, m, k * P:(k + 1) * P], ident[:])
                    ins.then_inc(turned, 1)

                def hidden(i, u, again):
                    pe.wait_ge(turned_out, 4 * i + 2 * (u + 1))
                    for b in range(HB):
                        if again or u * HB + b >= 4:
                            pe.wait_ge(hid_out, i * (2 * HB) + (u * HB + b - 3))
                        for k in range(KD):
                            ins = pe.matmul(psum[:, 1 + b % 4, 0:MT], w1[:, u, k, b * P:(b + 1) * P], xt[:, u, k, :],
                                            start=k == 0, stop=k == KD - 1)
                        ins.then_inc(hid, 1)

                def product(i, u, again):
                    pe.wait_ge(hid_out, i * (2 * HB) + (u + 1) * HB)
                    for m in range(2):
                        if again:
                            pe.wait_ge(made_out, 4 * i + (2 * u + m - 1))
                        for b in range(HB):
                            pe.matmul(psum[:, 5 + m, 0:D], ht[:, u, b, m * P:(m + 1) * P], w2[:, u, b, :],
                                      start=b == 0, stop=False)
                        pe.matmul(psum[:, 5 + m, 0:D], ones[0:1, :], b2[:, u, :], start=False, stop=True).then_inc(made, 1)

                turn(0, 0, False)
                hidden(0, 0, False)
                turn(0, 1, True)
                product(0, 0, False)
                with pe.Fori(0, PAIRS - 1) as i:
                    hidden(i, 1, True)
                    turn(i + 1, 0, True)
                    product(i, 1, True)
                    hidden(i + 1, 0, True)
                    turn(i + 1, 1, True)
                    product(i + 1, 0, True)
                hidden(PAIRS - 1, 1, True)
                product(PAIRS - 1, 1, True)

            @block.vector
            def _(dve):
                def tile(i, u, again):
                    dve.wait_ge(turned, 2 * i + (u + 1))
                    if again:
                        dve.wait_ge(hid, i * (2 * HB) + (u * HB - HB))
                    for k in range(KD):
                        dve.tensor_scalar(xt[:, u, k, :], psum[:, 0, k * MT:(k + 1) * MT], gain[:, u, k:k + 1],
                                          shift[:, u, k:k + 1], ALU.mult, ALU.add).then_inc(turned_out, 1)

                def result(i, u, again):
                    if again:
                        dve.wait_ge(stored[u], 16 * i)
                    for m in range(2):
                        dve.wait_ge(made, 4 * i + (2 * u + m + 1))
                        dve.tensor_copy(y[:, u, m, :], psum[:, 5 + m, 0:D]).then_inc(made_out, 1)

                tile(0, 0, False)
                tile(0, 1, False)
                result(0, 0, False)
                tile(1, 0, True)
                result(0, 1, False)
                tile(1, 1, True)
                with dve.Fori(1, PAIRS - 1) as i:
                    for u in range(2):
                        result(i, u, True)
                        tile(i + 1, u, True)
                result(PAIRS - 1, 0, True)
                result(PAIRS - 1, 1, True)

            @block.scalar
            def _(act):
                def store(i, u):
                    act.wait_ge(made_out, 4 * i + 2 * (u + 1))
                    act.dma_start(slots_out[bass.ts(2 * i + u, MT), :].rearrange("(s p) d -> p s d", p=P),
                                  y[:, u, :, :]).then_inc(stored[u], 16)

                def hidden(i, u, again):
                    if again:
                        act.wait_ge(made, 4 * i + (2 * u - 2))
                    act.wait_ge(loaded[u], (i + 1) * (16 * LOADS))
                    for b in range(HB):
                        act.wait_ge(hid, i * (2 * HB) + (u * HB + b + 1))
                        act.activation(ht[:, u, b, :], psum[:, 1 + b % 4, 0:MT], ACT.Gelu,
                                       bias=b1[:, u, b:b + 1]).then_inc(hid_out, 1)

                hidden(0, 0, False)
                hidden(0, 1, False)
                store(0, 0)
                with act.Fori(1, PAIRS) as i:
                    hidden(i, 0, True)
                    store(i - 1, 1)
                    hidden(i, 1, True)
                    store(i, 0)
                store(PAIRS - 1, 1)
                for u in range(2):
                    act.wait_ge(stored[u], 16 * PAIRS)

        RING = 2 * GROUP
        with ExitStack() as scope, nc.Block() as block:
            got = sb("c_got", [P, RING, D], at=scope)
            fetched = [sem(f"c_fetched{r}") for r in range(RING)]
            added = sem("c_added")
            stored = sem("c_stored")

            @block.gpsimd
            def _(pool):
                for c in range(2 * NT):
                    if c >= RING:
                        pool.wait_ge(added, c - RING + 1)
                    pool.indirect_dma_start(got[:, c % RING, :], None, slots_out,
                                            bass.IndirectOffsetOnAxis(ap=slot[:, c:c + 1].bitcast(U32), axis=0)
                                            ).then_inc(fetched[c % RING], 16)

            @block.vector
            def _(dve):
                with dve.Fori(0, NT // GROUP) as g:
                    for r in range(RING):
                        own = X[:, bass.ds(g * GROUP + r // 2, 1), :].rearrange("p a d -> p (a d)")
                        dve.wait_ge(fetched[r], (g + 1) * 16)
                        if r % 2:
                            dve.wait_ge(added, g * RING + r)
                        dve.scalar_tensor_tensor(own, got[:, r, :], share[:, bass.ds(g * GROUP + r // 2, 1), r % 2], own,
                                                 ALU.mult, ALU.add).then_inc(added, 1)

            @block.sync
            def _(sp):
                sp.wait_ge(added, 2 * NT)
                sp.dma_start(by_node(out), X[:, 0:NT - 1, :]).then_inc(stored, 16)
                sp.dma_start(out[(NT - 1) * P:N, :], X[0:NLAST, NT - 1, :]).then_inc(stored, 16)
                sp.wait_ge(stored, 32)
        moe.close()


def kernel(x, src, dst, edge_weight, L0_gnn_W, L0_gnn_bias, L0_gnn_gamma, L0_gnn_beta, L0_ffn_attention_mask, L0_ffn_wr,
           L0_ffn_br, L0_ffn_w1, L0_ffn_b1, L0_ffn_w2, L0_ffn_b2, L1_gnn_W1, L1_gnn_b1, L1_gnn_W2, L1_gnn_b2, L1_gnn_eps,
           L1_gnn_offset, L1_gnn_scale, L1_ffn_Wr, L1_ffn_br, L1_ffn_ln_g, L1_ffn_ln_b, L1_ffn_W1, L1_ffn_b1, L1_ffn_W2,
           L1_ffn_b2):
    import numpy as np
    import concourse.bacc as bacc
    from concourse.bass_utils import run_bass_kernel_spmd

    def blocks(a):
        return np.asarray(a).reshape(NE, -1, P).transpose(0, 2, 1)

    def weight_blocks(a):
        a = np.asarray(a)
        return a.reshape(NE, -1, P, a.shape[2]).transpose(0, 2, 1, 3)

    column_blocks = lambda a: np.asarray(a).reshape(-1, P).T
    flat = lambda a: np.asarray(a).reshape(-1)
    laid = {
        "x": x, "src": src, "dst": dst, "edge_weight": edge_weight, "g0_w": L0_gnn_W, "g0_bias": L0_gnn_bias,
        "g0_gamma": L0_gnn_gamma, "g0_beta": L0_gnn_beta, "f0_wr": flat(L0_ffn_wr), "f0_br": L0_ffn_br,
        "f0_w1": L0_ffn_w1, "f0_b1": column_blocks(L0_ffn_b1), "f0_w2": L0_ffn_w2, "f0_b2": L0_ffn_b2,
        "g1_w1": L1_gnn_W1, "g1_b1": column_blocks(L1_gnn_b1), "g1_w2": L1_gnn_W2, "g1_b2": L1_gnn_b2,
        "g1_eps": L1_gnn_eps, "g1_offset": L1_gnn_offset, "g1_scale": L1_gnn_scale, "m_wr": L1_ffn_Wr, "m_br": L1_ffn_br,
        "m_g": blocks(L1_ffn_ln_g), "m_b": blocks(L1_ffn_ln_b), "m_w1": weight_blocks(L1_ffn_W1),
        "m_b1": blocks(L1_ffn_b1), "m_w2": weight_blocks(L1_ffn_W2), "m_b2": L1_ffn_b2,
    }
    nc = bacc.Bacc("TRN2", target_bir_lowering=False, num_devices=1)
    arrays = {name: np.ascontiguousarray(a) for name, a in laid.items()}
    args = {name: nc.dram_tensor("in_" + name, a.shape, mybir.dt.from_np(a.dtype), kind="ExternalInput").ap()
            for name, a in arrays.items()}
    out = nc.dram_tensor("out", (N, D), F32, kind="ExternalOutput").ap()
    build(nc, **args, out=out)
    r = run_bass_kernel_spmd(nc, [{"in_" + name: a for name, a in arrays.items()}], core_ids=[0])
    return r.results[0]["out"]
```

```python
from contextlib import ExitStack, contextmanager

import concourse.bass as bass
from concourse import mybir

ALU = mybir.AluOpType
ACT = mybir.ActivationFunctionType
AX = mybir.AxisListType
F32 = mybir.dt.float32
I32 = mybir.dt.int32
U32 = mybir.dt.uint32

P = 128
D = 256
KD = D // P
N = 6250
NT = -(-N // P)
NLAST = N - (NT - 1) * P
E = 100000
EJ = -(-E // P)
ETAIL = E - (P - 1) * EJ
NB = NT + 1
SORT_J = 23
SORT_STEPS = EJ // SORT_J
CHUNKS = -(-((E + NT * (P - 1)) // P + 1) // 32) * 32
REC = 4
GB = 16
GSEM = 4
BANK = 512
GROUP = 7
GROUPS = NT // GROUP
HALF = GROUP * P // 2
TOPK = max(1, int(0.5 * N)) - 1
NE = 8
HM = 1024
MT = 2 * P
MTILES = (2 * NT * P + NE * (MT - 1)) // MT
ZEROS = MTILES // 4
assert SORT_STEPS * SORT_J == EJ and SORT_STEPS % 2 == 0 and NT % GROUP == 0 and GROUPS % 2 == 1 and MTILES % 4 == 0


class Steps:

    def __init__(self, engine, sem):
        self.engine, self.sem, self.base, self.n = engine, sem, 0, 0

    def __call__(self, instruction):
        self.n += 1
        instruction.then_inc(self.sem, 1)
        self.engine.wait_ge(self.sem, self.base + self.n)

    @contextmanager
    def loop(self, first, last, per):
        start = self.base + self.n
        with self.engine.Fori(first, last) as i:
            self.base, self.n = (i - first) * per + start, 0
            yield i
            assert self.n == per, self.n
        self.base, self.n = start + (last - first) * per, 0


def build(nc, x, src, dst, edge_weight, g0_w, g0_bias, g0_gamma, g0_beta, f0_wr, f0_br, f0_w1, f0_b1, f0_w2, f0_b2,
          g1_w1, g1_b1, g1_w2, g1_b2, g1_eps, g1_offset, g1_scale, m_wr, m_br, m_g, m_b, m_w1, m_b1, m_w2, m_b2, out):
    dram = lambda name, shape, dt=F32: nc.dram_tensor(name, shape, dt, kind="Internal").ap()
    table = [dram("table0", (NT * P, D)), dram("table1", (NT * P, D))]
    records = dram("records", (P * CHUNKS, REC), I32)
    chunk_tile_row = dram("chunk_tile_row", (7 * P,), I32)
    slots_in = dram("slots_in", (MTILES * MT, D))
    slots_out = dram("slots_out", (MTILES * MT, D))
    expert_row = dram("expert_row", (P,), I32)
    by_node = lambda a: a[0:(NT - 1) * P, :].rearrange("(t p) d -> p t d", p=P)

    ctx = ExitStack()
    with ctx:
        def sem(name):
            return ctx.enter_context(nc.semaphore(name))

        def sb(name, shape, dt=F32, at=None):
            return (at or ctx).enter_context(nc.sbuf_tensor(name, shape, dt))

        psum = ctx.enter_context(nc.psum_tensor("psum", [P, 8, BANK], F32))

        X = sb("X", [P, NT, D])
        ident = sb("ident", [P, P])
        columns = sb("columns", [P, P])
        before = sb("before", [P, P])
        ones = sb("ones", [P, P])
        ones_last = sb("ones_last", [P, P])
        part = sb("part", [P, 1])
        chunk_tile = sb("chunk_tile", [1, 7 * P], I32)
        stats = sb("stats", [P, NT, 6])
        moments = sb("moments", [P, NT, 2])
        rstd = sb("rstd", [P, NT])
        mw = sb("mw", [P, NT])
        expert = sb("expert", [1, P], I32)
        slot = sb("slot", [P, 2 * NT], I32)
        share = sb("share", [P, NT, 2])
        wgt = sb("wgt", [P, NT])
        f0_br_row = sb("f0_br_row", [P, 1])
        offset = sb("offset", [P, D])
        scale1 = sb("scale1", [P, D])

        def row(of, t):
            return of[:, bass.ds(t, 1), :].rearrange("p a d -> p (a d)")

        def group_rows(of, g):
            return of[:, bass.ts(g, GROUP), :]

        def over_groups(engine, body):
            body(0, 0, False)
            body(1, 1, False)
            with engine.Fori(1, GROUPS // 2) as i:
                body(2 * i, 0, True)
                body(2 * i + 1, 1, True)
            body(GROUPS - 1, 0, True)

        def row_stats(dve, steps, rows, before_tile=None):
            with steps.loop(0, GROUPS, 1) as g:
                for m in range(GROUP):
                    if before_tile:
                        before_tile(g * GROUP + m)
                    ins = dve.bn_stats(row(stats, g * GROUP + m), row(rows, g * GROUP + m))
                steps(ins)
            mean, var = moments[:, :, 0], moments[:, :, 1]
            steps(dve.tensor_tensor(mean, stats[:, :, 1], stats[:, :, 4], ALU.add))
            steps(dve.tensor_scalar(mean, mean, 0.5, None, ALU.mult))
            steps(dve.tensor_tensor(rstd[:], stats[:, :, 1], stats[:, :, 4], ALU.subtract))
            steps(dve.scalar_tensor_tensor(rstd[:], rstd[:], 0.25, rstd[:], ALU.mult, ALU.mult))
            steps(dve.tensor_tensor(var, stats[:, :, 2], stats[:, :, 5], ALU.add))
            steps(dve.scalar_tensor_tensor(var, var, 1.0 / D, rstd[:], ALU.mult, ALU.add))

        def row_rstd(dve, steps, eps, var_ready, root_ready, n=1):
            dve.tensor_scalar(rstd[:], moments[:, :, 1], eps, None, ALU.add).then_inc(var_ready, 1)
            dve.wait_ge(root_ready, n)
            steps(dve.reciprocal(rstd[:], rstd[:]))

        def row_root(act, var_ready, root_ready, n=1):
            act.wait_ge(var_ready, n)
            act.activation(rstd[:], rstd[:], ACT.Sqrt).then_inc(root_ready, 1)

        def normalise_tile(dve, to, rows, t):
            return dve.tensor_scalar(to, row(rows, t), moments[:, bass.ds(t, 1), 0], rstd[:, bass.ds(t, 1)],
                                     ALU.subtract, ALU.mult)

        with ExitStack() as scope, nc.Block() as block:
            here = lambda name, shape, dt=F32: sb(name, shape, dt, scope)
            src_i = here("src_i", [P, EJ], I32)
            dst_i = here("dst_i", [P, EJ], I32)
            w_e = here("w_e", [P, EJ])
            tile_i = here("tile_i", [P, EJ], I32)
            tile_f = here("tile_f", [P, EJ])
            local_f = here("local_f", [P, EJ])
            junk = here("junk", [P, EJ])
            count = here("count", [P, NB])
            nchunk_i = here("nchunk_i", [P, NB], I32)
            nchunk = here("nchunk", [P, NB])
            upto = here("upto", [P, NB])
            first = here("first", [P, NB])
            chunk_no_i = here("chunk_no_i", [P, 7], I32)
            chunk_no = here("chunk_no", [P, 7])
            passed = here("passed", [P, 7, NT])
            chunk_tile_f = here("chunk_tile_f", [P, 7])
            chunk_tile_i = here("chunk_tile_i", [P, 7], I32)
            hot = here("hot", [P, NB, SORT_J + 1])
            keep = here("keep", [P, NB, SORT_J + 1])
            upto_slot = here("upto_slot", [P, NB, SORT_J + 1])
            picked = here("picked", [P, NB, SORT_J])
            slot_f = here("slot_f", [P, SORT_J])
            slot_i = here("slot_i", [P, SORT_J], I32)
            slot_q = here("slot_q", [P, SORT_J], I32)
            slot_c = here("slot_c", [P, SORT_J], I32)
            place = here("place", [P, 2, SORT_J], I32)
            rec = here("rec", [P, 2, SORT_J, REC], I32)
            zero = here("zero", [P, CHUNKS * REC], I32)
            iota_i = here("iota_i", [P, P], I32)
            part_i = here("part_i", [P, 1], I32)
            w0 = here("w0", [P, KD, D])
            xn = here("xn", [P, 2, D])
            xt = here("xt", [P, 2, KD, P])
            h_out = here("h_out", [P, 2, D])

            s_step = sem("sort_step")
            loaded = sem("edges_loaded")
            x_loaded = sem("x_loaded")
            w0_loaded = sem("w0_loaded")
            pads_set = sem("pads_set")
            iota_done = sem("iota_done")
            consts_done = sem("consts_done")
            local_done = sem("local_done")
            counted = sem("counted")
            totals = sem("totals")
            zero_set = sem("zero_set")
            prefilled, records_clear = sem("prefilled"), sem("records_clear")
            map_ready = sem("map_ready")
            map_out = sem("map_out")
            map_in = sem("map_in")
            placed = sem("placed")
            rec_filled = sem("rec_filled")
            scattered = [sem("scattered0"), sem("scattered1")]
            step_open = sem("scatter_open")
            var_ready, root_ready = sem("ln0_var"), sem("ln0_root")
            xn_ready = sem("ln0_rows")
            turned, turned_out = sem("h_turned"), sem("h_turned_out")
            made, made_out = sem("h_made"), sem("h_made_out")
            stored = [sem("h_stored0"), sem("h_stored1")]

            @block.sync
            def _(sp):
                sp.wait_ge(pads_set, 4)
                for to, of in ((src_i, src), (dst_i, dst), (w_e, edge_weight)):
                    sp.dma_start(to[0:P - 1, :], of[0:(P - 1) * EJ].rearrange("(p j) -> p j", j=EJ)).then_inc(loaded, 16)
                    sp.dma_start(to[P - 1:P, 0:ETAIL], of[(P - 1) * EJ:E].rearrange("(a j) -> a j", a=1)).then_inc(loaded, 16)
                sp.dma_start(X[:, 0:NT - 1, :], by_node(x)).then_inc(x_loaded, 16)
                sp.dma_start(X[0:NLAST, NT - 1, :], x[(NT - 1) * P:N, :]).then_inc(x_loaded, 16)
                sp.dma_start(w0[:], g0_w.rearrange("(k p) n -> p k n", p=P)).then_inc(w0_loaded, 16)
                sp.wait_ge(zero_set, 1)
                sp.dma_start(records.rearrange("(q c) f -> q (c f)", q=P), zero[:]).then_inc(records_clear, 16)
                sp.wait_ge(map_ready, 1)
                sp.dma_start(chunk_tile_row.rearrange("(k p) -> p k", p=P), chunk_tile_i[:],
                             allow_slow_non_contiguous=True).then_inc(map_out, 16)
                sp.wait_ge(map_out, 16)
                sp.dma_start(chunk_tile[:], chunk_tile_row.rearrange("(a k) -> a k", a=1)).then_inc(map_in, 16)

                for m in range(ZEROS):
                    sp.dma_start(slots_in[m * 4 * MT:(m + 1) * 4 * MT, :].rearrange("(q r) d -> q (r d)", q=P),
                                 zero[:, 0:4 * MT * D // P].bitcast(F32)).then_inc(prefilled, 16)

                def store(t, u):
                    sp.dma_start(table[0][bass.ts(t, P), :], h_out[:, u, :]).then_inc(stored[u], 16)

                with sp.Fori(0, NT // 2) as i:
                    for u in range(2):
                        sp.wait_ge(made_out, 2 * i + (u + 1))
                        store(2 * i + u, u)
                sp.wait_ge(made_out, NT)
                store(NT - 1, 0)
                sp.wait_ge(stored[0], 16 * (NT // 2 + 1))
                sp.wait_ge(stored[1], 16 * (NT // 2))
                sp.wait_ge(map_in, 16)
                sp.wait_ge(prefilled, 16 * ZEROS)

            @block.gpsimd
            def _(pool):
                pool.memset(zero[:], 0).then_inc(zero_set, 1)
                pool.iota(iota_i[:], [[1, P]], base=0, channel_multiplier=0).then_inc(iota_done, 1)
                pool.iota(part_i[:], [[0, 1]], base=0, channel_multiplier=1).then_inc(iota_done, 1)
                pool.iota(chunk_no_i[:], [[P, 7]], base=0, channel_multiplier=1).then_inc(iota_done, 1)
                pool.wait_ge(records_clear, 16)
                with pool.Fori(0, SORT_STEPS // 2) as i:
                    for u in range(2):
                        pool.wait_ge(placed, 2 * i + (u + 1))
                        pool.wait_ge(rec_filled, 6 * i + 3 * (u + 1) + 1)
                        pool.sem_inc(step_open, 1)
                        for j in range(SORT_J):
                            pool.indirect_dma_start(
                                records, bass.IndirectOffsetOnAxis(ap=place[:, u, j:j + 1].bitcast(U32), axis=0),
                                rec[:, u, j, :], None).then_inc(scattered[u], 16)
                for u in range(2):
                    pool.wait_ge(scattered[u], 16 * SORT_J * (SORT_STEPS // 2))

            @block.vector
            def _(dve):
                s = Steps(dve, s_step)
                dve.memset(src_i[:], NT * P).then_inc(pads_set, 1)
                dve.memset(dst_i[:], 0).then_inc(pads_set, 1)
                dve.memset(w_e[:], 0.0).then_inc(pads_set, 1)
                dve.memset(X[:, NT - 1, :], 0.0).then_inc(pads_set, 1)
                dve.wait_ge(iota_done, 3)
                s(dve.tensor_copy(columns[:], iota_i[:]))
                s(dve.tensor_copy(part[:], part_i[:]))
                s(dve.tensor_copy(chunk_no[:], chunk_no_i[:]))
                s(dve.tensor_scalar(ident[:], columns[:], part[:, 0:1], None, ALU.is_equal))
                s(dve.tensor_scalar(before[:], columns[:], part[:, 0:1], None, ALU.is_gt))
                s(dve.memset(ones[:], 1.0))
                s(dve.tensor_scalar(ones_last[:], ones[:], part[:, 0:1], float(NLAST), ALU.mult, ALU.is_lt))
                s(dve.memset(keep[:], 1.0))
                s(dve.memset(keep[:, :, 0:1], 0.0))
                dve.engine_nop().then_inc(consts_done, 1)
                dve.wait_ge(loaded, 96)
                s(dve.tensor_scalar(tile_i[:], src_i[:], 7, None, ALU.logical_shift_right))
                s(dve.tensor_scalar(src_i[:], src_i[:], P - 1, None, ALU.bitwise_and))
                s(dve.tensor_copy(tile_f[:], tile_i[:]))
                dve.tensor_copy(local_f[:], src_i[:]).then_inc(local_done, 1)
                for b in range(NB):
                    s(dve.tensor_scalar(junk[:], tile_f[:], float(b), 0.0, ALU.is_equal, ALU.add,
                                        accum_out=count[:, b:b + 1]))
                dve.engine_nop().then_inc(counted, 1)
                dve.wait_ge(totals, 2)
                s(dve.tensor_scalar(nchunk_i[:], psum[:, 1, 0:NB], float(P - 1), None, ALU.add))
                s(dve.tensor_scalar(nchunk_i[:], nchunk_i[:], 7, None, ALU.logical_shift_right))
                s(dve.tensor_copy(nchunk[:], nchunk_i[:]))
                s(dve.tensor_tensor_scan(upto[:], ones[:, 0:NB], nchunk[:], 0.0, ALU.mult, ALU.add))
                s(dve.tensor_tensor(first[:], upto[:], nchunk[:], ALU.subtract))
                s(dve.scalar_tensor_tensor(first[:], first[:], float(P), psum[:, 0, 0:NB], ALU.mult, ALU.add))
                s(dve.tensor_scalar(upto_slot[:, :, SORT_J], first[:], -1.0, None, ALU.add))
                s(dve.tensor_tensor(passed[:], chunk_no[:].unsqueeze(2).to_broadcast([P, 7, NT]),
                                    upto[:, 0:NT].unsqueeze(1).to_broadcast([P, 7, NT]), ALU.is_ge))
                s(dve.tensor_reduce(chunk_tile_f[:], passed[:], AX.X, ALU.add))
                dve.tensor_scalar(chunk_tile_i[:], chunk_tile_f[:], float(NT - 1), None, ALU.min).then_inc(map_ready, 1)

                def sort_step(k, u, reused):
                    s(dve.tensor_copy(hot[:, :, 0], upto_slot[:, :, SORT_J]))
                    s(dve.tensor_tensor(hot[:, :, 1:], tile_f[:, bass.ts(k, SORT_J)].unsqueeze(1).to_broadcast([P, NB, SORT_J]),
                                        columns[:, 0:NB].unsqueeze(2).to_broadcast([P, NB, SORT_J]), ALU.is_equal))
                    s(dve.tensor_tensor_scan(upto_slot[:].rearrange("p b j -> p (b j)"), keep[:].rearrange("p b j -> p (b j)"),
                                             hot[:].rearrange("p b j -> p (b j)"), 0.0, ALU.mult, ALU.add))
                    s(dve.tensor_tensor(picked[:], hot[:, :, 1:], upto_slot[:, :, 1:], ALU.mult))
                    s(dve.tensor_reduce(slot_f[:], picked[:].rearrange("p b j -> p j b"), AX.X, ALU.add))
                    s(dve.tensor_copy(slot_i[:], slot_f[:]))
                    s(dve.tensor_scalar(slot_q[:], slot_i[:], P - 1, None, ALU.bitwise_and))
                    s(dve.tensor_scalar(slot_c[:], slot_i[:], 7, None, ALU.logical_shift_right))
                    if reused is not None:
                        dve.wait_ge(scattered[u], reused)
                    dve.scalar_tensor_tensor(place[:, u, :], slot_q[:], float(CHUNKS), slot_c[:],
                                             ALU.mult, ALU.add).then_inc(placed, 1)

                for u in range(2):
                    sort_step(u, u, None)
                dve.wait_ge(x_loaded, 32)
                row_stats(dve, s, X)
                row_rstd(dve, s, 1e-5, var_ready, root_ready)

                def normalise(t, u, earlier):
                    if earlier is not None:
                        dve.wait_ge(turned, earlier)
                    normalise_tile(dve, xn[:, u, :], X, t).then_inc(xn_ready, 1)

                for t in range(2):
                    normalise(t, t, None)
                with dve.Fori(1, NT // 2) as i:
                    for u in range(2):
                        normalise(2 * i + u, u, 2 * i + (u - 1))
                normalise(NT - 1, 0, NT - 2)
                with s.loop(1, SORT_STEPS // 2, 16) as i:
                    for u in range(2):
                        sort_step(2 * i + u, u, i * (16 * SORT_J))

            @block.scalar
            def _(act):
                def fill(k, u, reused):
                    if reused is not None:
                        act.wait_ge(scattered[u], reused)
                    at = bass.ts(k, SORT_J)
                    act.copy(rec[:, u, :, 0], dst_i[:, at]).then_inc(rec_filled, 1)
                    act.copy(rec[:, u, :, 1].bitcast(F32), local_f[:, at]).then_inc(rec_filled, 1)
                    act.copy(rec[:, u, :, 2].bitcast(F32), w_e[:, at]).then_inc(rec_filled, 1)

                act.wait_ge(zero_set, 1)
                act.copy(rec[:].bitcast(F32).rearrange("p a j f -> p (a j f)"), zero[:, 0:2 * SORT_J * REC].bitcast(F32)).then_inc(rec_filled, 1)
                act.wait_ge(rec_filled, 1)
                act.wait_ge(loaded, 96)
                act.wait_ge(local_done, 1)
                for u in range(2):
                    fill(u, u, None)
                row_root(act, var_ready, root_ready)

                def tile(t, u, reused):
                    act.wait_ge(turned, t + 1)
                    act.copy(xt[:, u, :, :].rearrange("p k n -> p (k n)"), psum[:, 2 + u, 0:D]).then_inc(turned_out, 1)
                    act.wait_ge(made, t + 1)
                    if reused is not None:
                        act.wait_ge(stored[u], reused)
                    act.copy(h_out[:, u, :], psum[:, 4 + u, 0:D]).then_inc(made_out, 1)

                for t in range(2):
                    tile(t, t, None)
                with act.Fori(1, NT // 2) as i:
                    for u in range(2):
                        tile(2 * i + u, u, i * 16)
                tile(NT - 1, 0, 16 * (NT // 2))
                with act.Fori(1, SORT_STEPS // 2) as i:
                    for u in range(2):
                        fill(2 * i + u, u, i * (16 * SORT_J))

            @block.tensor
            def _(pe):
                pe.wait_ge(consts_done, 1)
                pe.wait_ge(counted, 1)
                pe.matmul(psum[:, 0, 0:NB], before[:], count[:], start=True, stop=True).then_inc(totals, 1)
                pe.matmul(psum[:, 1, 0:NB], ones[:], count[:], start=True, stop=True).then_inc(totals, 1)
                pe.wait_ge(w0_loaded, 16)

                def tile(t, u, earlier):
                    if earlier is not None:
                        pe.wait_ge(turned_out, earlier)
                    pe.wait_ge(xn_ready, t + 1)
                    for k in range(KD):
                        ins = pe.transpose(psum[:, 2 + u, k * P:(k + 1) * P], xn[:, u, k * P:(k + 1) * P], ident[:])
                    ins.then_inc(turned, 1)
                    pe.wait_ge(turned_out, t + 1)
                    if earlier is not None:
                        pe.wait_ge(made_out, earlier)
                    for k in range(KD):
                        ins = pe.matmul(psum[:, 4 + u, 0:D], xt[:, u, k, :], w0[:, k, :], start=k == 0, stop=k == KD - 1)
                    ins.then_inc(made, 1)

                for t in range(2):
                    tile(t, t, None)
                with pe.Fori(1, NT // 2) as i:
                    for u in range(2):
                        tile(2 * i + u, u, 2 * i + (u - 1))
                tile(NT - 1, 0, NT - 2)

        graph = ctx.enter_context(ExitStack())
        A = sb("A", [P, NT, D], at=graph)
        AT = sb("AT", [P, KD, NT * P], at=graph)

        def aggregate(rows, name, prepare, load_more=None):
            with ExitStack() as scope, nc.Block() as block:
                here = lambda what, shape, dt=F32: sb(name + what, shape, dt, scope)
                rec = here("rec", [P, 2, GB, REC], I32)
                got = here("got", [P, 2, GB, D])
                route = here("route", [P, 2, GB, P])
                step, added = sem(name + "step"), sem(name + "added")
                step_open = sem(name + "gather_open")
                rec_in = [sem(name + "rec_in0"), sem(name + "rec_in1")]
                gathered = [[sem(name + f"gathered{u}{g}") for g in range(GB // GSEM)] for u in range(2)]
                routed, summed = sem(name + "routed"), sem(name + "summed")
                by_chunk = records.rearrange("(q c) f -> q c f", q=P)
                STEPS = CHUNKS // GB

                def load(eng, n, u):
                    eng.dma_start(rec[:, u, :, :], by_chunk[:, bass.ts(n, GB), :]).then_inc(rec_in[u], 16)

                @block.sync
                def _(sp):
                    load(sp, 0, 0)
                    load(sp, 1, 1)
                    if load_more:
                        load_more(sp)
                    with sp.Fori(1, STEPS // 2) as i:
                        for u in range(2):
                            for g in range(GB // GSEM):
                                sp.wait_ge(gathered[u][g], i * (16 * GSEM))
                            sp.wait_ge(routed, 2 * i + (u - 1))
                            load(sp, 2 * i + u, u)

                @block.gpsimd
                def _(pool):
                    def gather(i, u, again):
                        pool.wait_ge(rec_in[u], 16 * (i + 1))
                        for g in range(GB // GSEM):
                            if again:
                                pool.wait_ge(summed, i * (2 * GB) + (u * GB + (g + 1) * GSEM - 2 * GB))
                            pool.sem_inc(step_open, 1)
                            for j in range(g * GSEM, (g + 1) * GSEM):
                                pool.indirect_dma_start(
                                    got[:, u, j, :], None, rows,
                                    bass.IndirectOffsetOnAxis(ap=rec[:, u, j, 0:1].bitcast(U32), axis=0)
                                ).then_inc(gathered[u][g], 16)

                    for u in range(2):
                        gather(0, u, False)
                    with pool.Fori(1, STEPS // 2) as i:
                        for u in range(2):
                            gather(i, u, True)

                @block.vector
                def _(dve):
                    s = Steps(dve, step)
                    prepare(dve, s)
                    dve.engine_nop().then_inc(added, 1)

                    def step_of(i, u, again):
                        dve.wait_ge(rec_in[u], 16 * (i + 1))
                        if again:
                            dve.wait_ge(summed, i * (2 * GB) + (u * GB - GB))
                        for j in range(GB):
                            ins = dve.tensor_scalar(route[:, u, j, :], columns[:], rec[:, u, j, 1:2].bitcast(F32),
                                                    rec[:, u, j, 2:3].bitcast(F32), ALU.is_equal, ALU.mult)
                        ins.then_inc(routed, 1)
                        first = i * (2 * GB) + u * GB
                        _, tiles = nc.values_load_multi_w_load_instructions(
                            chunk_tile[0:1, bass.ds(first, GB)], engines=(mybir.EngineType.DVE,), min_val=0, max_val=NT - 1,
                            skip_runtime_bounds_check_because="the map is clamped to the tiles")
                        for j in range(GB):
                            to = AT[:, :, bass.ts(tiles[j], P)]
                            dve.wait_ge(summed, first + j + 1)
                            dve.wait_ge(added, first + j + 1)
                            dve.tensor_tensor(to, to, psum[:, j % 8, 0:D].rearrange("p (k n) -> p k n", k=KD),
                                              ALU.add).then_inc(added, 1)

                    for u in range(2):
                        step_of(0, u, False)
                    with dve.Fori(1, STEPS // 2) as i:
                        for u in range(2):
                            step_of(i, u, True)
                    dve.wait_ge(added, CHUNKS + 1)

                @block.tensor
                def _(pe):
                    def step_of(i, u, again):
                        pe.wait_ge(routed, 2 * i + (u + 1))
                        for j in range(GB):
                            if j % GSEM == 0:
                                pe.wait_ge(gathered[u][j // GSEM], (i + 1) * (16 * GSEM))
                            if again or u * GB + j >= 8:
                                pe.wait_ge(added, i * (2 * GB) + (u * GB + j + 1 - 7))
                            for k in range(KD):
                                ins = pe.matmul(psum[:, j % 8, k * P:(k + 1) * P], got[:, u, j, k * P:(k + 1) * P],
                                                route[:, u, j, :], start=True, stop=True)
                            ins.then_inc(summed, 1)

                    for u in range(2):
                        step_of(0, u, False)
                    with pe.Fori(1, STEPS // 2) as i:
                        for u in range(2):
                            step_of(i, u, True)

        def start_from_zero(dve, s):
            for k in range(KD):
                s(dve.memset(AT[:, k, :], 0.0))

        aggregate(table[0], "g0_", start_from_zero)

        class Turn:

            def __init__(self, name, scope):
                self.ring = sb(name + "ring", [P, 2, GROUP, D], at=scope)
                self.ready, self.turned, self.out = sem(name + "ring_ready"), sem(name + "turned"), sem(name + "turned_out")

            def normalise(self, dve, g, u):
                for m in range(GROUP):
                    ins = normalise_tile(dve, self.ring[:, u, m, :], X, g * GROUP + m)
                ins.then_inc(self.ready, 1)

            def turn(self, pe, g, u, again):
                pe.wait_ge(self.ready, g + 1)
                for m in range(GROUP):
                    if again or u:
                        pe.wait_ge(self.out, g * GROUP + (m + 1 - GROUP))
                    for k in range(KD):
                        ins = pe.transpose(psum[:, m, k * P:(k + 1) * P], self.ring[:, u, m, k * P:(k + 1) * P], ident[:])
                    ins.then_inc(self.turned, 1)

        with ExitStack() as scope, nc.Block() as block:
            here = lambda what, shape, dt=F32: sb("bn_" + what, shape, dt, scope)
            FMAX = 512
            cuts = list(range(0, N, FMAX)) + [N]
            node_stats = here("node_stats", [P, KD, len(cuts) - 1, 6])
            node_moments = here("node_moments", [P, KD, 2])
            gamma, beta, bias = here("gamma", [P, KD]), here("beta", [P, KD]), here("bias", [P, KD])
            gain, shift, root = here("gain", [P, KD]), here("shift", [P, KD]), here("root", [P, KD])
            active = here("active", [P, 2, KD, GROUP * P])
            xr = here("xr", [P, GROUP, D])
            wr = here("wr", [P, KD])
            turn = Turn("ln1_", scope)

            step, params = sem("bn_step"), sem("bn_params")
            var_ready, root_ready, coef_ready = sem("bn_var"), sem("bn_root"), sem("bn_coef")
            activated, back, taken = sem("bn_activated"), sem("bn_back"), sem("bn_taken")
            ring_used, xr_ready, scored, scored_out = sem("ln1_used"), sem("ln1_xr"), sem("ln1_scored"), sem("ln1_scored_out")

            @block.sync
            def _(sp):
                for to, of in ((gamma, g0_gamma), (beta, g0_beta), (bias, g0_bias), (wr, f0_wr)):
                    sp.dma_start(to[:], of).then_inc(params, 16)
                sp.dma_start(f0_br_row[:], f0_br.partition_broadcast(P)).then_inc(params, 16)
                sp.wait_ge(params, 80)

            @block.scalar
            def _(act):
                act.wait_ge(var_ready, 1)
                act.activation(root[:], root[:], ACT.Sqrt).then_inc(root_ready, 1)
                act.wait_ge(coef_ready, 1)

                def activate(g, u, again):
                    if again:
                        act.wait_ge(back, g * GROUP - GROUP)
                    for k in range(KD):
                        act.activation(active[:, u, k, :], AT[:, k, bass.ts(g, GROUP * P)], ACT.Relu,
                                       bias=shift[:, k:k + 1], scale=gain[:, k:k + 1]).then_inc(activated, 1)
                over_groups(act, activate)
                row_root(act, var_ready, root_ready, 2)

                def turn_out(g, u, again):
                    for m in range(GROUP):
                        act.wait_ge(turn.turned, g * GROUP + (m + 1))
                        if again or u:
                            act.wait_ge(scored, g * GROUP + (m + 1 - GROUP))
                            act.wait_ge(scored_out, g * GROUP + (m + 1 - GROUP))
                        act.copy(xr[:, m, :], psum[:, m, 0:D]).then_inc(turn.out, 1)
                over_groups(act, turn_out)

            @block.gpsimd
            def _(pool):
                def to_at(g, u, again):
                    for m in range(GROUP):
                        pool.wait_ge(turn.out, g * GROUP + (m + 1))
                        pool.tensor_copy(AT[:, :, bass.ts(g * GROUP + m, P)],
                                         xr[:, m, :].rearrange("p (k n) -> p k n", k=KD)).then_inc(scored_out, 1)
                pool.wait_ge(back, NT)
                over_groups(pool, to_at)

            @block.tensor
            def _(pe):
                def turn_back(g, u, again):
                    pe.wait_ge(activated, KD * (g + 1))
                    for m in range(GROUP):
                        if again or u:
                            pe.wait_ge(taken, g * GROUP + (m + 1 - GROUP))
                        for k in range(KD):
                            ins = pe.transpose(psum[:, m, k * P:(k + 1) * P], active[:, u, k, m * P:(m + 1) * P], ident[:])
                        ins.then_inc(back, 1)
                over_groups(pe, turn_back)
                pe.wait_ge(taken, NT)
                pe.wait_ge(params, 80)

                def turn_and_score(g, u, again):
                    turn.turn(pe, g, u, again)
                    for m in range(GROUP):
                        pe.wait_ge(turn.out, g * GROUP + (m + 1))
                        for k in range(KD):
                            ins = pe.matmul(psum[:, 7, bass.ds(g * GROUP + m, 1)], xr[:, m, k * P:(k + 1) * P], wr[:, k:k + 1],
                                            start=k == 0, stop=k == KD - 1)
                        ins.then_inc(scored, 1)
                over_groups(pe, turn_and_score)

            @block.vector
            def _(dve):
                s = Steps(dve, step)
                for k in range(KD):
                    for i, (a, b) in enumerate(zip(cuts, cuts[1:])):
                        ins = dve.bn_stats(node_stats[:, k, i, :], AT[:, k, a:b])
                s(ins)
                for k in range(KD):
                    ins = dve.bn_aggr(node_moments[:, k, :], node_stats[:, k, :, :].rearrange("p i s -> p (i s)"))
                s(ins)
                dve.wait_ge(params, 80)
                dve.tensor_scalar(root[:], node_moments[:, :, 1], 1e-5, None, ALU.add).then_inc(var_ready, 1)
                s(dve.tensor_tensor(shift[:], node_moments[:, :, 0], bias[:], ALU.add))
                s(dve.tensor_tensor(shift[:], bias[:], shift[:], ALU.subtract))
                dve.wait_ge(root_ready, 1)
                s(dve.reciprocal(gain[:], root[:]))
                s(dve.tensor_tensor(gain[:], gain[:], gamma[:], ALU.mult))
                s(dve.tensor_tensor(shift[:], shift[:], gain[:], ALU.mult))
                dve.tensor_tensor(shift[:], shift[:], beta[:], ALU.add).then_inc(coef_ready, 1)

                def residual(g, u, again):
                    for m in range(GROUP):
                        dve.wait_ge(back, g * GROUP + (m + 1))
                        own = row(X, g * GROUP + m)
                        dve.tensor_tensor(own, own, psum[:, m, 0:D], ALU.add).then_inc(taken, 1)
                over_groups(dve, residual)
                dve.wait_ge(taken, NT)
                row_stats(dve, s, X)
                row_rstd(dve, s, 1e-5, var_ready, root_ready, 2)

                def normalise(g, u, again):
                    if again:
                        dve.wait_ge(turn.turned, g * GROUP - GROUP)
                        dve.wait_ge(ring_used, g - 1)
                    turn.normalise(dve, g, u)
                    dve.wait_ge(turn.ready, g + 1)
                    dve.tensor_tensor(group_rows(X, g), group_rows(X, g), turn.ring[:, u, :, :], ALU.add).then_inc(ring_used, 1)
                over_groups(dve, normalise)
                dve.wait_ge(scored, NT)
                s(dve.tensor_scalar(wgt[:], psum[:, 7, 0:NT], f0_br_row[:, 0:1], None, ALU.add))

        class TopK:
            STEPS = 36

            def __init__(self, scope):
                here = lambda what, shape, dt=F32: sb("topk_" + what, shape, dt, scope)
                self.valid, self.sign, self.key = here("valid", [P, NT]), here("sign", [P, NT], I32), here("key", [P, NT], I32)
                self.half_i, self.hi, self.lo = here("half_i", [P, NT], I32), here("hi", [P, NT]), here("lo", [P, NT])
                self.junk, self.bits = here("junk", [P, NT]), here("bits", [P, 16])
                self.T_hi, self.T_lo = here("T_hi", [P, 1]), here("T_lo", [P, 1])
                self.cand, self.hits, self.bit, self.want = (here(w, [P, 1]) for w in ("cand", "hits", "bit", "want"))
                self.above, self.equal = here("above", [P, NT]), here("equal", [P, NT])
                self.rank, self.colsum = here("rank", [P, NT]), here("colsum", [P, NT])
                self.counted, self.counted_all, self.done = sem("topk_counted"), sem("topk_all"), sem("topk_done")

            def product(self, pe, n):
                if n < 34:
                    pe.wait_ge(self.counted, n + 1)
                    pe.matmul(psum[:, 0, 0:1], ones[:], self.hits[:], start=True, stop=True).then_inc(self.counted_all, 1)
                else:
                    by, column = ((before, NT) if n == 34 else (ones, 2 * NT))
                    pe.matmul(psum[:, 0, column:column + NT], by[:], self.equal[:], start=True,
                              stop=True).then_inc(self.counted_all, 1)

            def search(self, dve, s):
                valid, sign, key, half_i, hi, lo = self.valid, self.sign, self.key, self.half_i, self.hi, self.lo
                junk, bits, cand, hits, bit, want = self.junk, self.bits, self.cand, self.hits, self.bit, self.want
                above, equal, rank, colsum = self.above, self.equal, self.rank, self.colsum
                counted, counted_all = self.counted, self.counted_all
                s(dve.memset(valid[:], 1.0))
                s(dve.tensor_copy(valid[:, NT - 1:NT], ones_last[:, 0:1]))
                for b in range(16):
                    ins = dve.memset(bits[:, b:b + 1], float(1 << (15 - b)))
                s(ins)
                w_i = wgt[:].bitcast(I32)
                s(dve.tensor_scalar(sign[:], w_i, 31, -(1 << 31), ALU.arith_shift_right, ALU.bitwise_or))
                s(dve.tensor_tensor(key[:], w_i, sign[:], ALU.bitwise_xor))
                s(dve.tensor_scalar(half_i[:], key[:], 16, 0xFFFF, ALU.logical_shift_right, ALU.bitwise_and))
                s(dve.tensor_copy(hi[:], half_i[:]))
                s(dve.tensor_scalar(half_i[:], key[:], 0xFFFF, None, ALU.bitwise_and))
                s(dve.tensor_copy(lo[:], half_i[:]))
                s(dve.scalar_tensor_tensor(hi[:], hi[:], 1.0, valid[:], ALU.add, ALU.mult))
                s(dve.tensor_scalar(hi[:], hi[:], -1.0, None, ALU.add))
                s(dve.memset(want[:], float(TOPK)))

                def find(keys, T, at):
                    s(dve.memset(T[:], 0.0))
                    with s.loop(0, 16, 3) as b:
                        s(dve.tensor_tensor(cand[:], T[:], bits[:, bass.ds(b, 1)], ALU.add))
                        dve.tensor_scalar(junk[:], keys[:], cand[:, 0:1], 0.0, ALU.is_ge, ALU.add,
                                          accum_out=hits[:]).then_inc(counted, 1)
                        dve.wait_ge(counted_all, b + (at + 1))
                        s(dve.tensor_tensor(bit[:], psum[:, 0, 0:1], want[:], ALU.is_ge))
                        s(dve.scalar_tensor_tensor(T[:], bit[:], bits[:, bass.ds(b, 1)], T[:], ALU.mult, ALU.add))

                find(hi, self.T_hi, 0)
                dve.tensor_scalar(above[:], hi[:], self.T_hi[:, 0:1], 0.0, ALU.is_gt, ALU.add,
                                  accum_out=hits[:]).then_inc(counted, 1)
                dve.wait_ge(counted_all, 17)
                s(dve.tensor_tensor(want[:], want[:], psum[:, 0, 0:1], ALU.subtract))
                s(dve.tensor_scalar(equal[:], hi[:], self.T_hi[:, 0:1], None, ALU.is_equal))
                s(dve.scalar_tensor_tensor(lo[:], lo[:], 1.0, equal[:], ALU.add, ALU.mult))
                s(dve.tensor_scalar(lo[:], lo[:], -1.0, None, ALU.add))
                find(lo, self.T_lo, 17)
                s(dve.tensor_scalar(equal[:], lo[:], self.T_lo[:, 0:1], None, ALU.is_equal))
                dve.tensor_scalar(junk[:], lo[:], self.T_lo[:, 0:1], 0.0, ALU.is_gt, ALU.add,
                                  accum_out=hits[:]).then_inc(counted, 1)
                dve.wait_ge(counted, 34)
                s(dve.tensor_tensor(above[:], above[:], junk[:], ALU.add))
                dve.wait_ge(counted_all, self.STEPS)
                s(dve.tensor_tensor(want[:], want[:], psum[:, 0, 0:1], ALU.subtract))
                s(dve.tensor_copy(colsum[:], psum[:, 0, 2 * NT:3 * NT]))
                s(dve.tensor_tensor_scan(rank[:], ones[:, 0:NT], colsum[:], 0.0, ALU.mult, ALU.add))
                s(dve.tensor_tensor(rank[:], rank[:], colsum[:], ALU.subtract))
                s(dve.tensor_tensor(rank[:], rank[:], psum[:, 0, NT:2 * NT], ALU.add))
                s(dve.scalar_tensor_tensor(rank[:], rank[:], want[:, 0:1], equal[:], ALU.is_lt, ALU.mult))
                s(dve.tensor_tensor(above[:], above[:], rank[:], ALU.add))
                s(dve.tensor_tensor(mw[:], wgt[:], above[:], ALU.mult))

        def mlp(name, w1_d, b1_d, w2_d, b2_d, width, function, leave, search, finish):
            HB = width // P
            with ExitStack() as scope, nc.Block() as block:
                here = lambda what, shape, dt=F32: sb(name + what, shape, dt, scope)
                w1 = here("w1", [P, KD, width])
                w2 = here("w2", [P, HB, D])
                b1 = here("b1", [P, HB])
                b2 = here("b2", [1, D])
                ht = here("ht", [P, HB, GROUP * P])
                topk = TopK(scope) if search else None
                params, step = sem(name + "params"), sem(name + "step")
                hid, hid_out = sem(name + "hid"), sem(name + "hid_out")
                made, made_out = sem(name + "made"), sem(name + "made_out")
                var_ready, root_ready = sem(name + "var"), sem(name + "root")
                HP = 2 * HB
                FIRST = -(-TopK.STEPS // (HP // 2 + GROUP)) if search else 1

                @block.sync
                def _(sp):
                    sp.dma_start(w1[:], w1_d.rearrange("(k p) n -> p k n", p=P)).then_inc(params, 16)
                    sp.dma_start(w2[:], w2_d.rearrange("(k p) n -> p k n", p=P)).then_inc(params, 16)
                    sp.dma_start(b1[:], b1_d).then_inc(params, 16)
                    sp.dma_start(b2[:], b2_d.rearrange("(a n) -> a n", a=1)).then_inc(params, 16)
                    sp.wait_ge(params, 64)

                @block.tensor
                def _(pe):
                    pe.wait_ge(params, 64)
                    asked = iter(range(TopK.STEPS if search else 0))

                    def search_product():
                        n = next(asked, None)
                        if n is not None:
                            topk.product(pe, n)

                    def group(g, again, searching):
                        for n in range(HP):
                            b, h = n // 2, n % 2
                            if again or n >= 4:
                                pe.wait_ge(hid_out, g * HP + (n - 3))
                            for k in range(KD):
                                ins = pe.matmul(psum[:, 1 + n % 4, 0:HALF], w1[:, k, b * P:(b + 1) * P],
                                                AT[:, k, bass.ds(g * (GROUP * P) + h * HALF, HALF)], start=k == 0, stop=k == KD - 1)
                            ins.then_inc(hid, 1)
                            if searching and n % 2:
                                search_product()
                        pe.wait_ge(hid_out, (g + 1) * HP)
                        for m in range(GROUP):
                            if again or m >= 3:
                                pe.wait_ge(made_out, g * GROUP + max(m - 2, 0))
                            for b in range(HB):
                                pe.matmul(psum[:, 5 + m % 3, 0:D], ht[:, b, m * P:(m + 1) * P], w2[:, b, :],
                                          start=b == 0, stop=False)
                            pe.matmul(psum[:, 5 + m % 3, 0:D], ones[0:1, :], b2[:], start=False, stop=True).then_inc(made, 1)
                            if searching:
                                search_product()

                    for g in range(FIRST):
                        group(g, g > 0, search)
                    assert next(asked, None) is None
                    with pe.Fori(FIRST, GROUPS) as g:
                        group(g, True, False)

                @block.scalar
                def _(act):
                    act.wait_ge(params, 64)

                    def group(g, again):
                        for n in range(HP):
                            b, h = n // 2, n % 2
                            act.wait_ge(hid, g * HP + (n + 1))
                            if again and n == 0:
                                act.wait_ge(made, g * GROUP)
                            act.activation(ht[:, b, h * HALF:(h + 1) * HALF], psum[:, 1 + n % 4, 0:HALF], function,
                                           bias=b1[:, b:b + 1]).then_inc(hid_out, 1)
                        for m in range(GROUP):
                            act.wait_ge(made, g * GROUP + (m + 1))
                            act.activation(row(A, g * GROUP + m), psum[:, 5 + m % 3, 0:D], leave).then_inc(made_out, 1)

                    group(0, False)
                    with act.Fori(1, GROUPS) as g:
                        group(g, True)
                    for n in range(finish.roots):
                        row_root(act, var_ready, root_ready, n + 1)

                @block.vector
                def _(dve):
                    s = Steps(dve, step)
                    if search:
                        topk.search(dve, s)
                    finish(dve, s, made_out, var_ready, root_ready)

        def token_finish(dve, s, made_out, var_ready, root_ready):
            with s.loop(0, GROUPS, 1) as g:
                for m in range(GROUP):
                    t = g * GROUP + m
                    dve.wait_ge(made_out, t + 1)
                    ins = dve.scalar_tensor_tensor(row(X, t), row(A, t), mw[:, bass.ds(t, 1)], row(X, t), ALU.mult, ALU.add)
                s(ins)
            row_stats(dve, s, X)

        token_finish.roots = 0
        mlp("f0m_", f0_w1, f0_b1, f0_w2, f0_b2, f0_w1.shape[1], ACT.Gelu_apprx_tanh, ACT.Copy, True, token_finish)

        with ExitStack() as scope, nc.Block() as block:
            eps1 = sb("eps1", [P, 1], at=scope)
            step, eps_in, eps_ready = sem("t1_step"), sem("t1_eps_in"), sem("t1_eps_ready")
            var_ready, root_ready = sem("t1_var"), sem("t1_root")
            stored = [sem("t1_stored0"), sem("t1_stored1")]
            turn = Turn("t1_", scope)
            table_rows = table[1].rearrange("(t p) d -> p t d", p=P)

            @block.sync
            def _(sp):
                sp.dma_start(eps1[:], g1_eps.partition_broadcast(P)).then_inc(eps_in, 16)

                def store(g, u, again):
                    sp.wait_ge(turn.ready, g + 1)
                    sp.dma_start(table_rows[:, bass.ts(g, GROUP), :], turn.ring[:, u, :, :]).then_inc(stored[u], 16)
                over_groups(sp, store)
                sp.wait_ge(stored[0], 16 * (GROUPS // 2 + 1))
                sp.wait_ge(stored[1], 16 * (GROUPS // 2))
                sp.wait_ge(eps_in, 16)

            @block.scalar
            def _(act):
                row_root(act, var_ready, root_ready)
                act.wait_ge(eps_ready, 1)

                def turn_out(g, u, again):
                    for m in range(GROUP):
                        act.wait_ge(turn.turned, g * GROUP + (m + 1))
                        act.activation(AT[:, :, bass.ts(g * GROUP + m, P)], psum[:, m, 0:D].rearrange("p (k n) -> p k n", k=KD),
                                       ACT.Copy, scale=eps1[:, 0:1]).then_inc(turn.out, 1)
                over_groups(act, turn_out)

            @block.tensor
            def _(pe):
                over_groups(pe, lambda g, u, again: turn.turn(pe, g, u, again))

            @block.vector
            def _(dve):
                s = Steps(dve, step)
                dve.wait_ge(eps_in, 16)
                dve.tensor_scalar(eps1[:], eps1[:], 1.0, None, ALU.add).then_inc(eps_ready, 1)
                row_rstd(dve, s, 1e-5, var_ready, root_ready)

                def normalise(g, u, again):
                    if again:
                        dve.wait_ge(turn.turned, g * GROUP - GROUP)
                        dve.wait_ge(stored[u], (g - u) * 8)
                    turn.normalise(dve, g, u)
                over_groups(dve, normalise)

        rows_in = sem("rows_in")

        def add_offset(dve, s):
            nc.vector.wait_ge(rows_in, 32)
            with s.loop(0, GROUPS, 1) as g:
                s(dve.tensor_tensor(group_rows(X, g), group_rows(X, g), offset[:].unsqueeze(1).to_broadcast([P, GROUP, D]), ALU.add))

        def load_rows(sp):
            sp.dma_start(offset[:], g1_offset.partition_broadcast(P)).then_inc(rows_in, 16)
            sp.dma_start(scale1[:], g1_scale.partition_broadcast(P)).then_inc(rows_in, 16)

        aggregate(table[1], "g1_", add_offset, load_rows)

        def graph_finish(dve, s, made_out, var_ready, root_ready):
            row_stats(dve, s, A, lambda t: dve.wait_ge(made_out, t + 1))
            row_rstd(dve, s, 1e-10, var_ready, root_ready, 1)
            with s.loop(0, GROUPS, 3) as g:
                for m in range(GROUP):
                    ins = normalise_tile(dve, row(A, g * GROUP + m), A, g * GROUP + m)
                s(ins)
                s(dve.tensor_tensor(group_rows(A, g), group_rows(A, g), scale1[:].unsqueeze(1).to_broadcast([P, GROUP, D]), ALU.mult))
                s(dve.tensor_tensor(group_rows(X, g), group_rows(X, g), group_rows(A, g), ALU.add))
            row_stats(dve, s, X)

        graph_finish.roots = 1
        mlp("m1m_", g1_w1, g1_b1, g1_w2, g1_b2, D, ACT.Relu, ACT.Relu, False, graph_finish)

        with ExitStack() as scope, nc.Block() as block:
            here = lambda what, shape, dt=F32: sb("r_" + what, shape, dt, scope)
            C = 2 * NT
            wr, br = here("wr", [P, KD, NE]), here("br", [P, NE])
            xr = here("xr", [P, GROUP, D])
            root2 = here("root2", [P, NT])
            logit, work, work2 = here("logit", [P, NT, NE]), here("work", [P, NT, NE]), here("work2", [P, NT, NE])
            hot = here("hot", [P, NT, 2, NE])
            top = here("top", [P, NT, 2])
            pick = here("pick", [P, NT])
            expo, total = here("expo", [P, NT, NE]), here("total", [P, NT])
            prob = here("prob", [P, NT, 2])
            sums = here("sums", [P, NE, C + 1])
            keep = here("keep", [P, NE, C + 1])
            upto = here("upto", [P, NE, C + 1])
            ntile_i, ntile = here("ntile_i", [P, NE], I32), here("ntile", [P, NE])
            tiles_upto, first = here("tiles_upto", [P, NE]), here("first", [P, NE])
            at = here("at", [P, C, NE])
            slot_f = here("slot_f", [P, C])
            past, exp_f, exp_i = here("past", [P, NE]), here("exp_f", [P, 1]), here("exp_i", [P, 1], I32)
            turn = Turn("r_", scope)

            step, params = sem("r_step"), sem("r_params")
            var_ready, root_ready = sem("r_var"), sem("r_root")
            scored, ring_used = sem("r_scored"), sem("r_ring_used")
            exp_ask, exp_done = sem("r_exp_ask"), sem("r_exp_done")
            hot_ready, ranked = sem("r_hot"), sem("r_ranked")
            map_ready, map_out, map_in = sem("r_map_ready"), sem("r_map_out"), sem("r_map_in")
            slots_ready, placed = sem("r_slots_ready"), sem("r_placed")

            @block.sync
            def _(sp):
                sp.dma_start(wr[:], m_wr.rearrange("(k p) n -> p k n", p=P)).then_inc(params, 16)
                sp.dma_start(br[:], m_br.partition_broadcast(P)).then_inc(params, 16)
                sp.wait_ge(params, 32)
                sp.wait_ge(map_ready, 1)
                sp.dma_start(expert_row.rearrange("(p a) -> p a", a=1), exp_i[:],
                             allow_slow_non_contiguous=True).then_inc(map_out, 16)
                sp.wait_ge(map_out, 16)
                sp.dma_start(expert[:], expert_row.rearrange("(a p) -> a p", a=1)).then_inc(map_in, 16)
                sp.wait_ge(map_in, 16)

            @block.scalar
            def _(act):
                row_root(act, var_ready, root_ready, 1)
                act.wait_ge(var_ready, 2)
                act.activation(root2[:], root2[:], ACT.Sqrt).then_inc(root_ready, 1)

                def turn_out(g, u, again):
                    for m in range(GROUP):
                        act.wait_ge(turn.turned, g * GROUP + (m + 1))
                        if again or u:
                            act.wait_ge(scored, g * GROUP + (m + 1 - GROUP))
                        act.copy(xr[:, m, :], psum[:, m, 0:D]).then_inc(turn.out, 1)
                over_groups(act, turn_out)
                act.wait_ge(exp_ask, 1)
                act.activation(expo[:].rearrange("p t e -> p (t e)"), work[:].rearrange("p t e -> p (t e)"),
                               ACT.Exp).then_inc(exp_done, 1)
                act.activation(prob[:].rearrange("p t e -> p (t e)"), top[:].rearrange("p t e -> p (t e)"),
                               ACT.Exp).then_inc(exp_done, 1)

            @block.tensor
            def _(pe):
                pe.wait_ge(params, 32)

                def turn_and_score(g, u, again):
                    turn.turn(pe, g, u, again)
                    for m in range(GROUP):
                        pe.wait_ge(turn.out, g * GROUP + (m + 1))
                        for k in range(KD):
                            ins = pe.matmul(psum[:, 7, bass.ds((g * GROUP + m) * NE, NE)], xr[:, m, k * P:(k + 1) * P],
                                            wr[:, k, :], start=k == 0, stop=k == KD - 1)
                        ins.then_inc(scored, 1)
                over_groups(pe, turn_and_score)
                pe.wait_ge(hot_ready, 1)
                flat = hot[:].rearrange("p t k e -> p (t k e)")
                for h in range(2):
                    part_of = flat[:, h * NT * NE:(h + 1) * NT * NE]
                    pe.matmul(psum[:, 3 + h, 0:NT * NE], before[:], part_of, start=True, stop=True).then_inc(ranked, 1)
                    pe.matmul(psum[:, 5 + h, 0:NT * NE], ones[:], part_of, start=True, stop=True).then_inc(ranked, 1)

            @block.gpsimd
            def _(pool):
                def keep_rows(g, u, again):
                    pool.wait_ge(turn.ready, g + 1)
                    pool.tensor_copy(group_rows(A, g), turn.ring[:, u, :, :]).then_inc(ring_used, 1)
                over_groups(pool, keep_rows)
                pool.wait_ge(ring_used, GROUPS)
                pool.wait_ge(slots_ready, 1)
                for t in range(NT):
                    for k in range(2):
                        c = 2 * t + k
                        pool.indirect_dma_start(
                            slots_in, bass.IndirectOffsetOnAxis(ap=slot[:, c:c + 1].bitcast(U32), axis=0),
                            A[:, t, :], None).then_inc(placed, 16)
                pool.wait_ge(placed, 16 * C)

            @block.vector
            def _(dve):
                s = Steps(dve, step)
                row_rstd(dve, s, 1e-5, var_ready, root_ready, 1)
                s(dve.tensor_tensor(root2[:], moments[:, :, 1], rstd[:], ALU.mult))
                s(dve.tensor_tensor(root2[:], root2[:], rstd[:], ALU.mult))
                dve.tensor_scalar(root2[:], root2[:], 1e-5, None, ALU.add).then_inc(var_ready, 1)
                dve.wait_ge(root_ready, 2)
                s(dve.reciprocal(pick[:], root2[:]))
                s(dve.tensor_tensor(rstd[:], rstd[:], pick[:], ALU.mult))

                def normalise(g, u, again):
                    if again:
                        dve.wait_ge(turn.turned, g * GROUP - GROUP)
                        dve.wait_ge(ring_used, g - 1)
                    turn.normalise(dve, g, u)
                over_groups(dve, normalise)
                s(dve.memset(keep[:], 1.0))
                s(dve.memset(keep[:, :, 0:1], 0.0))
                s(dve.memset(sums[:, :, 0:1], 0.0))
                dve.wait_ge(params, 32)
                dve.wait_ge(scored, NT)
                numbers = columns[:, 0:NE].unsqueeze(1).to_broadcast([P, NT, NE])
                wide = lambda a: a.unsqueeze(2).to_broadcast([P, NT, NE])
                s(dve.tensor_tensor(logit[:], psum[:, 7, 0:NT * NE].rearrange("p (t e) -> p t e", e=NE), wide(root2[:]), ALU.mult))
                s(dve.tensor_tensor(logit[:], logit[:], br[:].unsqueeze(1).to_broadcast([P, NT, NE]), ALU.add))

                def best(k, scores):
                    s(dve.tensor_reduce(top[:, :, k], scores[:], AX.X, ALU.max))
                    s(dve.tensor_tensor(work2[:], scores[:], wide(top[:, :, k]), ALU.is_equal))
                    s(dve.scalar_tensor_tensor(work2[:], work2[:], -float(NE), numbers, ALU.mult, ALU.add))
                    s(dve.tensor_reduce(pick[:], work2[:], AX.X, ALU.min))
                    s(dve.tensor_scalar(pick[:], pick[:], float(NE), None, ALU.add))
                    s(dve.tensor_tensor(hot[:, :, k, :], numbers, wide(pick[:]), ALU.is_equal))

                best(0, logit)
                s(dve.scalar_tensor_tensor(work[:], hot[:, :, 0, :], -1e30, logit[:], ALU.mult, ALU.add))
                best(1, work)
                dve.engine_nop().then_inc(hot_ready, 1)
                s(dve.tensor_tensor(work[:], logit[:], wide(top[:, :, 0]), ALU.subtract))
                s(dve.tensor_copy(pick[:], top[:, :, 0]))
                dve.tensor_tensor(top[:], top[:], pick[:].unsqueeze(2).to_broadcast([P, NT, 2]), ALU.subtract).then_inc(exp_ask, 1)
                dve.wait_ge(ranked, 4)
                for h in range(2):
                    s(dve.tensor_copy(sums[:, :, 1 + h * NT:1 + (h + 1) * NT],
                                      psum[:, 5 + h, 0:NT * NE].rearrange("p (c e) -> p e c", e=NE)))
                s(dve.tensor_tensor_scan(upto[:].rearrange("p e c -> p (e c)"), keep[:].rearrange("p e c -> p (e c)"),
                                         sums[:].rearrange("p e c -> p (e c)"), 0.0, ALU.mult, ALU.add))
                s(dve.tensor_scalar(ntile_i[:], upto[:, :, C], float(MT - 1), None, ALU.add))
                s(dve.tensor_scalar(ntile_i[:], ntile_i[:], 8, None, ALU.logical_shift_right))
                s(dve.tensor_copy(ntile[:], ntile_i[:]))
                s(dve.tensor_tensor_scan(tiles_upto[:], ones[:, 0:NE], ntile[:], 0.0, ALU.mult, ALU.add))
                s(dve.tensor_tensor(first[:], tiles_upto[:], ntile[:], ALU.subtract))
                s(dve.tensor_scalar(first[:], first[:], float(MT), None, ALU.mult))
                for h in range(2):
                    s(dve.tensor_tensor(at[:, h * NT:(h + 1) * NT, :], psum[:, 3 + h, 0:NT * NE].rearrange("p (c e) -> p c e", e=NE),
                                        upto[:, :, h * NT:(h + 1) * NT].rearrange("p e c -> p c e"), ALU.add))
                s(dve.tensor_tensor(at[:], at[:], first[:].unsqueeze(1).to_broadcast([P, C, NE]), ALU.add))
                s(dve.tensor_tensor(at[:], at[:], hot[:].rearrange("p t k e -> p (t k) e"), ALU.mult))
                s(dve.tensor_reduce(slot_f[:], at[:], AX.X, ALU.add))
                dve.tensor_copy(slot[:], slot_f[:]).then_inc(slots_ready, 1)
                s(dve.tensor_scalar(past[:], tiles_upto[:], part[:, 0:1], None, ALU.is_le))
                s(dve.tensor_reduce(exp_f[:], past[:], AX.X, ALU.add))
                dve.tensor_scalar(exp_i[:], exp_f[:], float(NE - 1), None, ALU.min).then_inc(map_ready, 1)
                dve.wait_ge(exp_done, 2)
                s(dve.tensor_reduce(total[:], expo[:], AX.X, ALU.add))
                s(dve.reciprocal(total[:], total[:]))
                s(dve.tensor_tensor(prob[:], prob[:], total[:].unsqueeze(2).to_broadcast([P, NT, 2]), ALU.mult))
                s(dve.tensor_reduce(total[:], prob[:], AX.X, ALU.add))
                s(dve.reciprocal(total[:], total[:]))
                s(dve.tensor_tensor(share[:], prob[:], total[:].unsqueeze(2).to_broadcast([P, NT, 2]), ALU.mult))
        graph.close()

        HB = HM // P
        with ExitStack() as scope, nc.Block() as block:
            here = lambda what, shape, dt=F32: sb("e_" + what, shape, dt, scope)
            w1, w2 = here("w1", [P, 2, KD, HM]), here("w2", [P, 2, HB, D])
            gain, shift, b1 = here("gain", [P, 2, KD]), here("shift", [P, 2, KD]), here("b1", [P, 2, HB])
            b2 = here("b2", [1, 2, D])
            rows = here("rows", [P, 2, 2, D])
            xt = here("xt", [P, 2, KD, MT])
            ht = here("ht", [P, 2, HB, MT])
            y = here("y", [P, 2, 2, D])
            rows_in = [sem("e_rows0"), sem("e_rows1")]
            first_in = [sem("e_first0"), sem("e_first1")]
            second_in = [sem("e_second0"), sem("e_second1")]
            turned, turned_out = sem("e_turned"), sem("e_turned_out")
            hid, hid_out = sem("e_hid"), sem("e_hid_out")
            made, made_out = sem("e_made"), sem("e_made_out")
            stored = [sem("e_stored0"), sem("e_stored1")]
            PAIRS = MTILES // 2

            @block.sync
            def _(sp):
                def load(n, u, i):
                    e = sp.value_load(expert[0:1, bass.ds(n, 1)], min_val=0, max_val=NE - 1)
                    one = bass.ds(e, 1)
                    if i is not None:
                        sp.wait_ge(turned, 2 * i + (u - 1))
                        sp.wait_ge(turned_out, 4 * i + (2 * u - 2))
                    sp.dma_start(rows[:, u, :, :], slots_in[bass.ts(n, MT), :].rearrange("(s p) d -> p s d", p=P)).then_inc(rows_in[u], 16)
                    sp.dma_start(gain[:, u, :], m_g[one, :, :].rearrange("a p k -> p (a k)")).then_inc(rows_in[u], 16)
                    sp.dma_start(shift[:, u, :], m_b[one, :, :].rearrange("a p k -> p (a k)")).then_inc(rows_in[u], 16)
                    if i is not None:
                        sp.wait_ge(hid_out, i * (2 * HB) + (u * HB - HB))
                    sp.dma_start(w1[:, u, :, :], m_w1[one, :, :, :].rearrange("a p k n -> p (a k) n")).then_inc(first_in[u], 16)
                    sp.dma_start(b1[:, u, :], m_b1[one, :, :].rearrange("a p k -> p (a k)")).then_inc(first_in[u], 16)
                    if i is not None:
                        sp.wait_ge(made, 4 * i + (2 * u - 2))
                    sp.dma_start(w2[:, u, :, :], m_w2[one, :, :, :].rearrange("a p k n -> p (a k) n")).then_inc(second_in[u], 16)
                    sp.dma_start(b2[:, u, :], m_b2[one, :]).then_inc(second_in[u], 16)
                load(0, 0, None)
                load(1, 1, None)
                with sp.Fori(1, PAIRS) as i:
                    for u in range(2):
                        load(2 * i + u, u, i)

            @block.tensor
            def _(pe):
                def turn(i, u, again):
                    pe.wait_ge(rows_in[u], (i + 1) * 48)
                    if again:
                        pe.wait_ge(turned_out, 4 * i + 2 * u)
                    for k in range(KD):
                        for m in range(2):
                            ins = pe.transpose(psum[:, 0, k * MT + m * P:k * MT + (m + 1) * P],
                                               rows[:, u, m, k * P:(k + 1) * P], ident[:])
                    ins.then_inc(turned, 1)

                def hidden(i, u, again):
                    pe.wait_ge(turned_out, 4 * i + 2 * (u + 1))
                    pe.wait_ge(first_in[u], (i + 1) * 32)
                    for b in range(HB):
                        if again or u * HB + b >= 4:
                            pe.wait_ge(hid_out, i * (2 * HB) + (u * HB + b - 3))
                        for k in range(KD):
                            ins = pe.matmul(psum[:, 1 + b % 4, 0:MT], w1[:, u, k, b * P:(b + 1) * P], xt[:, u, k, :],
                                            start=k == 0, stop=k == KD - 1)
                        ins.then_inc(hid, 1)

                def product(i, u, again):
                    pe.wait_ge(hid_out, i * (2 * HB) + (u + 1) * HB)
                    pe.wait_ge(second_in[u], (i + 1) * 32)
                    for m in range(2):
                        if again:
                            pe.wait_ge(made_out, 4 * i + (2 * u + m - 1))
                        for b in range(HB):
                            pe.matmul(psum[:, 5 + m, 0:D], ht[:, u, b, m * P:(m + 1) * P], w2[:, u, b, :],
                                      start=b == 0, stop=False)
                        pe.matmul(psum[:, 5 + m, 0:D], ones[0:1, :], b2[:, u, :], start=False, stop=True).then_inc(made, 1)

                turn(0, 0, False)
                hidden(0, 0, False)
                turn(0, 1, True)
                product(0, 0, False)
                with pe.Fori(0, PAIRS - 1) as i:
                    hidden(i, 1, True)
                    turn(i + 1, 0, True)
                    product(i, 1, True)
                    hidden(i + 1, 0, True)
                    turn(i + 1, 1, True)
                    product(i + 1, 0, True)
                hidden(PAIRS - 1, 1, True)
                product(PAIRS - 1, 1, True)

            @block.vector
            def _(dve):
                def tile(i, u, again):
                    dve.wait_ge(turned, 2 * i + (u + 1))
                    dve.wait_ge(rows_in[u], (i + 1) * 48)
                    if again:
                        dve.wait_ge(hid, i * (2 * HB) + (u * HB - HB))
                    for k in range(KD):
                        dve.tensor_scalar(xt[:, u, k, :], psum[:, 0, k * MT:(k + 1) * MT], gain[:, u, k:k + 1],
                                          shift[:, u, k:k + 1], ALU.mult, ALU.add).then_inc(turned_out, 1)

                def result(i, u, again):
                    if again:
                        dve.wait_ge(stored[u], 16 * i)
                    for m in range(2):
                        dve.wait_ge(made, 4 * i + (2 * u + m + 1))
                        dve.tensor_copy(y[:, u, m, :], psum[:, 5 + m, 0:D]).then_inc(made_out, 1)

                tile(0, 0, False)
                tile(0, 1, False)
                result(0, 0, False)
                tile(1, 0, True)
                result(0, 1, False)
                tile(1, 1, True)
                with dve.Fori(1, PAIRS - 1) as i:
                    for u in range(2):
                        result(i, u, True)
                        tile(i + 1, u, True)
                result(PAIRS - 1, 0, True)
                result(PAIRS - 1, 1, True)

            @block.scalar
            def _(act):
                def store(i, u):
                    act.wait_ge(made_out, 4 * i + 2 * (u + 1))
                    act.dma_start(slots_out[bass.ts(2 * i + u, MT), :].rearrange("(s p) d -> p s d", p=P),
                                  y[:, u, :, :]).then_inc(stored[u], 16)

                def hidden(i, u, again):
                    if again:
                        act.wait_ge(made, 4 * i + (2 * u - 2))
                    act.wait_ge(first_in[u], (i + 1) * 32)
                    for b in range(HB):
                        act.wait_ge(hid, i * (2 * HB) + (u * HB + b + 1))
                        act.activation(ht[:, u, b, :], psum[:, 1 + b % 4, 0:MT], ACT.Gelu,
                                       bias=b1[:, u, b:b + 1]).then_inc(hid_out, 1)

                hidden(0, 0, False)
                hidden(0, 1, False)
                store(0, 0)
                with act.Fori(1, PAIRS) as i:
                    hidden(i, 0, True)
                    store(i - 1, 1)
                    hidden(i, 1, True)
                    store(i, 0)
                store(PAIRS - 1, 1)
                for u in range(2):
                    act.wait_ge(stored[u], 16 * PAIRS)

        RING = 2 * GROUP
        with ExitStack() as scope, nc.Block() as block:
            got = sb("c_got", [P, RING, D], at=scope)
            fetched = [sem(f"c_fetched{r}") for r in range(RING)]
            added = sem("c_added")
            stored = sem("c_stored")

            @block.gpsimd
            def _(pool):
                for c in range(2 * NT):
                    if c >= RING:
                        pool.wait_ge(added, c - RING + 1)
                    pool.indirect_dma_start(got[:, c % RING, :], None, slots_out,
                                            bass.IndirectOffsetOnAxis(ap=slot[:, c:c + 1].bitcast(U32), axis=0)
                                            ).then_inc(fetched[c % RING], 16)

            @block.vector
            def _(dve):
                with dve.Fori(0, NT // GROUP) as g:
                    for r in range(RING):
                        own = X[:, bass.ds(g * GROUP + r // 2, 1), :].rearrange("p a d -> p (a d)")
                        dve.wait_ge(fetched[r], (g + 1) * 16)
                        if r % 2:
                            dve.wait_ge(added, g * RING + r)
                        dve.scalar_tensor_tensor(own, got[:, r, :], share[:, bass.ds(g * GROUP + r // 2, 1), r % 2], own,
                                                 ALU.mult, ALU.add).then_inc(added, 1)

            @block.sync
            def _(sp):
                sp.wait_ge(added, 2 * NT)
                sp.dma_start(by_node(out), X[:, 0:NT - 1, :]).then_inc(stored, 16)
                sp.dma_start(out[(NT - 1) * P:N, :], X[0:NLAST, NT - 1, :]).then_inc(stored, 16)
                sp.wait_ge(stored, 32)


def kernel(x, src, dst, edge_weight, L0_gnn_W, L0_gnn_bias, L0_gnn_gamma, L0_gnn_beta, L0_ffn_attention_mask, L0_ffn_wr,
           L0_ffn_br, L0_ffn_w1, L0_ffn_b1, L0_ffn_w2, L0_ffn_b2, L1_gnn_W1, L1_gnn_b1, L1_gnn_W2, L1_gnn_b2, L1_gnn_eps,
           L1_gnn_offset, L1_gnn_scale, L1_ffn_Wr, L1_ffn_br, L1_ffn_ln_g, L1_ffn_ln_b, L1_ffn_W1, L1_ffn_b1, L1_ffn_W2,
           L1_ffn_b2):
    import numpy as np
    import concourse.bacc as bacc
    from concourse.bass_utils import run_bass_kernel_spmd

    def blocks(a):
        return np.asarray(a).reshape(NE, -1, P).transpose(0, 2, 1)

    def weight_blocks(a):
        a = np.asarray(a)
        return a.reshape(NE, -1, P, a.shape[2]).transpose(0, 2, 1, 3)

    column_blocks = lambda a: np.asarray(a).reshape(-1, P).T
    laid = {
        "x": x, "src": src, "dst": dst, "edge_weight": edge_weight, "g0_w": L0_gnn_W, "g0_bias": column_blocks(L0_gnn_bias),
        "g0_gamma": column_blocks(L0_gnn_gamma), "g0_beta": column_blocks(L0_gnn_beta), "f0_wr": column_blocks(L0_ffn_wr), "f0_br": L0_ffn_br,
        "f0_w1": L0_ffn_w1, "f0_b1": column_blocks(L0_ffn_b1), "f0_w2": L0_ffn_w2, "f0_b2": L0_ffn_b2,
        "g1_w1": L1_gnn_W1, "g1_b1": column_blocks(L1_gnn_b1), "g1_w2": L1_gnn_W2, "g1_b2": L1_gnn_b2,
        "g1_eps": L1_gnn_eps, "g1_offset": L1_gnn_offset, "g1_scale": L1_gnn_scale, "m_wr": L1_ffn_Wr, "m_br": L1_ffn_br,
        "m_g": blocks(L1_ffn_ln_g), "m_b": blocks(L1_ffn_ln_b), "m_w1": weight_blocks(L1_ffn_W1),
        "m_b1": blocks(L1_ffn_b1), "m_w2": weight_blocks(L1_ffn_W2), "m_b2": L1_ffn_b2,
    }
    nc = bacc.Bacc("TRN2", target_bir_lowering=False, num_devices=1)
    arrays = {name: np.ascontiguousarray(a) for name, a in laid.items()}
    args = {name: nc.dram_tensor("in_" + name, a.shape, mybir.dt.from_np(a.dtype), kind="ExternalInput").ap()
            for name, a in arrays.items()}
    out = nc.dram_tensor("out", (N, D), F32, kind="ExternalOutput").ap()
    build(nc, **args, out=out)
    r = run_bass_kernel_spmd(nc, [{"in_" + name: a for name, a in arrays.items()}], core_ids=[0])
    return r.results[0]["out"]
```

```python
from contextlib import ExitStack, contextmanager

import concourse.bass as bass
from concourse import mybir

ALU = mybir.AluOpType
ACT = mybir.ActivationFunctionType
AX = mybir.AxisListType
F32 = mybir.dt.float32
I32 = mybir.dt.int32
U32 = mybir.dt.uint32
F32R = mybir.dt.float32r

P = 128
D = 256
KD = D // P
N = 6250
NT = -(-N // P)
NLAST = N - (NT - 1) * P
E = 100000
EJ = -(-E // P)
ETAIL = E - (P - 1) * EJ
NB = NT + 1
SORT_J = 23
SORT_STEPS = EJ // SORT_J
PER = 3
CHUNKS = -(-((E + NT * (P - 1)) // P + 1) // 32) * 32
REC = 4
GB = 16
GSEM = 4
BANK = 512
GROUP = 7
GROUPS = NT // GROUP
TOPK = max(1, int(0.5 * N)) - 1
NE = 8
HM = 1024
MT = 2 * P
UNITS = -(-NT // 2)
MTILES = (2 * NT * P + NE * (MT - 1)) // MT
SC = MTILES * MT // P
MIN_PAIRS = 2 * NT * P // (2 * MT)
PEELED = 4
assert MIN_PAIRS > PEELED and (MTILES - 2 * MIN_PAIRS) * MT % (2 * P) == 0
assert SORT_STEPS * SORT_J == EJ and SORT_STEPS % 2 == 0 and (SORT_STEPS // 2 - 1) * PER == NT - 1 and NT % GROUP == 0 and GROUPS % 2 == 1


class Steps:

    def __init__(self, engine, sem):
        self.engine, self.sem, self.base, self.n = engine, sem, 0, 0

    def __call__(self, instruction):
        self.n += 1
        instruction.then_inc(self.sem, 1)
        self.engine.wait_ge(self.sem, self.base + self.n)

    @contextmanager
    def loop(self, first, last, per):
        start = self.base + self.n
        with self.engine.Fori(first, last) as i:
            self.base, self.n = (i - first) * per + start, 0
            yield i
            assert self.n == per, self.n
        self.base, self.n = start + (last - first) * per, 0


def wait(engine, sem, value):
    if not (isinstance(value, int) and value <= 0):
        engine.wait_ge(sem, value)


def build(nc, x, src, dst, edge_weight, g0_w, g0_bias, g0_gamma, g0_beta, f0_wr, f0_br, f0_w1, f0_b1, f0_w2, f0_b2,
          g1_w1, g1_b1, g1_w2, g1_b2, g1_eps, g1_offset, g1_scale, m_wr, m_br, m_g, m_b, m_w1, m_b1, m_w2, m_b2, out):
    dram = lambda name, shape, dt=F32: nc.dram_tensor(name, shape, dt, kind="Internal").ap()
    table = [dram("table0", (NT * P, D)), dram("table1", (NT * P, D))]
    records = dram("records", (P * CHUNKS, REC), I32)
    chunk_tile_row = dram("chunk_tile_row", (7 * P,), I32)
    expert_table = dram("expert_table", (NT * P, D))
    slots_out = dram("slots_out", (MTILES * MT, D))
    expert_row = dram("expert_row", (P,), I32)
    by_node = lambda a: a[0:(NT - 1) * P, :].rearrange("(t p) d -> p t d", p=P)

    ctx = ExitStack()
    with ctx:
        def sem(name):
            return ctx.enter_context(nc.semaphore(name))

        def sb(name, shape, dt=F32, at=None):
            return (at or ctx).enter_context(nc.sbuf_tensor(name, shape, dt))

        s = Steps(nc.vector, sem("vector_step"))
        dma_open = sem("indirect_dma_open")
        psum = ctx.enter_context(nc.psum_tensor("psum", [P, 8, BANK], F32))

        X = sb("X", [P, NT, D])
        ident = sb("ident", [P, P])
        columns = sb("columns", [P, P])
        before = sb("before", [P, P])
        ones = sb("ones", [P, P])
        ones_last = sb("ones_last", [P, P])
        part = sb("part", [P, 1])
        chunk_tile = sb("chunk_tile", [1, 7 * P], I32)
        stats = sb("stats", [P, NT, 6])
        moments = sb("moments", [P, NT, 2])
        rstd = sb("rstd", [P, NT])
        node_stats = sb("node_stats", [P, KD, NT, 6])
        mw = sb("mw", [P, NT])
        expert = sb("expert", [1, P], I32)
        tile_pairs = sb("tile_pairs", [P, 1], I32)
        slot = sb("slot", [P, 2 * NT], I32)
        share = sb("share", [P, NT, 2])
        node_of = sb("node_of", [P, SC], I32)
        wgt = sb("wgt", [P, NT])
        f0_br_row = sb("f0_br_row", [P, 1])

        def split_product(pe, to, a_hi, a_lo, b_hi, b_lo, first, last):
            pe.matmul(to, a_hi, b_hi, start=first, stop=False)
            pe.matmul(to, a_hi, b_lo, start=False, stop=False)
            return pe.matmul(to, a_lo, b_hi, start=False, stop=last)

        def row(of, t):
            return of[:, bass.ds(t, 1), :].rearrange("p a d -> p (a d)")

        def group_rows(of, g):
            return of[:, bass.ts(g, GROUP), :]

        def each_group(body):
            for g in range(GROUPS):
                body(g, g, g > 0)

        def over_groups(engine, body):
            body(0, 0, False)
            body(1, 1, False)
            with engine.Fori(1, GROUPS // 2) as i:
                body(2 * i, 0, True)
                body(2 * i + 1, 1, True)
            body(GROUPS - 1, 0, True)

        def row_stats(dve, steps, rows):
            with steps.loop(0, GROUPS, 1) as g:
                for m in range(GROUP):
                    ins = dve.bn_stats(row(stats, g * GROUP + m), row(rows, g * GROUP + m))
                steps(ins)
            row_moments(dve, steps)

        def row_moments(dve, steps):
            mean, var = moments[:, :, 0], moments[:, :, 1]
            steps(dve.tensor_tensor(mean, stats[:, :, 1], stats[:, :, 4], ALU.add))
            steps(dve.tensor_scalar(mean, mean, 0.5, None, ALU.mult))
            steps(dve.tensor_tensor(rstd[:], stats[:, :, 1], stats[:, :, 4], ALU.subtract))
            steps(dve.scalar_tensor_tensor(rstd[:], rstd[:], 0.25, rstd[:], ALU.mult, ALU.mult))
            steps(dve.tensor_tensor(var, stats[:, :, 2], stats[:, :, 5], ALU.add))
            steps(dve.scalar_tensor_tensor(var, var, 1.0 / D, rstd[:], ALU.mult, ALU.add))

        var_ready, root_ready = sem("var_ready"), sem("root_ready")

        def row_rstd(dve, steps, eps, n):
            dve.tensor_scalar(rstd[:], moments[:, :, 1], eps, None, ALU.add).then_inc(var_ready, 1)
            dve.wait_ge(root_ready, n)
            steps(dve.reciprocal(rstd[:], rstd[:]))

        def row_root(act, n):
            act.wait_ge(var_ready, n)
            act.activation(rstd[:], rstd[:], ACT.Sqrt).then_inc(root_ready, 1)

        def normalise_tile(dve, to, rows, t):
            return dve.tensor_scalar(to, row(rows, t), moments[:, bass.ds(t, 1), 0], rstd[:, bass.ds(t, 1)],
                                     ALU.subtract, ALU.mult)

        with ExitStack() as scope, nc.Block() as block:
            here = lambda name, shape, dt=F32: sb(name, shape, dt, scope)
            src_i = here("src_i", [P, EJ], I32)
            dst_i = here("dst_i", [P, EJ], I32)
            w_e = here("w_e", [P, EJ])
            tile_i = here("tile_i", [P, EJ], I32)
            tile_f = here("tile_f", [P, EJ])
            local_f = here("local_f", [P, EJ])
            junk = here("junk", [P, 2, EJ])
            count = here("count", [P, NB])
            nchunk_i = here("nchunk_i", [P, NB], I32)
            nchunk = here("nchunk", [P, NB])
            upto = here("upto", [P, NB])
            first = here("first", [P, NB])
            chunk_no_i = here("chunk_no_i", [P, 7], I32)
            chunk_no = here("chunk_no", [P, 7])
            passed = here("passed", [P, 7, NT])
            chunk_tile_f = here("chunk_tile_f", [P, 7])
            chunk_tile_i = here("chunk_tile_i", [P, 7], I32)
            hot = here("hot", [P, NB, SORT_J + 1])
            keep = here("keep", [P, NB, SORT_J + 1])
            upto_slot = here("upto_slot", [P, NB, SORT_J + 1])
            picked = here("picked", [P, NB, SORT_J])
            slot_f = here("slot_f", [P, SORT_J])
            slot_i = here("slot_i", [P, SORT_J], I32)
            slot_q = here("slot_q", [P, SORT_J], I32)
            slot_c = here("slot_c", [P, SORT_J], I32)
            place = here("place", [P, 2, SORT_J], I32)
            rec = here("rec", [P, 2, SORT_J, REC], I32)
            zero = here("zero", [P, CHUNKS * REC], I32)
            iota_i = here("iota_i", [P, P], I32)
            part_i = here("part_i", [P, 1], I32)
            w0 = here("w0", [P, KD, D])
            xn = here("xn", [P, PER, D])
            xt = here("xt", [P, PER, KD, P])
            h_out = here("h_out", [P, PER, D])

            loaded = sem("edges_loaded")
            x_loaded = sem("x_loaded")
            w0_loaded = sem("w0_loaded")
            pads_set = sem("pads_set")
            iota_done = sem("iota_done")
            consts_done = sem("consts_done")
            local_done = sem("local_done")
            counted = sem("counted")
            totals = sem("totals")
            zero_set = sem("zero_set")
            records_clear, slots_clear = sem("records_clear"), sem("slots_clear")
            map_ready = sem("map_ready")
            map_out = sem("map_out")
            map_in = sem("map_in")
            placed = sem("placed")
            rec_filled = sem("rec_filled")
            scattered = [sem("scattered0"), sem("scattered1")]
            xn_ready = sem("ln0_rows")
            turned, turned_out = sem("h_turned"), sem("h_turned_out")
            made, made_out = sem("h_made"), sem("h_made_out")
            stored = [sem(f"h_stored{u}") for u in range(PER)]

            @block.sync
            def _(sp):
                sp.wait_ge(pads_set, 4)
                for to, of in ((src_i, src), (dst_i, dst), (w_e, edge_weight)):
                    sp.dma_start(to[0:P - 1, :], of[0:(P - 1) * EJ].rearrange("(p j) -> p j", j=EJ)).then_inc(loaded, 16)
                    sp.dma_start(to[P - 1:P, 0:ETAIL], of[(P - 1) * EJ:E].rearrange("(a j) -> a j", a=1)).then_inc(loaded, 16)
                sp.dma_start(X[:, 0:NT - 1, :], by_node(x)).then_inc(x_loaded, 16)
                sp.dma_start(X[0:NLAST, NT - 1, :], x[(NT - 1) * P:N, :]).then_inc(x_loaded, 16)
                sp.dma_start(w0[:], g0_w.rearrange("(k p) n -> p k n", p=P)).then_inc(w0_loaded, 16)
                sp.wait_ge(zero_set, 1)
                sp.dma_start(records.rearrange("(q c) f -> q (c f)", q=P), zero[:]).then_inc(records_clear, 16)
                left = slots_out[2 * MIN_PAIRS * MT:MTILES * MT, :].rearrange("(h q r) d -> h q (r d)", h=2, q=P)
                for h in range(2):
                    sp.dma_start(left[h], zero[:, 0:(MTILES - 2 * MIN_PAIRS) * MT // (2 * P) * D].bitcast(F32)).then_inc(slots_clear, 16)
                sp.wait_ge(map_ready, 1)
                sp.dma_start(chunk_tile_row.rearrange("(k p) -> p k", p=P), chunk_tile_i[:],
                             allow_slow_non_contiguous=True).then_inc(map_out, 16)
                sp.wait_ge(map_out, 16)
                sp.dma_start(chunk_tile[:], chunk_tile_row.rearrange("(a k) -> a k", a=1)).then_inc(map_in, 16)

                def store(t, u):
                    sp.dma_start(table[0][bass.ts(t, P), :], h_out[:, u, :]).then_inc(stored[u], 16)

                with sp.Fori(0, NT // PER) as i:
                    for u in range(PER):
                        sp.wait_ge(made_out, PER * i + (u + 1))
                        store(PER * i + u, u)
                sp.wait_ge(made_out, NT)
                store(NT - 1, 0)
                for u in range(PER):
                    sp.wait_ge(stored[u], 16 * (NT // PER + (u == 0)))
                sp.wait_ge(map_in, 16)
                sp.wait_ge(slots_clear, 32)

            @block.gpsimd
            def _(pool):
                pool.memset(zero[:], 0).then_inc(zero_set, 1)
                pool.iota(iota_i[:], [[1, P]], base=0, channel_multiplier=0).then_inc(iota_done, 1)
                pool.iota(part_i[:], [[0, 1]], base=0, channel_multiplier=1).then_inc(iota_done, 1)
                pool.iota(chunk_no_i[:], [[P, 7]], base=0, channel_multiplier=1).then_inc(iota_done, 1)
                pool.wait_ge(records_clear, 16)
                with pool.Fori(0, SORT_STEPS // 2) as i:
                    for u in range(2):
                        pool.wait_ge(placed, 2 * i + (u + 1))
                        pool.wait_ge(rec_filled, 6 * i + 3 * (u + 1) + 1)
                        pool.sem_inc(dma_open, 1)
                        for j in range(SORT_J):
                            pool.indirect_dma_start(
                                records, bass.IndirectOffsetOnAxis(ap=place[:, u, j:j + 1].bitcast(U32), axis=0),
                                rec[:, u, j, :], None).then_inc(scattered[u], 16)
                for u in range(2):
                    pool.wait_ge(scattered[u], 16 * SORT_J * (SORT_STEPS // 2))

            @block.vector
            def _(dve):
                dve.memset(src_i[:], NT * P).then_inc(pads_set, 1)
                dve.memset(dst_i[:], 0).then_inc(pads_set, 1)
                dve.memset(w_e[:], 0.0).then_inc(pads_set, 1)
                dve.memset(X[:, NT - 1, :], 0.0).then_inc(pads_set, 1)
                dve.wait_ge(iota_done, 3)
                s(dve.tensor_copy(columns[:], iota_i[:]))
                s(dve.tensor_copy(part[:], part_i[:]))
                s(dve.tensor_copy(chunk_no[:], chunk_no_i[:]))
                s(dve.tensor_scalar(ident[:], columns[:], part[:, 0:1], None, ALU.is_equal))
                s(dve.tensor_scalar(before[:], columns[:], part[:, 0:1], None, ALU.is_gt))
                s(dve.memset(ones[:], 1.0))
                s(dve.tensor_scalar(ones_last[:], ones[:], part[:, 0:1], float(NLAST), ALU.mult, ALU.is_lt))
                s(dve.memset(keep[:], 1.0))
                s(dve.memset(keep[:, :, 0:1], 0.0))
                dve.engine_nop().then_inc(consts_done, 1)
                dve.wait_ge(loaded, 96)
                s(dve.tensor_scalar(tile_i[:], src_i[:], 7, None, ALU.logical_shift_right))
                s(dve.tensor_scalar(src_i[:], src_i[:], P - 1, None, ALU.bitwise_and))
                s(dve.tensor_copy(tile_f[:], tile_i[:]))
                dve.tensor_copy(local_f[:], src_i[:]).then_inc(local_done, 1)
                for b in range(NB):
                    if b >= 2:
                        dve.wait_ge(counted, b - 1)
                    dve.tensor_scalar(junk[:, b % 2, :], tile_f[:], float(b), 0.0, ALU.is_equal, ALU.add,
                                      accum_out=count[:, b:b + 1]).then_inc(counted, 1)
                dve.wait_ge(totals, 2)
                s(dve.tensor_scalar(nchunk_i[:], psum[:, 1, 0:NB], float(P - 1), None, ALU.add))
                s(dve.tensor_scalar(nchunk_i[:], nchunk_i[:], 7, None, ALU.logical_shift_right))
                s(dve.tensor_copy(nchunk[:], nchunk_i[:]))
                s(dve.tensor_tensor_scan(upto[:], ones[:, 0:NB], nchunk[:], 0.0, ALU.mult, ALU.add))
                s(dve.tensor_tensor(first[:], upto[:], nchunk[:], ALU.subtract))
                s(dve.scalar_tensor_tensor(first[:], first[:], float(P), psum[:, 0, 0:NB], ALU.mult, ALU.add))
                s(dve.tensor_scalar(upto_slot[:, :, SORT_J], first[:], -1.0, None, ALU.add))
                s(dve.tensor_tensor(passed[:], chunk_no[:].unsqueeze(2).to_broadcast([P, 7, NT]),
                                    upto[:, 0:NT].unsqueeze(1).to_broadcast([P, 7, NT]), ALU.is_ge))
                s(dve.tensor_reduce(chunk_tile_f[:], passed[:], AX.X, ALU.add))
                dve.tensor_scalar(chunk_tile_i[:], chunk_tile_f[:], float(NT - 1), None, ALU.min).then_inc(map_ready, 1)

                def sort_step(k, u, reused):
                    s(dve.tensor_copy(hot[:, :, 0], upto_slot[:, :, SORT_J]))
                    s(dve.tensor_tensor(hot[:, :, 1:], tile_f[:, bass.ts(k, SORT_J)].unsqueeze(1).to_broadcast([P, NB, SORT_J]),
                                        columns[:, 0:NB].unsqueeze(2).to_broadcast([P, NB, SORT_J]), ALU.is_equal))
                    s(dve.tensor_tensor_scan(upto_slot[:].rearrange("p b j -> p (b j)"), keep[:].rearrange("p b j -> p (b j)"),
                                             hot[:].rearrange("p b j -> p (b j)"), 0.0, ALU.mult, ALU.add))
                    s(dve.tensor_tensor(picked[:], hot[:, :, 1:], upto_slot[:, :, 1:], ALU.mult))
                    s(dve.tensor_reduce(slot_f[:], picked[:].rearrange("p b j -> p j b"), AX.X, ALU.add))
                    s(dve.tensor_copy(slot_i[:], slot_f[:]))
                    s(dve.tensor_scalar(slot_q[:], slot_i[:], P - 1, None, ALU.bitwise_and))
                    s(dve.tensor_scalar(slot_c[:], slot_i[:], 7, None, ALU.logical_shift_right))
                    if reused is not None:
                        dve.wait_ge(scattered[u], reused)
                    dve.scalar_tensor_tensor(place[:, u, :], slot_q[:], float(CHUNKS), slot_c[:],
                                             ALU.mult, ALU.add).then_inc(placed, 1)

                for u in range(2):
                    sort_step(u, u, None)
                dve.wait_ge(x_loaded, 32)
                row_stats(dve, s, X)
                row_rstd(dve, s, 1e-5, 1)

                def normalise(t, u, earlier):
                    if earlier is not None:
                        dve.wait_ge(turned, earlier)
                    normalise_tile(dve, xn[:, u, :], X, t).then_inc(xn_ready, 1)

                def pair(i, first):
                    for u in range(2):
                        sort_step(2 * i + u, u, i * (16 * SORT_J))
                        for m in range(u, 1 + u * (PER - 1)):
                            normalise((i - 1) * PER + m, m, None if first else (i - 1) * PER + (m + 1 - PER))

                pair(1, True)
                with s.loop(2, SORT_STEPS // 2, 16) as i:
                    pair(i, False)
                normalise(NT - 1, 0, NT - PER)

            @block.scalar
            def _(act):
                def fill(k, u, reused):
                    if reused is not None:
                        act.wait_ge(scattered[u], reused)
                    at = bass.ts(k, SORT_J)
                    act.copy(rec[:, u, :, 0], dst_i[:, at]).then_inc(rec_filled, 1)
                    act.copy(rec[:, u, :, 1].bitcast(F32), local_f[:, at]).then_inc(rec_filled, 1)
                    act.copy(rec[:, u, :, 2].bitcast(F32), w_e[:, at]).then_inc(rec_filled, 1)

                act.wait_ge(zero_set, 1)
                act.copy(rec[:].bitcast(F32).rearrange("p a j f -> p (a j f)"), zero[:, 0:2 * SORT_J * REC].bitcast(F32)).then_inc(rec_filled, 1)
                act.wait_ge(rec_filled, 1)
                act.wait_ge(loaded, 96)
                act.wait_ge(local_done, 1)
                for u in range(2):
                    fill(u, u, None)
                row_root(act, 1)

                def tile(t, u, reused):
                    act.wait_ge(turned, t + 1)
                    act.copy(xt[:, u, :, :].rearrange("p k n -> p (k n)"), psum[:, 2 + u, 0:D]).then_inc(turned_out, 1)
                    act.wait_ge(made, t + 1)
                    if reused is not None:
                        act.wait_ge(stored[u], reused)
                    act.copy(h_out[:, u, :], psum[:, 2 + PER + u, 0:D]).then_inc(made_out, 1)

                def pair(i, first):
                    for u in range(2):
                        fill(2 * i + u, u, i * (16 * SORT_J))
                        for m in range(u, 1 + u * (PER - 1)):
                            tile((i - 1) * PER + m, m, None if first else (i - 1) * 16)

                pair(1, True)
                with act.Fori(2, SORT_STEPS // 2) as i:
                    pair(i, False)
                tile(NT - 1, 0, 16 * (NT // PER))

            @block.tensor
            def _(pe):
                pe.wait_ge(consts_done, 1)
                pe.wait_ge(counted, NB)
                pe.matmul(psum[:, 0, 0:NB], before[:], count[:], start=True, stop=True).then_inc(totals, 1)
                pe.matmul(psum[:, 1, 0:NB], ones[:], count[:], start=True, stop=True).then_inc(totals, 1)
                pe.wait_ge(w0_loaded, 16)

                def tile(t, u, earlier):
                    if earlier is not None:
                        pe.wait_ge(turned_out, earlier)
                    pe.wait_ge(xn_ready, t + 1)
                    for k in range(KD):
                        ins = pe.transpose(psum[:, 2 + u, k * P:(k + 1) * P], xn[:, u, k * P:(k + 1) * P], ident[:])
                    ins.then_inc(turned, 1)
                    pe.wait_ge(turned_out, t + 1)
                    if earlier is not None:
                        pe.wait_ge(made_out, earlier)
                    for k in range(KD):
                        ins = pe.matmul(psum[:, 2 + PER + u, 0:D], xt[:, u, k, :], w0[:, k, :], start=k == 0, stop=k == KD - 1)
                    ins.then_inc(made, 1)

                for t in range(PER):
                    tile(t, t, None)
                with pe.Fori(1, NT // PER) as i:
                    for u in range(PER):
                        tile(PER * i + u, u, PER * i + (u + 1 - PER))
                tile(NT - 1, 0, NT - PER)

        graph = ctx.enter_context(ExitStack())
        AT = sb("AT", [P, KD, UNITS * MT], at=graph)

        class GraphTiles:
            LOADS = 6
            PER_TILE = 5

            def __init__(self, here):
                self.w1, self.w2 = here("w1", [P, KD, D]), here("w2", [P, KD, D])
                self.b1, self.b2 = here("b1", [P, KD]), here("b2", [1, D])
                self.offset, self.scale = here("offset", [P, D]), here("scale", [P, D])
                self.hidden, self.centred = here("hidden", [P, KD, P]), here("centred", [P, D])
                self.stat, self.mean_var, self.root = here("stat", [P, KD, 6]), here("mean_var", [P, 2]), here("root", [P, 1])
                self.loaded = sem("g1_params")
                self.hid, self.hid_out, self.made, self.made_out = (sem("g1_" + w) for w in ("hid", "hid_out", "made", "made_out"))
                self.var_ready, self.root_ready = sem("g1_var"), sem("g1_root")
                self.step, self.stat_open = sem("g1_tile_step"), sem("g1_stat_open")

            def load(self, sp):
                sp.dma_start(self.w1[:], g1_w1.rearrange("(k p) n -> p k n", p=P)).then_inc(self.loaded, 16)
                sp.dma_start(self.w2[:], g1_w2.rearrange("(k p) n -> p k n", p=P)).then_inc(self.loaded, 16)
                sp.dma_start(self.b1[:], g1_b1).then_inc(self.loaded, 16)
                sp.dma_start(self.b2[:], g1_b2.rearrange("(a n) -> a n", a=1)).then_inc(self.loaded, 16)
                sp.dma_start(self.offset[:], g1_offset.partition_broadcast(P)).then_inc(self.loaded, 16)
                sp.dma_start(self.scale[:], g1_scale.partition_broadcast(P)).then_inc(self.loaded, 16)

            def result(self, t):
                return AT[:, :, bass.ts(t, P)]

            def open(self, act):
                act.sem_inc(self.made_out, 1)

            def products(self, pe, t):
                pe.wait_ge(self.made_out, t + 1)
                for b in range(KD):
                    for k in range(KD):
                        ins = pe.matmul(psum[:, 7, b * P:(b + 1) * P], self.w1[:, k, b * P:(b + 1) * P],
                                        AT[:, k, bass.ts(t, P)], start=k == 0, stop=k == KD - 1)
                ins.then_inc(self.hid, 1)
                pe.wait_ge(self.hid_out, KD * t + KD)
                for b in range(KD):
                    pe.matmul(psum[:, 7, D:2 * D], self.hidden[:, b, :], self.w2[:, b, :], start=b == 0, stop=False)
                pe.matmul(psum[:, 7, D:2 * D], ones[0:1, :], self.b2[:], start=False, stop=True).then_inc(self.made, 1)

            def functions(self, act, t):
                act.wait_ge(self.hid, t + 1)
                for b in range(KD):
                    act.activation(self.hidden[:, b, :], psum[:, 7, b * P:(b + 1) * P], ACT.Relu,
                                   bias=self.b1[:, b:b + 1]).then_inc(self.hid_out, 1)
                act.wait_ge(self.made, t + 1)
                act.activation(self.result(t), psum[:, 7, D:2 * D].rearrange("p (k n) -> p k n", k=KD), ACT.Relu).then_inc(self.made_out, 1)

            def root_of(self, act, t):
                act.wait_ge(self.var_ready, t + 1)
                act.activation(self.root[:], self.root[:], ACT.Sqrt).then_inc(self.root_ready, 1)

            def finish(self, dve, t):
                done = Steps(dve, self.step)
                done.base = t * self.PER_TILE
                halves = lambda a: a.rearrange("p (k n) -> p k n", k=KD)
                dve.wait_ge(self.made_out, t + 2)
                for k in range(KD):
                    ins = dve.bn_stats(self.stat[:, k, :], AT[:, k, bass.ts(t, P)])
                done(ins)
                dve.sem_inc(self.stat_open, 1)
                done(dve.bn_aggr(self.mean_var[:], self.stat[:].rearrange("p k s -> p (k s)")))
                dve.tensor_scalar(self.root[:], self.mean_var[:, 1:2], 1e-10, None, ALU.add).then_inc(self.var_ready, 1)
                done(dve.scalar_tensor_tensor(halves(self.centred[:]), self.result(t), self.mean_var[:, 0:1], halves(self.scale[:]),
                                              ALU.subtract, ALU.mult))
                dve.wait_ge(self.root_ready, t + 1)
                done(dve.reciprocal(self.root[:], self.root[:]))
                done(dve.scalar_tensor_tensor(row(X, t), self.centred[:], self.root[:, 0:1], row(X, t), ALU.mult, ALU.add))
                assert done.n == self.PER_TILE

            def add_offset(self, dve):
                dve.wait_ge(self.loaded, self.LOADS * 16)
                with s.loop(0, GROUPS, 1) as g:
                    s(dve.tensor_tensor(group_rows(X, g), group_rows(X, g), self.offset[:].unsqueeze(1).to_broadcast([P, GROUP, D]),
                                        ALU.add))

        def aggregate(rows, name, prepare, banks, make_tiles=None):
            since = [next(d for d in range(1, 2 * GB + 1) if banks[(c - d) % (2 * GB)] == banks[c]) for c in range(2 * GB)]
            with ExitStack() as scope, nc.Block() as block:
                here = lambda what, shape, dt=F32: sb(name + what, shape, dt, scope)
                rec = here("rec", [P, 2, GB, REC], I32)
                got = here("got", [P, 2, GB, D])
                route = here("route", [P, 2, GB, P])
                added = sem(name + "added")
                rec_in = [sem(name + "rec_in0"), sem(name + "rec_in1")]
                gathered = [[sem(name + f"gathered{u}{g}") for g in range(GB // GSEM)] for u in range(2)]
                routed, summed = sem(name + "routed"), sem(name + "summed")
                by_chunk = records.rearrange("(q c) f -> q c f", q=P)
                STEPS = CHUNKS // GB
                through_mlp = make_tiles is GraphTiles
                if make_tiles:
                    tiles_of = make_tiles(here)
                    first_tile = here("first_tile", [1, STEPS], I32)
                    first_tile_ready = sem(name + "first_tile")
                else:
                    tiles_of = None

                def complete_tiles(eng, n, body):
                    if n is None:
                        return
                    first, end = (eng.value_load(first_tile[0:1, bass.ds(m, 1)], min_val=0, max_val=NT - 1) for m in (n, n + 1))
                    with eng.If(first < end):
                        with eng.Fori(first, end) as t:
                            body(t)

                def last_tiles(eng, n, body, end=NT):
                    first_left = eng.value_load(first_tile[0:1, n + 1:n + 2], min_val=0, max_val=NT - 1)
                    with eng.If(first_left < end):
                        with eng.Fori(first_left, end) as t:
                            body(t)

                def steps_back(i, u, back):
                    return None if isinstance(i, int) and 2 * i + u < back else 2 * i + (u - back)

                def load(eng, n, u):
                    eng.dma_start(rec[:, u, :, :], by_chunk[:, bass.ts(n, GB), :]).then_inc(rec_in[u], 16)

                @block.sync
                def _(sp):
                    load(sp, 0, 0)
                    load(sp, 1, 1)
                    if through_mlp:
                        tiles_of.load(sp)
                    with sp.Fori(1, STEPS // 2) as i:
                        for u in range(2):
                            for g in range(GB // GSEM):
                                sp.wait_ge(gathered[u][g], i * (16 * GSEM))
                            sp.wait_ge(routed, 2 * i + (u - 1))
                            load(sp, 2 * i + u, u)

                @block.gpsimd
                def _(pool):
                    def gather(i, u, again):
                        pool.wait_ge(rec_in[u], 16 * (i + 1))
                        for g in range(GB // GSEM):
                            if again:
                                pool.wait_ge(summed, i * (2 * GB) + (u * GB + (g + 1) * GSEM - 2 * GB))
                            pool.sem_inc(dma_open, 1)
                            for j in range(g * GSEM, (g + 1) * GSEM):
                                pool.indirect_dma_start(
                                    got[:, u, j, :], None, rows,
                                    bass.IndirectOffsetOnAxis(ap=rec[:, u, j, 0:1].bitcast(U32), axis=0)
                                ).then_inc(gathered[u][g], 16)

                    for u in range(2):
                        gather(0, u, False)
                    with pool.Fori(1, STEPS // 2) as i:
                        for u in range(2):
                            gather(i, u, True)

                @block.vector
                def _(dve):
                    if prepare:
                        prepare(dve)
                    if tiles_of:
                        dve.tensor_copy(first_tile[:], chunk_tile[0:1, 0:CHUNKS].rearrange("a (n g) -> a n g", g=GB)[:, :, 0]
                                        ).then_inc(first_tile_ready, 1)
                        dve.wait_ge(first_tile_ready, 1)
                        dve.memset(first_tile[:, 0:1], 0).then_inc(first_tile_ready, 1)
                        dve.wait_ge(first_tile_ready, 2)
                    if through_mlp:
                        tiles_of.add_offset(dve)
                    dve.engine_nop().then_inc(added, 1)

                    def step_of(i, u, again):
                        dve.wait_ge(rec_in[u], 16 * (i + 1))
                        if again:
                            dve.wait_ge(summed, i * (2 * GB) + (u * GB - GB))
                        for j in range(GB):
                            ins = dve.tensor_scalar(route[:, u, j, :], columns[:], rec[:, u, j, 1:2].bitcast(F32),
                                                    rec[:, u, j, 2:3].bitcast(F32), ALU.is_equal, ALU.mult)
                        ins.then_inc(routed, 1)
                        if through_mlp:
                            complete_tiles(dve, steps_back(i, u, 2), lambda t: tiles_of.finish(dve, t))
                        elif again or u:
                            def finish_tile(t):
                                dve.wait_ge(added, i * (2 * GB) + (u * GB + 1))
                                tiles_of.finish(dve, t)
                            complete_tiles(dve, steps_back(i, u, 1), finish_tile)
                        first = i * (2 * GB) + u * GB
                        _, tiles = nc.values_load_multi_w_load_instructions(
                            chunk_tile[0:1, bass.ds(first, GB)], engines=(mybir.EngineType.DVE,), min_val=0, max_val=NT - 1,
                            skip_runtime_bounds_check_because="the map is clamped to the tiles")
                        for j in range(GB):
                            to = AT[:, :, bass.ts(tiles[j], P)]
                            if j % 2 == 0:
                                dve.wait_ge(summed, first + j + 2)
                            dve.wait_ge(added, first + j + 1)
                            dve.tensor_tensor(to, to, psum[:, banks[u * GB + j], 0:D].rearrange("p (k n) -> p k n", k=KD),
                                              ALU.add).then_inc(added, 1)

                    for u in range(2):
                        step_of(0, u, False)
                    with dve.Fori(1, STEPS // 2) as i:
                        for u in range(2):
                            step_of(i, u, True)
                    dve.wait_ge(added, CHUNKS + 1)
                    if through_mlp:
                        last_tiles(dve, STEPS - 3, lambda t: tiles_of.finish(dve, t))
                    else:
                        last_tiles(dve, STEPS - 2, lambda t: tiles_of.finish(dve, t), NT - 1)
                        tiles_of.finish(dve, NT - 1, NLAST)

                @block.tensor
                def _(pe):
                    def step_of(i, u, again):
                        pe.wait_ge(routed, 2 * i + (u + 1))
                        for j in range(GB):
                            if j % GSEM == 0:
                                pe.wait_ge(gathered[u][j // GSEM], (i + 1) * (16 * GSEM))
                            c = u * GB + j
                            if again or c >= since[c]:
                                pe.wait_ge(added, i * (2 * GB) + (c + 2 - since[c]))
                            for k in range(KD):
                                ins = pe.matmul(psum[:, banks[c], k * P:(k + 1) * P], got[:, u, j, k * P:(k + 1) * P],
                                                route[:, u, j, :], start=True, stop=True)
                            ins.then_inc(summed, 1)
                        if through_mlp:
                            complete_tiles(pe, steps_back(i, u, 1), lambda t: tiles_of.products(pe, t))

                    if through_mlp:
                        pe.wait_ge(tiles_of.loaded, tiles_of.LOADS * 16)
                        pe.wait_ge(first_tile_ready, 2)
                    for u in range(2):
                        step_of(0, u, False)
                    with pe.Fori(1, STEPS // 2) as i:
                        for u in range(2):
                            step_of(i, u, True)
                    if through_mlp:
                        pe.wait_ge(added, CHUNKS + 1)
                        last_tiles(pe, STEPS - 2, lambda t: tiles_of.products(pe, t))

                if through_mlp:
                    @block.scalar
                    def _(act):
                        act.wait_ge(tiles_of.loaded, tiles_of.LOADS * 16)
                        act.wait_ge(first_tile_ready, 2)
                        tiles_of.open(act)

                        def step_of(i, u):
                            complete_tiles(act, steps_back(i, u, 2), lambda t: tiles_of.root_of(act, t))
                            complete_tiles(act, steps_back(i, u, 1), lambda t: tiles_of.functions(act, t))
                        for u in range(2):
                            step_of(0, u)
                        with act.Fori(1, STEPS // 2) as i:
                            for u in range(2):
                                step_of(i, u)
                        complete_tiles(act, STEPS - 2, lambda t: tiles_of.root_of(act, t))
                        last_tiles(act, STEPS - 2, lambda t: tiles_of.functions(act, t))
                        last_tiles(act, STEPS - 2, lambda t: tiles_of.root_of(act, t))

        def start_from_zero(dve):
            for k in range(KD):
                s(dve.memset(AT[:, k, :], 0.0))

        class NodeStats:

            def __init__(self, here):
                pass

            def finish(self, dve, t, nodes=P):
                for k in range(KD):
                    dve.bn_stats(node_stats[:, k, bass.ds(t, 1), :].rearrange("p a s -> p (a s)"),
                                 AT[:, k, bass.ds(t * P, nodes)])

        aggregate(table[0], "g0_", start_from_zero, [c % 8 for c in range(2 * GB)], NodeStats)

        class Turn:

            def __init__(self, name, scope, groups=2):
                self.ring = sb(name + "ring", [P, groups, GROUP, D], at=scope)
                self.ready, self.turned, self.out = sem(name + "ring_ready"), sem(name + "turned"), sem(name + "turned_out")

            def normalise(self, dve, g, u):
                for m in range(GROUP):
                    ins = normalise_tile(dve, self.ring[:, u, m, :], X, g * GROUP + m)
                ins.then_inc(self.ready, 1)

            def turn(self, pe, g, u, m, again):
                if m == 0:
                    pe.wait_ge(self.ready, g + 1)
                if again:
                    pe.wait_ge(self.out, g * GROUP + (m + 1 - GROUP))
                for k in range(KD):
                    ins = pe.transpose(psum[:, m, k * P:(k + 1) * P], self.ring[:, u, m, k * P:(k + 1) * P], ident[:])
                ins.then_inc(self.turned, 1)

        class TokenWeights:

            def __init__(self, scope):
                here = lambda what, shape, dt=F32: sb("f0_" + what, shape, dt, scope)
                self.ht = here("ht", [P, HB * MT])
                self.w1_hi, self.w1_lo = here("w1_hi", [P, KD * HB * P], F32R), here("w1_lo", [P, KD * HB * P], F32R)
                self.w2, self.w2_hi = here("w2", [P, HB * D]), here("w2_hi", [P, HB * D], F32R)
                self.w2_lo = here("w2_lo", [P, HB * D], F32R)
                self.b1, self.b2, self.b2_hi = here("b1", [P, HB]), here("b2", [1, D]), here("b2_hi", [1, D], F32R)
                self.b2_lo, self.ones_r = here("b2_lo", [1, D], F32R), here("ones_r", [1, P], F32R)
                self.loaded, self.high, self.low = sem("f0_weights"), sem("f0_weights_hi"), sem("f0_weights_lo")

            def load(self, sp):
                sp.dma_start(self.ht[:].rearrange("p (k n) -> p k n", k=KD), f0_w1.rearrange("(k p) n -> p k n", p=P)).then_inc(self.loaded, 16)
                sp.dma_start(self.w2[:].rearrange("p (k n) -> p k n", k=HB), f0_w2.rearrange("(k p) n -> p k n", p=P)).then_inc(self.loaded, 16)
                sp.dma_start(self.b1[:], f0_b1).then_inc(self.loaded, 16)
                sp.dma_start(self.b2[:], f0_b2.rearrange("(a n) -> a n", a=1)).then_inc(self.loaded, 16)

            def split_high(self, act):
                act.wait_ge(self.loaded, 64)
                act.copy(self.w1_hi[:], self.ht[:]).then_inc(self.high, 1)
                act.copy(self.w2_hi[:], self.w2[:]).then_inc(self.high, 1)
                act.copy(self.b2_hi[:], self.b2[:]).then_inc(self.high, 1)
                act.copy(self.ones_r[:], ones[0:1, :]).then_inc(self.high, 1)

            def split_low(self, pool):
                pool.wait_ge(self.high, 4)
                pool.tensor_tensor(self.w1_lo[:], self.ht[:], self.w1_hi[:], ALU.subtract).then_inc(self.low, 1)
                pool.tensor_tensor(self.w2_lo[:], self.w2[:], self.w2_hi[:], ALU.subtract).then_inc(self.low, 1)
                pool.tensor_tensor(self.b2_lo[:], self.b2[:], self.b2_hi[:], ALU.subtract).then_inc(self.low, 1)

        HB = HM // P
        assert f0_w1.shape[1] == HM
        token_scope = ctx.enter_context(ExitStack())
        token = TokenWeights(token_scope)
        with ExitStack() as scope, nc.Block() as block:
            here = lambda what, shape, dt=F32: sb("bn_" + what, shape, dt, scope)
            node_moments = here("node_moments", [P, KD, 2])
            gamma, beta, bias = here("gamma", [P, KD]), here("beta", [P, KD]), here("bias", [P, KD])
            gain, shift, root = here("gain", [P, KD]), here("shift", [P, KD]), here("root", [P, KD])
            active = here("active", [P, 2, KD, GROUP * P])
            wr = here("wr", [P, D])
            scored = here("scored", [P, GROUP, D])
            turn = Turn("ln1_", scope)

            params = sem("bn_params")
            coef_ready = sem("bn_coef")
            activated, back, taken = sem("bn_activated"), sem("bn_back"), sem("bn_taken")
            ring_used, score_step = sem("ln1_used"), sem("ln1_score_step")

            @block.sync
            def _(sp):
                for to, of in ((gamma, g0_gamma), (beta, g0_beta), (bias, g0_bias)):
                    sp.dma_start(to[:], of).then_inc(params, 16)
                sp.dma_start(wr[:], f0_wr.partition_broadcast(P)).then_inc(params, 16)
                sp.dma_start(f0_br_row[:], f0_br.partition_broadcast(P)).then_inc(params, 16)
                token.load(sp)
                sp.wait_ge(params, 80)

            @block.scalar
            def _(act):
                act.wait_ge(var_ready, 2)
                act.activation(root[:], root[:], ACT.Sqrt).then_inc(root_ready, 1)
                act.wait_ge(coef_ready, 1)

                def activate(g, u, again):
                    if again:
                        act.wait_ge(back, g * GROUP - GROUP)
                    for k in range(KD):
                        act.activation(active[:, u, k, :], AT[:, k, bass.ts(g, GROUP * P)], ACT.Relu,
                                       bias=shift[:, k:k + 1], scale=gain[:, k:k + 1]).then_inc(activated, 1)
                token.split_high(act)
                over_groups(act, activate)
                row_root(act, 3)

                def turn_out(g, u, again):
                    for m in range(GROUP):
                        act.wait_ge(turn.turned, g * GROUP + (m + 1))
                        act.copy(AT[:, :, bass.ds((g * GROUP + m) * P, P)], psum[:, m, 0:D].rearrange("p (k n) -> p k n", k=KD)
                                 ).then_inc(turn.out, 1)
                over_groups(act, turn_out)

            @block.gpsimd
            def _(pool):
                token.split_low(pool)

                def residual(g, u, again):
                    pool.wait_ge(turn.ready, g + 1)
                    pool.tensor_tensor(group_rows(X, g), group_rows(X, g), turn.ring[:, u, :, :], ALU.add).then_inc(ring_used, 1)
                over_groups(pool, residual)

            @block.tensor
            def _(pe):
                def turn_back(g, u, again):
                    pe.wait_ge(activated, KD * (g + 1))
                    for m in range(GROUP):
                        if again or u:
                            pe.wait_ge(taken, g * GROUP + (m + 1 - GROUP))
                        for k in range(KD):
                            ins = pe.transpose(psum[:, m, k * P:(k + 1) * P], active[:, u, k, m * P:(m + 1) * P], ident[:])
                        ins.then_inc(back, 1)
                over_groups(pe, turn_back)
                pe.wait_ge(taken, NT)
                pe.wait_ge(params, 80)

                over_groups(pe, lambda g, u, again: [turn.turn(pe, g, u, m, u or again) for m in range(GROUP)])

            @block.vector
            def _(dve):
                for k in range(KD):
                    ins = dve.bn_aggr(node_moments[:, k, :], node_stats[:, k, :, :].rearrange("p i s -> p (i s)"))
                s(ins)
                dve.wait_ge(params, 80)
                dve.tensor_scalar(root[:], node_moments[:, :, 1], 1e-5, None, ALU.add).then_inc(var_ready, 1)
                s(dve.tensor_tensor(shift[:], node_moments[:, :, 0], bias[:], ALU.add))
                s(dve.tensor_tensor(shift[:], bias[:], shift[:], ALU.subtract))
                dve.wait_ge(root_ready, 2)
                s(dve.reciprocal(gain[:], root[:]))
                s(dve.tensor_tensor(gain[:], gain[:], gamma[:], ALU.mult))
                s(dve.tensor_tensor(shift[:], shift[:], gain[:], ALU.mult))
                dve.tensor_tensor(shift[:], shift[:], beta[:], ALU.add).then_inc(coef_ready, 1)

                def residual(g, u, again):
                    for m in range(GROUP):
                        dve.wait_ge(back, g * GROUP + (m + 1))
                        own = row(X, g * GROUP + m)
                        dve.tensor_tensor(own, own, psum[:, m, 0:D], ALU.add).then_inc(taken, 1)
                over_groups(dve, residual)
                dve.wait_ge(taken, NT)
                row_stats(dve, s, X)
                row_rstd(dve, s, 1e-5, 3)

                def normalise(g, u, again):
                    if again:
                        dve.wait_ge(turn.turned, g * GROUP - GROUP)
                        dve.wait_ge(ring_used, g - 1)
                    turn.normalise(dve, g, u)
                    dve.wait_ge(turn.ready, g + 1)
                    dve.tensor_tensor(scored[:], turn.ring[:, u, :, :], wr[:].unsqueeze(1).to_broadcast([P, GROUP, D]),
                                      ALU.mult).then_inc(score_step, 1)
                    dve.wait_ge(score_step, 2 * g + 1)
                    dve.tensor_reduce(wgt[:, bass.ts(g, GROUP)], scored[:], AX.X, ALU.add).then_inc(score_step, 1)
                    dve.wait_ge(score_step, 2 * g + 2)
                over_groups(dve, normalise)
                s(dve.tensor_scalar(wgt[:], wgt[:], f0_br_row[:, 0:1], None, ALU.add))

        class TopK:
            STEPS = 36

            def __init__(self, scope):
                here = lambda what, shape, dt=F32: sb("topk_" + what, shape, dt, scope)
                self.valid, self.sign, self.key = here("valid", [P, NT]), here("sign", [P, NT], I32), here("key", [P, NT], I32)
                self.half_i, self.hi, self.lo = here("half_i", [P, NT], I32), here("hi", [P, NT]), here("lo", [P, NT])
                self.junk, self.bits = here("junk", [P, NT]), here("bits", [P, 16])
                self.T_hi, self.T_lo = here("T_hi", [P, 1]), here("T_lo", [P, 1])
                self.cand, self.hits, self.bit, self.want = (here(w, [P, 1]) for w in ("cand", "hits", "bit", "want"))
                self.above, self.equal = here("above", [P, NT]), here("equal", [P, NT])
                self.rank, self.colsum = here("rank", [P, NT]), here("colsum", [P, NT])
                self.counted, self.counted_all, self.done = sem("topk_counted"), sem("topk_all"), sem("topk_done")

            def product(self, pe, n):
                if not isinstance(n, int) or n < 34:
                    pe.wait_ge(self.counted, n + 1)
                    pe.matmul(psum[:, 0, 0:1], ones[:], self.hits[:], start=True, stop=True).then_inc(self.counted_all, 1)
                else:
                    by, column = ((before, NT) if n == 34 else (ones, 2 * NT))
                    pe.matmul(psum[:, 0, column:column + NT], by[:], self.equal[:], start=True,
                              stop=True).then_inc(self.counted_all, 1)

            def search(self, dve, s):
                valid, sign, key, half_i, hi, lo = self.valid, self.sign, self.key, self.half_i, self.hi, self.lo
                junk, bits, cand, hits, bit, want = self.junk, self.bits, self.cand, self.hits, self.bit, self.want
                above, equal, rank, colsum = self.above, self.equal, self.rank, self.colsum
                counted, counted_all = self.counted, self.counted_all
                s(dve.memset(valid[:], 1.0))
                s(dve.tensor_copy(valid[:, NT - 1:NT], ones_last[:, 0:1]))
                for b in range(16):
                    ins = dve.memset(bits[:, b:b + 1], float(1 << (15 - b)))
                s(ins)
                w_i = wgt[:].bitcast(I32)
                s(dve.tensor_scalar(sign[:], w_i, 31, -(1 << 31), ALU.arith_shift_right, ALU.bitwise_or))
                s(dve.tensor_tensor(key[:], w_i, sign[:], ALU.bitwise_xor))
                s(dve.tensor_scalar(half_i[:], key[:], 16, 0xFFFF, ALU.logical_shift_right, ALU.bitwise_and))
                s(dve.tensor_copy(hi[:], half_i[:]))
                s(dve.tensor_scalar(half_i[:], key[:], 0xFFFF, None, ALU.bitwise_and))
                s(dve.tensor_copy(lo[:], half_i[:]))
                s(dve.scalar_tensor_tensor(hi[:], hi[:], 1.0, valid[:], ALU.add, ALU.mult))
                s(dve.tensor_scalar(hi[:], hi[:], -1.0, None, ALU.add))
                s(dve.memset(want[:], float(TOPK)))

                def find(keys, T, at):
                    s(dve.memset(T[:], 0.0))
                    with s.loop(0, 16, 3) as b:
                        s(dve.tensor_tensor(cand[:], T[:], bits[:, bass.ds(b, 1)], ALU.add))
                        dve.tensor_scalar(junk[:], keys[:], cand[:, 0:1], 0.0, ALU.is_ge, ALU.add,
                                          accum_out=hits[:]).then_inc(counted, 1)
                        dve.wait_ge(counted_all, b + (at + 1))
                        s(dve.tensor_tensor(bit[:], psum[:, 0, 0:1], want[:], ALU.is_ge))
                        s(dve.scalar_tensor_tensor(T[:], bit[:], bits[:, bass.ds(b, 1)], T[:], ALU.mult, ALU.add))

                find(hi, self.T_hi, 0)
                dve.tensor_scalar(above[:], hi[:], self.T_hi[:, 0:1], 0.0, ALU.is_gt, ALU.add,
                                  accum_out=hits[:]).then_inc(counted, 1)
                dve.wait_ge(counted_all, 17)
                s(dve.tensor_tensor(want[:], want[:], psum[:, 0, 0:1], ALU.subtract))
                s(dve.tensor_scalar(equal[:], hi[:], self.T_hi[:, 0:1], None, ALU.is_equal))
                s(dve.scalar_tensor_tensor(lo[:], lo[:], 1.0, equal[:], ALU.add, ALU.mult))
                s(dve.tensor_scalar(lo[:], lo[:], -1.0, None, ALU.add))
                find(lo, self.T_lo, 17)
                s(dve.tensor_scalar(equal[:], lo[:], self.T_lo[:, 0:1], None, ALU.is_equal))
                dve.tensor_scalar(junk[:], lo[:], self.T_lo[:, 0:1], 0.0, ALU.is_gt, ALU.add,
                                  accum_out=hits[:]).then_inc(counted, 1)
                dve.wait_ge(counted, 34)
                s(dve.tensor_tensor(above[:], above[:], junk[:], ALU.add))
                dve.wait_ge(counted_all, self.STEPS)
                s(dve.tensor_tensor(want[:], want[:], psum[:, 0, 0:1], ALU.subtract))
                s(dve.tensor_copy(colsum[:], psum[:, 0, 2 * NT:3 * NT]))
                s(dve.tensor_tensor_scan(rank[:], ones[:, 0:NT], colsum[:], 0.0, ALU.mult, ALU.add))
                s(dve.tensor_tensor(rank[:], rank[:], colsum[:], ALU.subtract))
                s(dve.tensor_tensor(rank[:], rank[:], psum[:, 0, NT:2 * NT], ALU.add))
                s(dve.scalar_tensor_tensor(rank[:], rank[:], want[:, 0:1], equal[:], ALU.is_lt, ALU.mult))
                s(dve.tensor_tensor(above[:], above[:], rank[:], ALU.add))
                s(dve.tensor_tensor(mw[:], wgt[:], above[:], ALU.mult))

        with ExitStack() as scope, nc.Block() as block:
            here = lambda what, shape, dt=F32: sb("f0_" + what, shape, dt, scope)
            ht, w1_hi, w1_lo, w2_hi, w2_lo = token.ht, token.w1_hi, token.w1_lo, token.w2_hi, token.w2_lo
            b1, b2_hi, b2_lo, ones_r = token.b1, token.b2_hi, token.b2_lo, token.ones_r
            xt_hi, xt_lo = here("xt_hi", [P, 2, KD, MT], F32R), here("xt_lo", [P, 2, KD, MT], F32R)
            ht_hi, ht_lo = here("ht_hi", [P, 2, HB * MT], F32R), here("ht_lo", [P, 2, HB * MT], F32R)
            topk = TopK(scope)
            x_hi_ready, x_ready = sem("f0_x_hi"), sem("f0_x_ready")
            hid, hid_out, h_hi, h_split = sem("f0_hid"), sem("f0_hid_out"), sem("f0_h_hi"), sem("f0_h_split")
            made, made_out = sem("f0_made"), sem("f0_made_out")
            QUARTER = HB * MT // 4
            ASKED = 4
            SEARCH_UNITS = TopK.STEPS // ASKED
            assert SEARCH_UNITS * ASKED == TopK.STEPS and SEARCH_UNITS % 2 == 1 and UNITS % 2 == 1

            def rounds(engine, start, work):
                def at(n, u):
                    def part(d):
                        if isinstance(n, int) and not 0 <= n + d < UNITS:
                            return None
                        return n + d, (u + d) % 2
                    return part
                for n in range(start, 2):
                    work(n, n >= 0, at(n, n % 2))
                with engine.Fori(1, SEARCH_UNITS // 2) as i:
                    for u in range(2):
                        work(2 * i + u, True, at(2 * i + u, u))
                for n in range(SEARCH_UNITS - 1, SEARCH_UNITS + 1):
                    work(n, n < SEARCH_UNITS, at(n, n % 2))
                with engine.Fori((SEARCH_UNITS + 1) // 2, UNITS // 2 - 1) as i:
                    for u in range(2):
                        work(2 * i + u, False, at(2 * i + u, u))
                for n in range(UNITS - 3, UNITS):
                    work(n, False, at(n, n % 2))

            @block.tensor
            def _(pe):
                def work(n, searching, part):
                    if part(1):
                        m, u = part(1)
                        pe.wait_ge(x_ready, m + 1)
                        for b in range(HB):
                            wait(pe, hid_out, m * HB + (b - 3))
                            for k in range(KD):
                                at_w = slice((k * HB + b) * P, (k * HB + b + 1) * P)
                                ins = split_product(pe, psum[:, 1 + b % 4, 0:MT], w1_hi[:, at_w], w1_lo[:, at_w],
                                                    xt_hi[:, u, k, :], xt_lo[:, u, k, :], k == 0, k == KD - 1)
                            ins.then_inc(hid, 1)
                            if b % 2 == 1 and searching:
                                topk.product(pe, ASKED * n + b // 2)
                    if part(0):
                        m, u = part(0)
                        pe.wait_ge(h_split, (m + 1) * 4)
                        for j in range(2):
                            wait(pe, made_out, 2 * m + (j - 1))
                            for b in range(HB):
                                at_h = slice(b * MT + j * P, b * MT + (j + 1) * P)
                                at_w = slice(b * D, (b + 1) * D)
                                split_product(pe, psum[:, 5 + j, 0:D], ht_hi[:, u, at_h], ht_lo[:, u, at_h],
                                              w2_hi[:, at_w], w2_lo[:, at_w], b == 0, False)
                            pe.matmul(psum[:, 5 + j, 0:D], ones_r[:], b2_hi[:], start=False, stop=False)
                            pe.matmul(psum[:, 5 + j, 0:D], ones_r[:], b2_lo[:], start=False, stop=True).then_inc(made, 1)
                rounds(pe, -1, work)

            @block.scalar
            def _(act):
                def work(n, searching, part):
                    if part(2):
                        m, u = part(2)
                        wait(act, hid, HB * (m - 1))
                        act.copy(xt_hi[:, u, :, :], AT[:, :, bass.ts(m, MT)]).then_inc(x_hi_ready, 1)
                    if part(1):
                        m, u = part(1)
                        wait(act, made, 2 * (m - 1))
                        for q in range(4):
                            wait(act, h_split, 4 * (m - 1) + (q + 1))
                            for b in range(q * HB // 4, (q + 1) * HB // 4):
                                act.wait_ge(hid, m * HB + (b + 1))
                                act.activation(ht[:, b * MT:(b + 1) * MT], psum[:, 1 + b % 4, 0:MT], ACT.Gelu_apprx_tanh,
                                               bias=b1[:, b:b + 1]).then_inc(hid_out, 1)
                            of = slice(q * QUARTER, (q + 1) * QUARTER)
                            act.wait_ge(hid_out, m * HB + (q + 1) * (HB // 4))
                            act.copy(ht_hi[:, u, of], ht[:, of]).then_inc(h_hi, 1)
                    if part(0):
                        m, u = part(0)
                        act.wait_ge(x_ready, m + 1)
                        for j in range(2):
                            act.wait_ge(made, 2 * m + (j + 1))
                            act.copy(AT[:, :, bass.ts(2 * m + j, P)],
                                     psum[:, 5 + j, 0:D].rearrange("p (k n) -> p k n", k=KD)).then_inc(made_out, 1)
                rounds(act, -2, work)

            @block.gpsimd
            def _(pool):
                def work(n, searching, part):
                    if part(2):
                        m, u = part(2)
                        pool.wait_ge(x_hi_ready, m + 1)
                        pool.tensor_tensor(xt_lo[:, u, :, :], AT[:, :, bass.ts(m, MT)], xt_hi[:, u, :, :],
                                           ALU.subtract).then_inc(x_ready, 1)
                    if part(1):
                        m, u = part(1)
                        for q in range(4):
                            of = slice(q * QUARTER, (q + 1) * QUARTER)
                            pool.wait_ge(h_hi, 4 * m + (q + 1))
                            pool.tensor_tensor(ht_lo[:, u, of], ht[:, of], ht_hi[:, u, of], ALU.subtract).then_inc(h_split, 1)
                rounds(pool, -2, work)

            @block.vector
            def _(dve):
                topk.search(dve, s)
                with s.loop(0, GROUPS, 2) as g:
                    for m in range(GROUP):
                        t = g * GROUP + m
                        own = row(X, t).rearrange("p (k n) -> p k n", k=KD)
                        dve.wait_ge(made_out, t + 1)
                        ins = dve.scalar_tensor_tensor(own, AT[:, :, bass.ts(t, P)], mw[:, bass.ds(t, 1)], own, ALU.mult, ALU.add)
                    s(ins)
                    for m in range(GROUP):
                        ins = dve.bn_stats(row(stats, g * GROUP + m), row(X, g * GROUP + m))
                    s(ins)
                row_moments(dve, s)
        token_scope.close()

        with ExitStack() as scope, nc.Block() as block:
            eps1 = sb("eps1", [P, 1], at=scope)
            eps_in, eps_ready = sem("t1_eps_in"), sem("t1_eps_ready")
            stored = sem("t1_stored")
            turn = Turn("t1_", scope, GROUPS)
            table_rows = table[1].rearrange("(t p) d -> p t d", p=P)

            @block.sync
            def _(sp):
                sp.dma_start(eps1[:], g1_eps.partition_broadcast(P)).then_inc(eps_in, 16)

                def store(g, u, again):
                    sp.wait_ge(turn.ready, g + 1)
                    sp.dma_start(table_rows[:, bass.ts(g, GROUP), :], turn.ring[:, u, :, :]).then_inc(stored, 16)
                each_group(store)
                sp.wait_ge(stored, 16 * GROUPS)
                sp.wait_ge(eps_in, 16)

            @block.scalar
            def _(act):
                row_root(act, 4)
                act.wait_ge(eps_ready, 1)

                def turn_out(g, u, again):
                    for m in range(GROUP):
                        act.wait_ge(turn.turned, g * GROUP + (m + 1))
                        act.activation(AT[:, :, bass.ts(g * GROUP + m, P)], psum[:, m, 0:D].rearrange("p (k n) -> p k n", k=KD),
                                       ACT.Copy, scale=eps1[:, 0:1]).then_inc(turn.out, 1)
                each_group(turn_out)

            @block.tensor
            def _(pe):
                each_group(lambda g, u, again: [turn.turn(pe, g, u, m, again) for m in range(GROUP)])

            @block.vector
            def _(dve):
                dve.wait_ge(eps_in, 16)
                dve.tensor_scalar(eps1[:], eps1[:], 1.0, None, ALU.add).then_inc(eps_ready, 1)
                row_rstd(dve, s, 1e-5, 4)

                each_group(lambda g, u, again: turn.normalise(dve, g, u))

        seven = [c for turn_length in (6, 6, 6, 7, 7) for c in range(turn_length)]
        aggregate(table[1], "g1_", None, seven, GraphTiles)

        graph.close()

        with ExitStack() as scope, nc.Block() as block:
            here = lambda what, shape, dt=F32: sb("r_" + what, shape, dt, scope)
            C = 2 * NT
            wr, br = here("wr", [P, KD, NE]), here("br", [P, NE])
            xr = here("xr", [P, GROUP, D])
            root2 = here("root2", [P, NT])
            logit, work, work2 = here("logit", [P, NT, NE]), here("work", [P, NT, NE]), here("work2", [P, NT, NE])
            hot = here("hot", [P, NT, 2, NE])
            top = here("top", [P, NT, 2])
            pick = here("pick", [P, NT])
            expo, total = here("expo", [P, NT, NE]), here("total", [P, NT])
            prob = here("prob", [P, NT, 2])
            sums = here("sums", [P, NE, C + 1])
            keep = here("keep", [P, NE, C + 1])
            upto = here("upto", [P, NE, C + 1])
            ntile_i, ntile = here("ntile_i", [P, NE], I32), here("ntile", [P, NE])
            tiles_upto, first = here("tiles_upto", [P, NE]), here("first", [P, NE])
            at = here("at", [P, C, NE])
            slot_f = here("slot_f", [P, C])
            past, exp_f, exp_i = here("past", [P, NE]), here("exp_f", [P, 1]), here("exp_i", [P, 1], I32)
            slot_part, slot_lo, slot_hi = here("slot_part", [P, C], I32), here("slot_lo", [P, C]), here("slot_hi", [P, C])
            zero_row = here("zero_row", [1, P])
            node = here("node", [P, NT])
            is_lo = here("is_lo", [P, 2, 2 * GROUP, P])
            is_hi = here("is_hi", [P, 2, 2 * GROUP, SC])
            turn = Turn("r_", scope, GROUPS)

            params = sem("r_params")
            scored = sem("r_scored")
            kept = sem("r_kept")
            exp_ask, exp_done = sem("r_exp_ask"), sem("r_exp_done")
            hot_ready, ranked = sem("r_hot"), sem("r_ranked")
            map_ready, map_out, map_in = sem("r_map_ready"), sem("r_map_out"), sem("r_map_in")
            hots_ready, placed = sem("r_hots_ready"), sem("r_placed")

            @block.sync
            def _(sp):
                sp.dma_start(wr[:], m_wr.rearrange("(k p) n -> p k n", p=P)).then_inc(params, 16)
                sp.dma_start(br[:], m_br.partition_broadcast(P)).then_inc(params, 16)
                table_rows = expert_table.rearrange("(t p) d -> p t d", p=P)

                def keep_rows(g, u, again):
                    sp.wait_ge(turn.ready, g + 1)
                    sp.dma_start(table_rows[:, bass.ts(g, GROUP), :], turn.ring[:, u, :, :]).then_inc(kept, 16)
                each_group(keep_rows)
                sp.wait_ge(kept, 16 * GROUPS)
                sp.wait_ge(params, 32)
                sp.wait_ge(map_ready, 1)
                sp.dma_start(expert_row.rearrange("(p a) -> p a", a=1), exp_i[:],
                             allow_slow_non_contiguous=True).then_inc(map_out, 16)
                sp.wait_ge(map_out, 16)
                sp.dma_start(expert[:], expert_row.rearrange("(a p) -> a p", a=1)).then_inc(map_in, 16)
                sp.wait_ge(map_in, 16)

            @block.scalar
            def _(act):
                row_root(act, 5)
                act.wait_ge(var_ready, 6)
                act.activation(root2[:], root2[:], ACT.Sqrt).then_inc(root_ready, 1)

                def turn_out(g, u, again):
                    for m in range(GROUP):
                        act.wait_ge(turn.turned, g * GROUP + (m + 1))
                        if again or u:
                            act.wait_ge(scored, g * GROUP + (m + 1 - GROUP))
                        act.copy(xr[:, m, :], psum[:, m, 0:D]).then_inc(turn.out, 1)
                each_group(turn_out)
                act.wait_ge(exp_ask, 1)
                act.activation(expo[:].rearrange("p t e -> p (t e)"), work[:].rearrange("p t e -> p (t e)"),
                               ACT.Exp).then_inc(exp_done, 1)
                act.activation(prob[:].rearrange("p t e -> p (t e)"), top[:].rearrange("p t e -> p (t e)"),
                               ACT.Exp).then_inc(exp_done, 1)

            @block.tensor
            def _(pe):
                pe.wait_ge(params, 32)

                def score(g, m):
                    pe.wait_ge(turn.out, g * GROUP + (m + 1))
                    for k in range(KD):
                        ins = pe.matmul(psum[:, 7, (g * GROUP + m) * NE:(g * GROUP + m + 1) * NE], xr[:, m, k * P:(k + 1) * P],
                                        wr[:, k, :], start=k == 0, stop=k == KD - 1)
                    ins.then_inc(scored, 1)
                for g in range(-1, GROUPS):
                    for m in range(GROUP):
                        if g + 1 < GROUPS:
                            turn.turn(pe, g + 1, g + 1, m, g >= 0)
                        if g >= 0:
                            score(g, m)
                pe.wait_ge(hot_ready, 1)
                flat = hot[:].rearrange("p t k e -> p (t k e)")
                for h in range(2):
                    part_of = flat[:, h * NT * NE:(h + 1) * NT * NE]
                    pe.matmul(psum[:, 3 + h, 0:NT * NE], before[:], part_of, start=True, stop=True).then_inc(ranked, 1)
                    pe.matmul(psum[:, 5 + h, 0:NT * NE], ones[:], part_of, start=True, stop=True).then_inc(ranked, 1)

                def place(g, u, again):
                    pe.wait_ge(hots_ready, 2 * g + 2)
                    for c in range(2 * GROUP):
                        ins = pe.matmul(psum[:, 0, 0:SC], is_lo[:, u, c, :], is_hi[:, u, c, :], start=False, stop=False)
                    ins.then_inc(placed, 1)
                pe.matmul(psum[:, 0, 0:SC], zero_row[:], zero_row[:, 0:SC], start=True, stop=False)
                over_groups(pe, place)
                pe.matmul(psum[:, 0, 0:SC], zero_row[:], zero_row[:, 0:SC], start=False, stop=True).then_inc(placed, 1)

            @block.vector
            def _(dve):
                row_stats(dve, s, X)
                row_rstd(dve, s, 1e-5, 5)
                s(dve.tensor_tensor(root2[:], moments[:, :, 1], rstd[:], ALU.mult))
                s(dve.tensor_tensor(root2[:], root2[:], rstd[:], ALU.mult))
                dve.tensor_scalar(root2[:], root2[:], 1e-5, None, ALU.add).then_inc(var_ready, 1)
                dve.wait_ge(root_ready, 6)
                s(dve.reciprocal(pick[:], root2[:]))
                s(dve.tensor_tensor(rstd[:], rstd[:], pick[:], ALU.mult))

                each_group(lambda g, u, again: turn.normalise(dve, g, u))
                s(dve.memset(keep[:], 1.0))
                s(dve.memset(keep[:, :, 0:1], 0.0))
                s(dve.memset(sums[:, :, 0:1], 0.0))
                s(dve.memset(zero_row[:], 0.0))
                s(dve.tensor_scalar(node[:], columns[:, 0:NT], float(P), part[:, 0:1], ALU.mult, ALU.add))
                dve.wait_ge(params, 32)
                dve.wait_ge(scored, NT)
                numbers = columns[:, 0:NE].unsqueeze(1).to_broadcast([P, NT, NE])
                wide = lambda a: a.unsqueeze(2).to_broadcast([P, NT, NE])
                s(dve.tensor_tensor(logit[:], psum[:, 7, 0:NT * NE].rearrange("p (t e) -> p t e", e=NE), wide(root2[:]), ALU.mult))
                s(dve.tensor_tensor(logit[:], logit[:], br[:].unsqueeze(1).to_broadcast([P, NT, NE]), ALU.add))

                def best(k, scores):
                    s(dve.tensor_reduce(top[:, :, k], scores[:], AX.X, ALU.max))
                    s(dve.tensor_tensor(work2[:], scores[:], wide(top[:, :, k]), ALU.is_equal))
                    s(dve.scalar_tensor_tensor(work2[:], work2[:], -float(NE), numbers, ALU.mult, ALU.add))
                    s(dve.tensor_reduce(pick[:], work2[:], AX.X, ALU.min))
                    s(dve.tensor_scalar(pick[:], pick[:], float(NE), None, ALU.add))
                    s(dve.tensor_tensor(hot[:, :, k, :], numbers, wide(pick[:]), ALU.is_equal))

                best(0, logit)
                s(dve.scalar_tensor_tensor(work[:], hot[:, :, 0, :], -1e30, logit[:], ALU.mult, ALU.add))
                best(1, work)
                dve.engine_nop().then_inc(hot_ready, 1)
                s(dve.tensor_tensor(work[:], logit[:], wide(top[:, :, 0]), ALU.subtract))
                s(dve.tensor_copy(pick[:], top[:, :, 0]))
                dve.tensor_tensor(top[:], top[:], pick[:].unsqueeze(2).to_broadcast([P, NT, 2]), ALU.subtract).then_inc(exp_ask, 1)
                dve.wait_ge(ranked, 4)
                for h in range(2):
                    s(dve.tensor_copy(sums[:, :, 1 + h * NT:1 + (h + 1) * NT],
                                      psum[:, 5 + h, 0:NT * NE].rearrange("p (c e) -> p e c", e=NE)))
                s(dve.tensor_tensor_scan(upto[:].rearrange("p e c -> p (e c)"), keep[:].rearrange("p e c -> p (e c)"),
                                         sums[:].rearrange("p e c -> p (e c)"), 0.0, ALU.mult, ALU.add))
                s(dve.tensor_scalar(ntile_i[:], upto[:, :, C], float(MT - 1), None, ALU.add))
                s(dve.tensor_scalar(ntile_i[:], ntile_i[:], 8, None, ALU.logical_shift_right))
                s(dve.tensor_copy(ntile[:], ntile_i[:]))
                s(dve.tensor_tensor_scan(tiles_upto[:], ones[:, 0:NE], ntile[:], 0.0, ALU.mult, ALU.add))
                s(dve.tensor_tensor(first[:], tiles_upto[:], ntile[:], ALU.subtract))
                s(dve.tensor_scalar(first[:], first[:], float(MT), None, ALU.mult))
                for h in range(2):
                    s(dve.tensor_tensor(at[:, h * NT:(h + 1) * NT, :], psum[:, 3 + h, 0:NT * NE].rearrange("p (c e) -> p c e", e=NE),
                                        upto[:, :, h * NT:(h + 1) * NT].rearrange("p e c -> p c e"), ALU.add))
                s(dve.tensor_tensor(at[:], at[:], first[:].unsqueeze(1).to_broadcast([P, C, NE]), ALU.add))
                s(dve.tensor_tensor(at[:], at[:], hot[:].rearrange("p t k e -> p (t k) e"), ALU.mult))
                s(dve.tensor_reduce(slot_f[:], at[:], AX.X, ALU.add))
                s(dve.tensor_copy(slot[:], slot_f[:]))
                s(dve.tensor_scalar(slot_part[:], slot[:], P - 1, None, ALU.bitwise_and))
                s(dve.tensor_copy(slot_lo[:], slot_part[:]))
                s(dve.tensor_scalar(slot_part[:], slot[:], 7, None, ALU.logical_shift_right))
                s(dve.tensor_copy(slot_hi[:], slot_part[:]))

                def hots(g, u, again):
                    if again:
                        dve.wait_ge(placed, g - 1)
                    for c in range(2 * GROUP):
                        at_c = bass.ds(g * (2 * GROUP) + c, 1)
                        ins = dve.tensor_scalar(is_lo[:, u, c, :], columns[:], slot_lo[:, at_c], node[:, bass.ds(g * GROUP + c // 2, 1)],
                                                ALU.is_equal, ALU.mult)
                    ins.then_inc(hots_ready, 1)
                    dve.tensor_tensor(is_hi[:, u, :, :], columns[:, 0:SC].unsqueeze(1).to_broadcast([P, 2 * GROUP, SC]),
                                      slot_hi[:, bass.ts(g, 2 * GROUP)].unsqueeze(2).to_broadcast([P, 2 * GROUP, SC]),
                                      ALU.is_equal).then_inc(hots_ready, 1)
                over_groups(dve, hots)
                s(dve.tensor_scalar(past[:], tiles_upto[:], part[:, 0:1], None, ALU.is_le))
                s(dve.tensor_reduce(exp_f[:], past[:], AX.X, ALU.add))
                dve.tensor_scalar(exp_i[:], exp_f[:], float(NE - 1), None, ALU.min).then_inc(map_ready, 1)
                s(dve.tensor_scalar(tile_pairs[:], tiles_upto[:, NE - 1:NE], 1.0, None, ALU.add))
                s(dve.tensor_scalar(tile_pairs[:], tile_pairs[:], 1, None, ALU.logical_shift_right))
                s(dve.tensor_scalar(tile_pairs[:], tile_pairs[:], float(-PEELED), None, ALU.add))
                dve.wait_ge(exp_done, 2)
                s(dve.tensor_reduce(total[:], expo[:], AX.X, ALU.add))
                s(dve.reciprocal(total[:], total[:]))
                s(dve.tensor_tensor(prob[:], prob[:], total[:].unsqueeze(2).to_broadcast([P, NT, 2]), ALU.mult))
                s(dve.tensor_reduce(total[:], prob[:], AX.X, ALU.add))
                s(dve.reciprocal(total[:], total[:]))
                s(dve.tensor_tensor(share[:], prob[:], total[:].unsqueeze(2).to_broadcast([P, NT, 2]), ALU.mult))
                dve.wait_ge(placed, GROUPS + 1)
                s(dve.tensor_copy(node_of[:], psum[:, 0, 0:SC]))

        with ExitStack() as scope, nc.Block() as block:
            here = lambda what, shape, dt=F32: sb("e_" + what, shape, dt, scope)
            w1, w2 = here("w1", [P, KD * HM]), here("w2", [P, HB * D])
            w1_hi, w1_lo = here("w1_hi", [P, 2, KD * HM], F32R), here("w1_lo", [P, 2, KD * HM], F32R)
            w2_hi, w2_lo = here("w2_hi", [P, 2, HB * D], F32R), here("w2_lo", [P, 2, HB * D], F32R)
            gain, shift = here("gain", [P, NE, KD]), here("shift", [P, NE, KD])
            b1, b2 = here("b1", [P, NE, HB]), here("b2", [P, NE, D])
            nodes = here("nodes", [P, 2, 2], I32)
            rows = here("rows", [P, 2, 2, D])
            xt = here("xt", [P, KD * MT])
            xt_hi, xt_lo = here("xt_hi", [P, 2, KD * MT], F32R), here("xt_lo", [P, 2, KD * MT], F32R)
            ht = here("ht", [P, HB * MT])
            ht_hi, ht_lo = here("ht_hi", [P, 2, HB * MT], F32R), here("ht_lo", [P, 2, HB * MT], F32R)
            y = here("y", [P, 2, 2, D])
            nodes_ready = sem("e_nodes_ready")
            rows_in = [sem("e_rows0"), sem("e_rows1")]
            params = sem("e_params")
            w1_in, w1_hi_ready, w1_ready = sem("e_w1_in"), sem("e_w1_hi"), sem("e_w1_ready")
            w2_in, w2_hi_ready, w2_ready = sem("e_w2_in"), sem("e_w2_hi"), sem("e_w2_ready")
            turned, x_ready = sem("e_turned"), sem("e_x_ready")
            hid, hid_out, h_split = sem("e_hid"), sem("e_hid_out"), sem("e_h_split")
            made, made_out = sem("e_made"), sem("e_made_out")
            stored = [sem("e_stored0"), sem("e_stored1")]
            QUARTER = HB * MT // 4

            def rounds(engine, start, work, loop=None):
                def at(n, u, left):
                    def part(d):
                        if isinstance(n, int) and n + d < 0 or d >= left:
                            return None
                        return n + d, (u + d) % 2
                    return part
                pairs = engine.value_load(tile_pairs[0:1, 0:1], min_val=MIN_PAIRS - PEELED, max_val=MTILES // 2 - PEELED)
                for n in range(start, 2):
                    work(at(n, n % 2, 4))
                with (loop or engine.Fori)(1, pairs + (PEELED - 2)) as i:
                    for u in range(2):
                        work(at(2 * i + u, u, 4))
                for r in range(4):
                    work(at(2 * pairs + (2 * PEELED - 4 + r), r % 2, 4 - r))
                return pairs

            def expert_of(engine, m):
                return bass.ds(engine.value_load(expert[0:1, bass.ds(m, 1)], min_val=0, max_val=NE - 1), 1)

            def uses(m, u, count):
                return (m - u) * (count // 2)

            @block.sync
            def _(sp):
                def work(part):
                    if part(3):
                        m, u = part(3)
                        one = expert_of(sp, m)
                        wait(sp, w1_ready, m)
                        sp.dma_start(w1[:], m_w1[one, :, :, :].rearrange("a p k n -> p (a k n)")).then_inc(w1_in, 16)
                    if part(2):
                        m, u = part(2)
                        one = expert_of(sp, m)
                        wait(sp, w2_ready, m)
                        sp.dma_start(w2[:], m_w2[one, :, :, :].rearrange("a p k n -> p (a k n)")).then_inc(w2_in, 16)
                sp.dma_start(gain[:], m_g.rearrange("e p k -> p e k")).then_inc(params, 16)
                sp.dma_start(shift[:], m_b.rearrange("e p k -> p e k")).then_inc(params, 16)
                sp.dma_start(b1[:], m_b1.rearrange("e p k -> p e k")).then_inc(params, 16)
                sp.dma_start(b2[:].rearrange("p e n -> p (e n)"), m_b2.rearrange("e n -> (e n)").partition_broadcast(P)).then_inc(params, 16)
                rounds(sp, -3, work)

            @block.gpsimd
            def _(pool):
                def work(part):
                    if part(3):
                        m, u = part(3)
                        wait(pool, turned, m - 1)
                        wait(pool, rows_in[u], uses(m, u, 32))
                        pool.tensor_copy(nodes[:, u, :], node_of[:, bass.ds(2 * m, 2)]).then_inc(nodes_ready, 1)
                        pool.wait_ge(nodes_ready, m + 1)
                        pool.sem_inc(dma_open, 1)
                        for j in range(2):
                            pool.indirect_dma_start(
                                rows[:, u, j, :], None, expert_table,
                                bass.IndirectOffsetOnAxis(ap=nodes[:, u, j:j + 1].bitcast(U32), axis=0)).then_inc(rows_in[u], 16)
                    if part(2):
                        m, u = part(2)
                        pool.wait_ge(w1_hi_ready, m + 1)
                        pool.tensor_tensor(w1_lo[:, u, :], w1[:], w1_hi[:, u, :], ALU.subtract).then_inc(w1_ready, 1)
                rounds(pool, -3, work)

            @block.tensor
            def _(pe):
                def work(part):
                    if part(1):
                        m, u = part(1)
                        pe.wait_ge(x_ready, m + 1)
                        pe.wait_ge(w1_ready, m + 1)
                        for b in range(HB):
                            wait(pe, hid_out, m * HB + (b - 3))
                            for k in range(KD):
                                at_w = slice(k * HM + b * P, k * HM + (b + 1) * P)
                                at_x = slice(k * MT, (k + 1) * MT)
                                ins = split_product(pe, psum[:, 1 + b % 4, 0:MT], w1_hi[:, u, at_w], w1_lo[:, u, at_w],
                                                    xt_hi[:, u, at_x], xt_lo[:, u, at_x], k == 0, k == KD - 1)
                            ins.then_inc(hid, 1)
                    if part(2):
                        m, u = part(2)
                        pe.wait_ge(rows_in[u], uses(m, u, 32) + 32)
                        wait(pe, x_ready, m - 1)
                        for k in range(KD):
                            for j in range(2):
                                ins = pe.transpose(psum[:, 7 * u, k * MT + j * P:k * MT + (j + 1) * P],
                                                   rows[:, u, j, k * P:(k + 1) * P], ident[:])
                        ins.then_inc(turned, 1)
                    if part(0):
                        m, u = part(0)
                        pe.wait_ge(h_split, (m + 1) * 4)
                        pe.wait_ge(w2_ready, m + 1)
                        for j in range(2):
                            wait(pe, made_out, 2 * m + (j - 1))
                            for b in range(HB):
                                at_h = slice(b * MT + j * P, b * MT + (j + 1) * P)
                                at_w = slice(b * D, (b + 1) * D)
                                ins = split_product(pe, psum[:, 5 + j, 0:D], ht_hi[:, u, at_h], ht_lo[:, u, at_h],
                                                    w2_hi[:, u, at_w], w2_lo[:, u, at_w], b == 0, b == HB - 1)
                            ins.then_inc(made, 1)
                rounds(pe, -2, work)

            @block.vector
            def _(dve):
                def work(part):
                    if part(1):
                        m, u = part(1)
                        wait(dve, made, 2 * (m - 1))
                        for q in range(4):
                            of = slice(q * QUARTER, (q + 1) * QUARTER)
                            dve.wait_ge(hid_out, m * HB + (q + 1) * (HB // 4))
                            s(dve.tensor_copy(ht_hi[:, u, of], ht[:, of]))
                            dve.tensor_tensor(ht_lo[:, u, of], ht[:, of], ht_hi[:, u, of], ALU.subtract).then_inc(h_split, 1)
                    if part(2):
                        m, u = part(2)
                        one = expert_of(dve, m)
                        dve.wait_ge(turned, m + 1)
                        wait(dve, hid, HB * (m - 1))
                        wait(dve, x_ready, m)
                        for k in range(KD):
                            ins = dve.tensor_scalar(xt[:, k * MT:(k + 1) * MT], psum[:, 7 * u, k * MT:(k + 1) * MT],
                                                    gain[:, one, k], shift[:, one, k], ALU.mult, ALU.add)
                        s(ins)
                        s(dve.tensor_copy(xt_hi[:, u, :], xt[:]))
                        dve.tensor_tensor(xt_lo[:, u, :], xt[:], xt_hi[:, u, :], ALU.subtract).then_inc(x_ready, 1)
                    if part(0):
                        m, u = part(0)
                        bias = b2[:, expert_of(dve, m), :].rearrange("p a n -> p (a n)")
                        wait(dve, stored[u], uses(m, u, 16))
                        for j in range(2):
                            dve.wait_ge(made, 2 * m + (j + 1))
                            dve.tensor_tensor(y[:, u, j, :], psum[:, 5 + j, 0:D], bias, ALU.add).then_inc(made_out, 1)
                    if part(1):
                        m, u = part(1)
                        dve.wait_ge(w2_hi_ready, m + 1)
                        dve.tensor_tensor(w2_lo[:, u, :], w2[:], w2_hi[:, u, :], ALU.subtract).then_inc(w2_ready, 1)
                dve.wait_ge(params, 64)
                rounds(dve, -2, work, lambda first, last: s.loop(first, last, 12))

            @block.scalar
            def _(act):
                def work(part):
                    if part(2):
                        m, u = part(2)
                        act.wait_ge(w1_in, (m + 1) * 16)
                        wait(act, hid, HB * (m - 1))
                        act.copy(w1_hi[:, u, :], w1[:]).then_inc(w1_hi_ready, 1)
                    if part(1):
                        m, u = part(1)
                        one = expert_of(act, m)
                        for b in range(HB):
                            if b % (HB // 4) == 0:
                                wait(act, h_split, 4 * (m - 1) + (b // (HB // 4) + 1))
                            act.wait_ge(hid, m * HB + (b + 1))
                            act.activation(ht[:, b * MT:(b + 1) * MT], psum[:, 1 + b % 4, 0:MT], ACT.Gelu,
                                           bias=b1[:, one, b]).then_inc(hid_out, 1)
                    if part(-1):
                        m, u = part(-1)
                        act.wait_ge(made_out, 2 * (m + 1))
                        act.dma_start(slots_out[bass.ts(m, MT), :].rearrange("(s p) d -> p s d", p=P),
                                      y[:, u, :, :]).then_inc(stored[u], 16)
                    if part(1):
                        m, u = part(1)
                        act.wait_ge(w2_in, (m + 1) * 16)
                        wait(act, made, 2 * (m - 1))
                        act.copy(w2_hi[:, u, :], w2[:]).then_inc(w2_hi_ready, 1)
                act.wait_ge(params, 64)
                pairs = rounds(act, -2, work)
                act.wait_ge(made_out, 4 * pairs + 4 * PEELED)
                act.dma_start(slots_out[bass.ts(2 * pairs + (2 * PEELED - 1), MT), :].rearrange("(s p) d -> p s d", p=P),
                              y[:, 1, :, :]).then_inc(stored[1], 16)
                for u in range(2):
                    act.wait_ge(stored[u], 16 * pairs + 16 * PEELED)
                    act.sem_inc(dma_open, 1)

        RING = 2 * GROUP
        with ExitStack() as scope, nc.Block() as block:
            got = sb("c_got", [P, RING, D], at=scope)
            fetched = [sem(f"c_fetched{m}") for m in range(GROUP)]
            added = sem("c_added")
            stored = sem("c_stored")

            @block.gpsimd
            def _(pool):
                for c in range(2 * NT):
                    if c >= RING:
                        pool.wait_ge(added, c - RING + 1)
                    pool.indirect_dma_start(got[:, c % RING, :], None, slots_out,
                                            bass.IndirectOffsetOnAxis(ap=slot[:, c:c + 1].bitcast(U32), axis=0)
                                            ).then_inc(fetched[c % RING // 2], 16)

            @block.vector
            def _(dve):
                with dve.Fori(0, NT // GROUP) as g:
                    for r in range(RING):
                        own = X[:, bass.ds(g * GROUP + r // 2, 1), :].rearrange("p a d -> p (a d)")
                        if r % 2 == 0:
                            dve.wait_ge(fetched[r // 2], (g + 1) * 32)
                        else:
                            dve.wait_ge(added, g * RING + r)
                        dve.scalar_tensor_tensor(own, got[:, r, :], share[:, bass.ds(g * GROUP + r // 2, 1), r % 2], own,
                                                 ALU.mult, ALU.add).then_inc(added, 1)

            @block.sync
            def _(sp):
                with sp.Fori(0, GROUPS - 1) as g:
                    sp.wait_ge(added, (g + 1) * RING)
                    sp.dma_start(by_node(out)[:, bass.ts(g, GROUP), :], group_rows(X, g)).then_inc(stored, 16)
                sp.wait_ge(added, 2 * NT)
                sp.dma_start(by_node(out)[:, NT - GROUP:NT - 1, :], X[:, NT - GROUP:NT - 1, :]).then_inc(stored, 16)
                sp.dma_start(out[(NT - 1) * P:N, :], X[0:NLAST, NT - 1, :]).then_inc(stored, 16)
                sp.wait_ge(stored, 16 * (GROUPS + 1))


def kernel(x, src, dst, edge_weight, L0_gnn_W, L0_gnn_bias, L0_gnn_gamma, L0_gnn_beta, L0_ffn_attention_mask, L0_ffn_wr,
           L0_ffn_br, L0_ffn_w1, L0_ffn_b1, L0_ffn_w2, L0_ffn_b2, L1_gnn_W1, L1_gnn_b1, L1_gnn_W2, L1_gnn_b2, L1_gnn_eps,
           L1_gnn_offset, L1_gnn_scale, L1_ffn_Wr, L1_ffn_br, L1_ffn_ln_g, L1_ffn_ln_b, L1_ffn_W1, L1_ffn_b1, L1_ffn_W2,
           L1_ffn_b2):
    import numpy as np
    import concourse.bacc as bacc
    from concourse.bass_utils import run_bass_kernel_spmd

    def blocks(a):
        return np.asarray(a).reshape(NE, -1, P).transpose(0, 2, 1)

    def weight_blocks(a):
        a = np.asarray(a)
        return a.reshape(NE, -1, P, a.shape[2]).transpose(0, 2, 1, 3)

    column_blocks = lambda a: np.asarray(a).reshape(-1, P).T
    laid = {
        "x": x, "src": src, "dst": dst, "edge_weight": edge_weight, "g0_w": L0_gnn_W, "g0_bias": column_blocks(L0_gnn_bias),
        "g0_gamma": column_blocks(L0_gnn_gamma), "g0_beta": column_blocks(L0_gnn_beta), "f0_wr": np.asarray(L0_ffn_wr).reshape(-1), "f0_br": L0_ffn_br,
        "f0_w1": L0_ffn_w1, "f0_b1": column_blocks(L0_ffn_b1), "f0_w2": L0_ffn_w2, "f0_b2": L0_ffn_b2,
        "g1_w1": L1_gnn_W1, "g1_b1": column_blocks(L1_gnn_b1), "g1_w2": L1_gnn_W2, "g1_b2": L1_gnn_b2,
        "g1_eps": L1_gnn_eps, "g1_offset": L1_gnn_offset, "g1_scale": L1_gnn_scale, "m_wr": L1_ffn_Wr, "m_br": L1_ffn_br,
        "m_g": blocks(L1_ffn_ln_g), "m_b": blocks(L1_ffn_ln_b), "m_w1": weight_blocks(L1_ffn_W1),
        "m_b1": blocks(L1_ffn_b1), "m_w2": weight_blocks(L1_ffn_W2), "m_b2": L1_ffn_b2,
    }
    nc = bacc.Bacc("TRN2", target_bir_lowering=False, num_devices=1)
    arrays = {name: np.ascontiguousarray(a) for name, a in laid.items()}
    args = {name: nc.dram_tensor("in_" + name, a.shape, mybir.dt.from_np(a.dtype), kind="ExternalInput").ap()
            for name, a in arrays.items()}
    out = nc.dram_tensor("out", (N, D), F32, kind="ExternalOutput").ap()
    build(nc, **args, out=out)
    r = run_bass_kernel_spmd(nc, [{"in_" + name: a for name, a in arrays.items()}], core_ids=[0])
    return r.results[0]["out"]
```
